# Optimizing a Trainium2 kernel written in Bass

```python
import numpy as np
import jax
import jax.numpy as jnp

def _softmax(x, axis=-1):
    return jax.nn.softmax(x, axis=axis)

def _gelu(x):
    return jax.nn.gelu(x, approximate=True)

def _silu(x):
    return jax.nn.silu(x)

def _sigmoid(x):
    return jax.nn.sigmoid(x)

def _layernorm(x, axis=-1, eps=1e-05):
    m = jnp.mean(x, axis=axis, keepdims=True)
    v = jnp.var(x, axis=axis, keepdims=True)
    return (x - m) / jnp.sqrt(v + eps)

def _scatter_add(tgt, idx, src, axis=0):
    return tgt.at[idx].add(src)

def _segment_sum(src, seg, n):
    return jax.ops.segment_sum(src, seg, n)
kernel_name = 'mk_macaron_d1_jaxref_r4_ffece8'

def setup_inputs(seed: int=0):
    np.random.seed(seed)
    _w = jnp.asarray

    def _L0_attn_setup():
        import jax, jax.numpy as jnp
        import numpy as np
        SEG = 64

        def _mha(x, w_in, b_in, w_out, b_out, n_heads):
            B, S, D = x.shape
            hd = D // n_heads
            qkv = x @ w_in.T + b_in
            q, k, v = jnp.split(qkv, 3, axis=-1)

            def heads(t):
                return t.reshape(B, S, n_heads, hd).transpose(0, 2, 1, 3)
            q, k, v = (heads(q), heads(k), heads(v))
            scores = jnp.einsum('bhqd,bhkd->bhqk', q, k) / jnp.sqrt(jnp.asarray(hd, x.dtype))
            attn = jax.nn.softmax(scores, axis=-1)
            out = jnp.einsum('bhqk,bhkd->bhqd', attn, v)
            out = out.transpose(0, 2, 1, 3).reshape(B, S, D)
            return out @ w_out.T + b_out
        key = jax.random.key(seed)
        ks = jax.random.split(key, 5)
        B, T, D = (4, 1024, 256)
        s = 1.0 / np.sqrt(D)
        return {'x': jax.random.normal(ks[0], (B, T, D), jnp.float32), 'w_in_local': jax.random.normal(ks[1], (3 * D, D), jnp.float32) * s, 'b_in_local': jnp.zeros((3 * D,), jnp.float32), 'w_out_local': jax.random.normal(ks[2], (D, D), jnp.float32) * s, 'b_out_local': jnp.zeros((D,), jnp.float32), 'w_in_global': jax.random.normal(ks[3], (3 * D, D), jnp.float32) * s, 'b_in_global': jnp.zeros((3 * D,), jnp.float32), 'w_out_global': jax.random.normal(ks[4], (D, D), jnp.float32) * s, 'b_out_global': jnp.zeros((D,), jnp.float32)}
    _L0_attn_in = _L0_attn_setup()

    def _L0_ffn_setup():
        import jax, jax.numpy as jnp
        import numpy as np
        H = 256
        I = 128
        E = 32
        TOP_K = 6
        N_GROUP = 8
        TOPK_GROUP = 4
        SCALE = 2.5
        N_SHARED = 2
        SI = I * N_SHARED
        B, S = (2, 256)
        key = jax.random.key(seed)
        ks = jax.random.split(key, 8)
        x = jax.random.normal(ks[0], (B, S, H), jnp.float32)
        gate_weight = jax.random.normal(ks[1], (E, H), jnp.float32) * 0.02
        e_score_correction_bias = jax.random.normal(ks[2], (E,), jnp.float32) * 0.01
        experts_gate_up = jax.random.normal(ks[3], (E, 2 * I, H), jnp.float32) * 0.02
        experts_down = jax.random.normal(ks[4], (E, H, I), jnp.float32) * 0.02
        shared_gate_w = jax.random.normal(ks[5], (SI, H), jnp.float32) * 0.02
        shared_up_w = jax.random.normal(ks[6], (SI, H), jnp.float32) * 0.02
        shared_down_w = jax.random.normal(ks[7], (H, SI), jnp.float32) * 0.02
        return {'x': x, 'gate_weight': gate_weight, 'e_score_correction_bias': e_score_correction_bias, 'experts_gate_up': experts_gate_up, 'experts_down': experts_down, 'shared_gate_w': shared_gate_w, 'shared_up_w': shared_up_w, 'shared_down_w': shared_down_w}
    _L0_ffn_in = _L0_ffn_setup()
    _d = {'L0_attn_x': _L0_attn_in['x'], 'L0_attn_w_in_local': _L0_attn_in['w_in_local'], 'L0_attn_b_in_local': _L0_attn_in['b_in_local'], 'L0_attn_w_out_local': _L0_attn_in['w_out_local'], 'L0_attn_b_out_local': _L0_attn_in['b_out_local'], 'L0_attn_w_in_global': _L0_attn_in['w_in_global'], 'L0_attn_b_in_global': _L0_attn_in['b_in_global'], 'L0_attn_w_out_global': _L0_attn_in['w_out_global'], 'L0_attn_b_out_global': _L0_attn_in['b_out_global'], 'L0_ffn_gate_weight': _L0_ffn_in['gate_weight'], 'L0_ffn_e_score_correction_bias': _L0_ffn_in['e_score_correction_bias'], 'L0_ffn_experts_gate_up': _L0_ffn_in['experts_gate_up'], 'L0_ffn_experts_down': _L0_ffn_in['experts_down'], 'L0_ffn_shared_gate_w': _L0_ffn_in['shared_gate_w'], 'L0_ffn_shared_up_w': _L0_ffn_in['shared_up_w'], 'L0_ffn_shared_down_w': _L0_ffn_in['shared_down_w']}
    _x0 = _d['L0_attn_x']
    _d['L0_attn_x'] = jax.random.normal(jax.random.fold_in(jax.random.key(seed), 1), (1, 4096, 256), dtype=_x0.dtype)
    del _x0
    return _d

def reference(L0_attn_x, L0_attn_w_in_local, L0_attn_b_in_local, L0_attn_w_out_local, L0_attn_b_out_local, L0_attn_w_in_global, L0_attn_b_in_global, L0_attn_w_out_global, L0_attn_b_out_global, L0_ffn_gate_weight, L0_ffn_e_score_correction_bias, L0_ffn_experts_gate_up, L0_ffn_experts_down, L0_ffn_shared_gate_w, L0_ffn_shared_up_w, L0_ffn_shared_down_w):

    def _L0_attn_ref(x, w_in_local, b_in_local, w_out_local, b_out_local, w_in_global, b_in_global, w_out_global, b_out_global):
        import jax, jax.numpy as jnp
        import numpy as np
        SEG = 64

        def _mha(x, w_in, b_in, w_out, b_out, n_heads):
            B, S, D = x.shape
            hd = D // n_heads
            qkv = x @ w_in.T + b_in
            q, k, v = jnp.split(qkv, 3, axis=-1)

            def heads(t):
                return t.reshape(B, S, n_heads, hd).transpose(0, 2, 1, 3)
            q, k, v = (heads(q), heads(k), heads(v))
            scores = jnp.einsum('bhqd,bhkd->bhqk', q, k) / jnp.sqrt(jnp.asarray(hd, x.dtype))
            attn = jax.nn.softmax(scores, axis=-1)
            out = jnp.einsum('bhqk,bhkd->bhqd', attn, v)
            out = out.transpose(0, 2, 1, 3).reshape(B, S, D)
            return out @ w_out.T + b_out
        B, T, D = x.shape
        n_seg = T // SEG
        xs = x.reshape(B, n_seg, SEG, D)
        local = _mha(xs.reshape(B * n_seg, SEG, D), w_in_local, b_in_local, w_out_local, b_out_local, 8)
        local = local.reshape(B, T, D)
        means = xs.mean(axis=2)
        glob = _mha(means, w_in_global, b_in_global, w_out_global, b_out_global, 4)
        glob_b = jnp.repeat(glob, SEG, axis=1)[:, :T, :]
        return local + glob_b

    def _L0_ffn_ref(x, gate_weight, e_score_correction_bias, experts_gate_up, experts_down, shared_gate_w, shared_up_w, shared_down_w):
        import jax, jax.numpy as jnp
        import numpy as np
        H = 256
        I = 128
        E = 32
        TOP_K = 6
        N_GROUP = 8
        TOPK_GROUP = 4
        SCALE = 2.5
        N_SHARED = 2
        SI = I * N_SHARED
        B, S = (2, 256)
        b, s, h = x.shape
        xf = x.reshape(-1, h)
        T = xf.shape[0]
        logits = xf.astype(jnp.float32) @ gate_weight.astype(jnp.float32).T
        scores = jax.nn.sigmoid(logits)
        sfc = scores + e_score_correction_bias[None, :]
        gs = E // N_GROUP
        group_scores = sfc.reshape(T, N_GROUP, gs).max(axis=-1)
        _, gidx = jax.lax.top_k(group_scores, TOPK_GROUP)
        gmask = jnp.zeros((T, N_GROUP), bool).at[jnp.arange(T)[:, None], gidx].set(True)
        smask = jnp.repeat(gmask, gs, axis=1)
        masked = jnp.where(smask, sfc, 0.0)
        _, topk_idx = jax.lax.top_k(masked, TOP_K)
        tw = jnp.take_along_axis(scores, topk_idx, axis=1)
        tw = tw / (tw.sum(-1, keepdims=True) + 1e-20)
        tw = (tw * SCALE).astype(xf.dtype)
        combine = jnp.zeros((T, E), xf.dtype).at[jnp.arange(T)[:, None], topk_idx].add(tw)

        def expert_step(acc, inp):
            gu, dn, c = inp
            g = xf @ gu[:I].T
            u = xf @ gu[I:].T
            o = jax.nn.silu(g) * u @ dn.T
            return (acc + c[:, None] * o, None)
        routed, _ = jax.lax.scan(expert_step, jnp.zeros_like(xf), (experts_gate_up, experts_down, combine.T))
        sh = jax.nn.silu(xf @ shared_gate_w.T) * (xf @ shared_up_w.T)
        shared_out = sh @ shared_down_w.T
        return (routed + shared_out).reshape(b, s, h)
    x = L0_attn_x
    x = x + 0.5 * _L0_ffn_ref(_layernorm(x, axis=-1), L0_ffn_gate_weight, L0_ffn_e_score_correction_bias, L0_ffn_experts_gate_up, L0_ffn_experts_down, L0_ffn_shared_gate_w, L0_ffn_shared_up_w, L0_ffn_shared_down_w)
    x = x + _L0_attn_ref(_layernorm(x, axis=-1), L0_attn_w_in_local, L0_attn_b_in_local, L0_attn_w_out_local, L0_attn_b_out_local, L0_attn_w_in_global, L0_attn_b_in_global, L0_attn_w_out_global, L0_attn_b_out_global)
    x = x + 0.5 * _L0_ffn_ref(_layernorm(x, axis=-1), L0_ffn_gate_weight, L0_ffn_e_score_correction_bias, L0_ffn_experts_gate_up, L0_ffn_experts_down, L0_ffn_shared_gate_w, L0_ffn_shared_up_w, L0_ffn_shared_down_w)
    return x

_drawn_inputs = setup_inputs


def setup_inputs(seed=0):
    import zlib

    import numpy as np

    out = dict(_drawn_inputs(seed))
    spreads = {'L0_attn_b_in_local': (0.0, 0.1),
     'L0_attn_b_out_local': (0.0, 0.1),
     'L0_attn_b_in_global': (0.0, 0.1),
     'L0_attn_b_out_global': (0.0, 0.1)}
    factors = {'L0_attn_w_in_global': 3.896,
     'L0_ffn_gate_weight': 5.68,
     'L0_ffn_e_score_correction_bias': 8.0,
     'L0_ffn_experts_gate_up': 5.071,
     'L0_ffn_experts_down': 5.068,
     'L0_ffn_shared_gate_w': 3.528,
     'L0_ffn_shared_up_w': 3.505,
     'L0_ffn_shared_down_w': 3.51}
    for name, (base, spread) in spreads.items():
        noise = np.random.default_rng([zlib.crc32(name.encode()), seed]).standard_normal(out[name].shape)
        drawn = base * np.exp(spread * noise) if base else spread * noise
        out[name] = jnp.asarray(drawn.astype(out[name].dtype))
    for name, factor in factors.items():
        out[name] = (out[name] * factor).astype(out[name].dtype)
    return out
```

```python
from contextlib import ExitStack

import numpy as np

import concourse.bass as bass
from concourse import mybir

F32 = mybir.dt.float32
I32 = mybir.dt.int32
U32 = mybir.dt.uint32
ALU = mybir.AluOpType
ACT = mybir.ActivationFunctionType
X_AXIS = mybir.AxisListType.X

P = 128
D = 256
KC = D // P
T = 4096
NT = T // P
E = 32
I = 128
SI = 256
TOPK = 6
NG = 8
GS = E // NG
TOPG = 4
SCALE = 2.5
HALF = 0.5
SEG = 64
NSEG = T // SEG
HL, HDL = 8, 32
HG, HDG = 4, 64
EPS = 1e-5

ROW = D + 2 * E
COL_W, COL_DEST = D, D + E
CAP = T + P
DUMMY = E * CAP
NOWHERE = 2 * T * TOPK
NB = 224
MAGIC = 0x5F3759DF


def positive(eng, sem, value):
    if isinstance(value, int) and value <= 0:
        return
    eng.wait_ge(sem, value)


def by_pairs(eng, n, body):
    body(0, 0)
    body(1, 1)
    with eng.Fori(1, n // 2) as pair:
        body(pair * 2, 0)
        body(pair * 2 + 1, 1)


class Steps:

    def __init__(self, eng, sem):
        self.eng, self.sem, self.base, self.n = eng, sem, 0, 0

    def rebase(self, base):
        self.base, self.n = base, 0

    def did(self, ins):
        ins.then_inc(self.sem, 1)
        self.n += 1

    def sync(self):
        self.eng.wait_ge(self.sem, self.base + self.n)

    def then(self, ins):
        self.did(ins)
        self.sync()

    def then_alone(self, ins, passed):
        self.then(ins)
        self.eng.sem_inc(passed, 1)


def build(nc, x_in, gate_t, gate_bias, wgu_in, wdn_in, wsg_in, wsu_in, wsd_in,
          wi_l, bi_l, wo_l, bo_l, wi_g, bi_g, wo_g, bo_g, out):
    ctx = ExitStack()
    with ctx:
        def sb(name, shape, dt=F32):
            return ctx.enter_context(nc.sbuf_tensor(name, shape, dt))

        def sem(name):
            return ctx.enter_context(nc.semaphore(name))

        rows_dram = nc.dram_tensor("dispatch_rows", [DUMMY + P, ROW], F32).ap()
        answers_dram = nc.dram_tensor("answers", [T * TOPK, D], F32).ap()
        xnt_dram = nc.dram_tensor("normed_transposed", [NT, P, D], F32).ap()

        wgu = sb("wgu", [P, KC, E * 2 * I])
        wdn = sb("wdn", [P, E * D])
        wsgu = sb("wsgu", [P, KC, 2 * SI])
        wsd = sb("wsd", [P, SI // P, D])
        wgate = sb("wgate", [P, KC, E])
        wil = sb("wil", [P, KC, 3 * D])
        wol = sb("wol", [P, KC, D])
        wig = sb("wig", [P, KC, 3 * D])
        wog = sb("wog", [P, KC, D])
        bil = sb("bil", [P, 3 * KC])
        big = sb("big", [P, 3 * KC])
        bout = sb("bout", [P, 2, D])
        gbias = sb("gbias", [P, E])
        ident = sb("ident", [P, P])
        ones = sb("ones", [P, P])
        before = sb("before", [P, P])
        seg_mean = sb("seg_mean", [P, 2])
        iota_e = sb("iota_e", [P, E])
        iota_cap = sb("iota_cap", [P, E])
        iota_thr = sb("iota_thr", [P, E])
        iota_blk = sb("iota_blk", [P, 2])
        tok6 = sb("tok6", [P, NT])
        magic = sb("magic", [P, 1])
        padt = sb("padt", [P, ROW])

        xres = sb("xres", [P, NT, D])
        mv = sb("mv", [P, NT, 2])
        rstd = sb("rstd", [P, NT])
        newt = sb("newt", [P, 3, NT])
        stats = sb("stats", [P, 6])
        mv1 = sb("mv1", [P, 2])
        rstd1 = sb("rstd1", [P, 1])

        rows = sb("rows", [P, 2, ROW])
        xnt = sb("xnt", [P, 2, D])
        ex = sb("ex", [P, E])
        sc = sb("sc", [P, E])
        sfc = sb("sfc", [P, E])
        g8 = sb("g8", [P, 3, NG])
        gi8 = sb("gi8", [P, 8], U32)
        og = sb("og", [P, TOPG, NG])
        t8 = sb("t8", [P, 8])
        ti8 = sb("ti8", [P, 8], U32)
        oh = sb("oh", [P, TOPK, E])
        ohs = sb("ohs", [P, TOPK, E])
        msk = sb("msk", [P, 2, E])
        sel = sb("sel", [P, E])
        cw = sb("cw", [P, E])
        csum = sb("csum", [P, 4])
        slot = sb("slot", [P, E])
        base = sb("base", [P, E])
        idx = sb("idx", [P, 2, 8], I32)

        tbl = sb("tbl", [P, 6, E])
        tcol = sb("tcol", [P, 12])
        etab = sb("etab", [P, 2 * P])
        itab = sb("itab", [1, 4 * P], I32)
        ptab = sb("ptab", [1, E], I32)

        blk = sb("blk", [P, 4, ROW])
        cmp_ = blk[:].rearrange("p q r -> p (q r)")[:, 0:E * E].rearrange("p (e j) -> p e j", e=E)
        xbt = sb("xbt", [P, 2, D])
        sg = sb("sg", [P, 2, I])
        hb = sb("hb", [P, 2, I])
        hbt = sb("hbt", [P, 2, I])
        yb = sb("yb", [P, 4, D])
        picked = sb("picked", [P, 2, E])
        wcol = sb("wcol", [P, 4])
        dcol = sb("dcol", [P, 4])
        didx = sb("didx", [P, 4], I32)

        ans = sb("ans", [P, 2, TOPK * D])
        red = [sb("red", [P, D])[:], hb[:].rearrange("p j i -> p (j i)")]
        xs = yb
        ssg = sb("ssg", [P, 2, SI])
        hsh = sb("hsh", [P, 2, SI])
        diag = ssg[:].rearrange("p j (a b) -> p (j a) b", a=2)

        flat = ans[:].rearrange("p j n -> p (j n)")
        at = [0]

        def share(*shape):
            n = int(np.prod(shape))
            v = flat[:, at[0]:at[0] + n]
            at[0] += n
            if len(shape) == 2:
                v = v.rearrange("p (a b) -> p a b", a=shape[0])
            return v

        xn2 = share(D)
        xn2t = share(D)
        qkt = share(4, P)
        ssub = share(HL, SEG)
        pt = share(HL, P)
        osb = share(D)
        ot = share(D)
        vau = sb("vau", [P, HL, HDL + 1])
        smax = sb("smax", [P, HL])
        prob = sb("prob", [P, HL, P])
        rden = sb("rden", [P, HL])
        selt = sb("selt", [NSEG, P])
        glob = sb("glob", [NSEG, D])
        bvb = sb("bvb", [P, 2 * KC, NSEG])

        ps = ctx.enter_context(nc.psum_tensor("ps", [P, 8, 512], F32))

        ld_x = [sem("ld_x0"), sem("ld_x1")]
        ld_small = sem("ld_small")
        ld_exp = sem("ld_exp")
        consts = sem("consts")
        vstep = sem("vector_step")
        vpassed = sem("vector_passed")
        pstep = sem("pool_step")

        block = ctx.enter_context(nc.Block())

        class RouteSems:
            def __init__(self, n):
                s = lambda name: sem(f"{name}_{n}")
                self.xn = s("rt_xn")
                self.xt = s("rt_xt")
                self.xts = s("rt_xts")
                self.store = [s("rt_store0"), s("rt_store1")]
                self.lg = s("rt_lg")
                self.ex = s("rt_ex")
                self.sel = s("rt_sel")
                self.rk = s("rt_rk")
                self.slots = s("rt_slots")
                self.take = s("rt_take")
                self.scat = [s("rt_scat0"), s("rt_scat1")]

        class ExpertSems:
            def __init__(self, n):
                self.n = n
                s = lambda name: sem(f"{name}_{n}")
                self.cnt = s("tb_diag")
                self.bc = s("tb_bc")
                self.tab = s("tb_tab")
                self.ptab = s("tb_ptab")
                self.pad = [s("tb_pad_sp"), s("tb_pad_act")]
                self.ld = [s(f"ex_ld{q}") for q in range(4)]
                self.tx = s("ex_tx")
                self.xt = s("ex_xt")
                self.pick = s("ex_pick")
                self.gu = s("ex_gu")
                self.sg = s("ex_sg")
                self.h = s("ex_h")
                self.ht = s("ex_ht")
                self.hts = s("ex_hts")
                self.d = s("ex_d")
                self.y = s("ex_y")
                self.take = s("ex_take")
                self.scat = [s(f"ex_scat{q}") for q in range(4)]

        class CombineSems:
            def __init__(self, n):
                s = lambda name: sem(f"{name}_{n}")
                self.ans = [s("cb_ans0"), s("cb_ans1")]
                self.xs = [s(f"cb_xs{q}") for q in range(4)]
                self.gu = s("cb_gu")
                self.sg = s("cb_sg")
                self.h = s("cb_h")
                self.d = s("cb_d")
                self.red = s("cb_red")
                self.part = s("cb_part")
                self.sum = s("cb_sum")
                self.out = s("cb_out")

        R = [RouteSems(n) for n in range(2)]
        X = [ExpertSems(n) for n in range(2)]
        C = [CombineSems(n) for n in range(2)]
        m_xn = sem("mean_xn")
        m_mm = sem("mean_mm")
        g_v = sem("glob_vector")
        g_p = sem("glob_tensor")
        g_a = sem("glob_scalar")
        a_xn = sem("at_xn")
        a_xt = sem("at_xt")
        a_xts = sem("at_xts")
        a_qk = sem("at_qk")
        a_qks = sem("at_qks")
        a_v = sem("at_v")
        a_vs = sem("at_vs")
        a_s = sem("at_s")
        a_sub = sem("at_sub")
        a_pr = sem("at_prob")
        a_pt = sem("at_pt")
        a_pts = sem("at_pts")
        a_o = sem("at_o")
        a_os = sem("at_os")
        a_ot = sem("at_ot")
        a_ots = sem("at_ots")
        a_sel = sem("at_sel")
        a_out = sem("at_out")
        a_x2 = sem("at_x2")

        N_SMALL = 16 * 14

        def load_inputs(sp):
            x_tiles = x_in.rearrange("b (n p) d -> p (b n) d", p=P)
            sp.dma_start(wgate[:], gate_t.rearrange("(c p) e -> p c e", p=P)).then_inc(ld_small, 16)
            for h in range(2):
                half = NT // 2
                sp.dma_start(xres[:, h * half:(h + 1) * half, :],
                             x_tiles[:, h * half:(h + 1) * half, :]).then_inc(ld_x[h], 16)
            sp.dma_start(gbias[:], gate_bias.rearrange("(a e) -> a e", a=1).to_broadcast([P, E])
                         ).then_inc(ld_small, 16)
            sp.dma_start(wsgu[:, :, 0:SI], wsg_in.rearrange("(c p) s -> p c s", p=P)).then_inc(ld_small, 16)
            sp.dma_start(wsgu[:, :, SI:2 * SI], wsu_in.rearrange("(c p) s -> p c s", p=P)).then_inc(ld_small, 16)
            sp.dma_start(wsd[:], wsd_in.rearrange("(c p) d -> p c d", p=P)).then_inc(ld_small, 16)
            for dst, src in ((wil, wi_l), (wol, wo_l), (wig, wi_g), (wog, wo_g)):
                sp.dma_start(dst[:], src.rearrange("(c p) d -> p c d", p=P)).then_inc(ld_small, 16)
            with nc.allow_non_contiguous_dma(reason="biases to partitions, once"):
                sp.dma_start(bil[:], bi_l.rearrange("(c p) -> p c", p=P)).then_inc(ld_small, 16)
                sp.dma_start(big[:], bi_g.rearrange("(c p) -> p c", p=P)).then_inc(ld_small, 16)
            for k, b in enumerate((bo_l, bo_g)):
                sp.dma_start(bout[:, k, :], b.rearrange("(a d) -> a d", a=1).to_broadcast([P, D])
                             ).then_inc(ld_small, 16)
            sp.dma_start(wdn[:], wdn_in).then_inc(ld_exp, 16)
            sp.wait_ge(consts, N_CONST)
            sp.dma_start(rows_dram[DUMMY:DUMMY + P, :], padt[:]).then_inc(ld_small, 16)
            sp.dma_start(wgu[:, 0, :], wgu_in[0]).then_inc(ld_exp, 16)
            sp.dma_start(wgu[:, 1, :], wgu_in[1]).then_inc(ld_exp, 16)

        def sp_route(sp, s):
            def body(i, j):
                sp.wait_ge(s.xts, i + 1)
                sp.dma_start(xnt_dram[bass.ds(i, 1)].rearrange("a p d -> (a p) d"),
                             xnt[:, j, :]).then_inc(s.store[j], 16)
            by_pairs(sp, NT, body)

        def pad_experts(eng, s, half):
            eng.wait_ge(s.ptab, 1)
            with eng.Fori(0, E // 2) as k:
                first = eng.value_load(ptab[0:1, bass.ds(k * 2 + half, 1)], min_val=0, max_val=DUMMY - P)
                eng.dma_start(rows_dram[bass.ds(first, P), :], padt[:]).then_inc(s.pad[half], 16)

        def sp_experts(sp, r, s):
            sp.wait_ge(s.tab, 1)
            for j in range(2):
                sp.wait_ge(r.scat[j], 16 * TOPK * (NT // 2))
                sp.wait_ge(s.pad[j], 16 * (E // 2))
            sp.wait_ge(ld_small, N_SMALL)

            def body(g, peeled):
                for q in range(4):
                    n = g * 4 + q
                    first = sp.value_load(itab[0:1, bass.ds(n + 2 * P, 1)], min_val=0, max_val=DUMMY)
                    if not peeled:
                        sp.wait_ge(s.tx, n - 3)
                        sp.wait_ge(s.pick, n * 2 - 6)
                    sp.dma_start(blk[:, q, :], rows_dram[bass.ds(first, P), :]).then_inc(s.ld[q], 16)
            body(0, True)
            with sp.Fori(1, NB // 4) as g:
                body(g, False)

        def sp_combine(sp, x, s, r, last):
            for q in range(4):
                sp.wait_ge(x.scat[q], 16 * (NB // 4))
            for j in range(2):
                sp.wait_ge(r.store[j], 16 * (NT // 2))
            ans_v = answers_dram.rearrange("(n p k) d -> n p (k d)", p=P, k=TOPK)

            def load_tokens(i, q):
                sp.dma_start(xs[:, q, :], xnt_dram[bass.ds(i, 1)].rearrange("a p d -> (a p) d")
                             ).then_inc(s.xs[q], 16)

            def load_answers(i, j):
                positive(sp, s.red, i - 1)
                sp.dma_start(ans[:, j, :], ans_v[bass.ds(i, 1)].rearrange("a p d -> (a p) d")
                             ).then_inc(s.ans[j], 16)

            for q in range(4):
                load_tokens(q, q)
            for q in range(2):
                load_answers(q, q % 2)
            with sp.Fori(0, NT // 4 - 1) as g:
                for q in range(4):
                    i = g * 4 + (q + 4)
                    sp.wait_ge(s.gu, i - 3)
                    load_tokens(i, q)
                    load_answers(i - 2, q % 2)
            for q in range(2, 4):
                load_answers(NT - 4 + q, q % 2)

        def make_consts(pool):
            st = Steps(pool, pstep)
            st.did(pool.memset(ones[:], 1.0))
            st.did(pool.memset(padt[:, 0:COL_DEST], 0.0))
            st.did(pool.memset(padt[:, COL_DEST:ROW], float(NOWHERE)))
            st.did(pool.memset(prob[:], 0.0))
            st.did(pool.memset(vau[:, :, HDL:HDL + 1], 1.0))
            st.did(pool.memset(seg_mean[:], 1.0 / SEG))
            st.sync()
            pool.affine_select(out=ident[:], in_=ones[:], compare_op=ALU.is_equal, fill=0.0, base=0,
                               pattern=[[-1, P]], channel_multiplier=1).then_inc(consts, 1)
            pool.affine_select(out=before[:], in_=ones[:], compare_op=ALU.is_gt, fill=0.0, base=0,
                               pattern=[[1, P]], channel_multiplier=-1).then_inc(consts, 1)
            st.then(pool.affine_select(out=seg_mean[:, 0:1], in_=seg_mean[:, 0:1], compare_op=ALU.is_gt,
                                       fill=0.0, base=SEG, pattern=[[0, 1]], channel_multiplier=-1))
            pool.affine_select(out=seg_mean[:, 1:2], in_=seg_mean[:, 1:2], compare_op=ALU.is_ge,
                               fill=0.0, base=-SEG, pattern=[[0, 1]], channel_multiplier=1).then_inc(consts, 1)

            def iota(dst, pattern, first, mul):
                pool.iota(dst, pattern=pattern, base=first, channel_multiplier=mul,
                          allow_small_or_imprecise_dtypes=True).then_inc(consts, 1)
            iota(iota_e[:], [[1, E]], 0, 0)
            iota(iota_cap[:], [[CAP, E]], 0, 0)
            iota(iota_thr[:], [[P, E]], 0, 0)
            iota(iota_blk[:], [[P, 2]], 0, 1)
            iota(tok6[:], [[TOPK * P, NT]], -1, TOPK)
            iota(magic[:], [[0, 1]], MAGIC, 0)

        N_CONST = 9

        def pool_route(pool, s):
            def body(i, j):
                pool.wait_ge(s.slots, i + 1)
                pool.sem_inc(s.take, 1)
                for k in range(TOPK):
                    pool.indirect_dma_start(
                        out=rows_dram, out_offset=bass.IndirectOffsetOnAxis(ap=idx[:, j, k:k + 1], axis=0),
                        in_=rows[:, j, :], in_offset=None).then_inc(s.scat[j], 16)
            by_pairs(pool, NT, body)

        def pool_experts(pool, s):
            with pool.Fori(0, NB // 4) as g:
                for q in range(4):
                    pool.wait_ge(s.y, g * 4 + (q + 1))
                    pool.sem_inc(s.take, 1)
                    pool.indirect_dma_start(
                        out=answers_dram, out_offset=bass.IndirectOffsetOnAxis(ap=didx[:, q:q + 1], axis=0),
                        in_=yb[:, q, :], in_offset=None, bounds_check=T * TOPK - 1,
                        oob_is_err=False).then_inc(s.scat[q], 16)

        def pool_combine(pool, s):
            def body(i, j):
                pool.wait_ge(s.red, i + 1)
                pool.tensor_tensor(xtile(i), xtile(i), red[j], ALU.add).then_inc(s.part, 1)
            by_pairs(pool, NT, body)

        T2, QK, VO, OL = 5, 4, 6, 7

        def mm(out_, lhs, rhs, start=True, stop=True):
            return nc.tensor.matmul(out_, lhs, rhs, start=start, stop=stop)

        def pe_route_t(pe, s, i, j):
            pe.wait_ge(s.xn, i + 1)
            for c in range(KC):
                m = pe.transpose(ps[:, T2, D + c * P:D + (c + 1) * P], rows[:, j, c * P:(c + 1) * P], ident[:])
            m.then_inc(s.xt, 1)

        def pe_route_lg(pe, s, i, j):
            pe.wait_ge(s.xts, i + 1)
            for c in range(KC):
                m = mm(ps[:, OL, 288:288 + E], xnt[:, j, c * P:(c + 1) * P], wgate[:, c, :],
                       start=(c == 0), stop=(c == KC - 1))
            m.then_inc(s.lg, 1)

        def pe_route_rk(pe, s, i, j):
            pe.wait_ge(s.sel, i + 1)
            mm(ps[:, OL, 320:320 + E], before[:], sel[:])
            mm(ps[:, OL, 352:352 + E], ones[:], sel[:]).then_inc(s.rk, 1)

        def pe_route(pe, s):
            def body(i, j):
                positive(pe, s.slots, i)
                pe_route_t(pe, s, i, j)
                pe_route_lg(pe, s, i, j)
                pe_route_rk(pe, s, i, j)
            by_pairs(pe, NT, body)

        def pe_table(pe, s):
            pe.wait_ge(s.cnt, 1)
            for k in range(4):
                m = mm(ps[:, 0, k * P:(k + 1) * P], ones[:], diag[:, k, :])
            m.then_inc(s.bc, 1)

        TX, GU, HT, DN = 0, 2, 4, 6

        def pe_experts(pe, s):
            now = [pe.alloc_register(f"expert_now{j}_{s.n}") for j in range(2)]
            old = [pe.alloc_register(f"expert_old{j}_{s.n}") for j in range(2)]
            pe.wait_ge(s.tab, 1)
            pe.wait_ge(ld_exp, 48)
            pe.reg_load(now[0], itab[0:1, 0:1])
            pe.reg_mov(now[1], 0)
            pe.reg_mov(old[0], 0)
            pe.reg_mov(old[1], 0)

            def tx(n, q):
                pe.wait_ge(s.ld[q], 16 * (n // 4 + 1) if isinstance(n, int) else n * 4 + (16 - 4 * q))
                for c in range(KC):
                    m = pe.transpose(ps[:, TX + q % 2, c * P:(c + 1) * P], blk[:, q, c * P:(c + 1) * P], ident[:])
                m.then_inc(s.tx, 1)

            def step(n, q, first=False, m=None):
                j = q % 2
                if m is None or n < NB:
                    e = pe.snap(now[j], min_val=0, max_val=E - 1)
                    pe.wait_ge(s.xt, n + 1)
                    for c in range(KC):
                        g = mm(ps[:, GU + j, 0:2 * I], xbt[:, j, c * P:(c + 1) * P],
                               wgu[:, c, bass.ds(e * (2 * I), 2 * I)], start=(c == 0), stop=(c == KC - 1))
                    g.then_inc(s.gu, 1)
                if m is None or n + 1 < NB:
                    pe.reg_mov(old[1 - j], now[1 - j])
                    pe.reg_load(now[1 - j], itab[0:1, bass.ds(n + 1, 1)])
                elif n + 1 == NB:
                    pe.reg_mov(old[1 - j], now[1 - j])
                if m is None or n >= 2:
                    e2 = pe.snap(old[j], min_val=0, max_val=E - 1)
                    if m is not None and n >= NB:
                        e2 = pe.snap(old[j] if n == NB else old[j], min_val=0, max_val=E - 1)
                    pe.wait_ge(s.hts, n - 1)
                    positive(pe, s.y, n - 3)
                    mm(ps[:, DN + j, 0:D], hbt[:, j, :], wdn[:, bass.ds(e2 * D, D)]).then_inc(s.d, 1)
                if m is None or 1 <= n < NB + 1:
                    pe.wait_ge(s.h, n)
                    pe.transpose(ps[:, HT + 1 - j, 0:P], hb[:, 1 - j, :], ident[:]).then_inc(s.ht, 1)
                if m is None or n + 2 < NB:
                    tx(n + 2, (q + 2) % 4)

            tx(0, 0)
            tx(1, 1)
            return step

        def pe_experts_run(pe, s):
            step = pe_experts(pe, s)
            for n in range(4):
                step(n, n % 4, m=0)
            with pe.Fori(1, NB // 4 - 1) as g:
                for q in range(4):
                    step(g * 4 + q, q)
            for n in range(NB - 4, NB + 2):
                step(n, n % 4, m=0)

        def pe_combine(pe, s):
            def gate_up(i, q):
                pe.wait_ge(s.xs[q], 16 * (i // 4 + 1) if isinstance(i, int) else i * 4 + (16 - 4 * q))
                for k in range(4):
                    for c in range(KC):
                        m = mm(ps[:, q % 2, k * P:(k + 1) * P], wsgu[:, c, k * P:(k + 1) * P],
                               xs[:, q, c * P:(c + 1) * P], start=(c == 0), stop=(c == KC - 1))
                m.then_inc(s.gu, 1)

            def down(i, j):
                pe.wait_ge(s.h, i + 1)
                positive(pe, s.sum, i - 1)
                for c in range(SI // P):
                    m = mm(ps[:, 2 + j, 0:D], hsh[:, j, c * P:(c + 1) * P], wsd[:, c, :],
                           start=(c == 0), stop=(c == SI // P - 1))
                m.then_inc(s.d, 1)

            gate_up(0, 0)
            for i in range(3):
                gate_up(i + 1, i + 1)
                down(i, i % 2)
            with pe.Fori(1, NT // 4) as g:
                for q in range(4):
                    gate_up(g * 4 + q, q)
                    down(g * 4 + (q - 1), (q + 1) % 2)
            down(NT - 1, 1)

        def pe_means(pe):
            def body(i, j):
                pe.wait_ge(m_xn, i + 1)
                for c in range(KC):
                    m = mm(ps[:, 0, bass.ds(c * NSEG + 2 * i, 2)], rows[:, j, c * P:(c + 1) * P], seg_mean[:])
                m.then_inc(m_mm, 1)
            by_pairs(pe, NT, body)

        def pe_global(pe):
            pe.wait_ge(g_v, 1)
            xg = lambda c: xn2t[:, c * NSEG:(c + 1) * NSEG]
            for m_ in range(4):
                for c in range(KC):
                    m = mm(ps[:, 1, m_ * NSEG:(m_ + 1) * NSEG], wig[:, c, m_ * P:(m_ + 1) * P], xg(c),
                           start=(c == 0), stop=(c == KC - 1))
            m.then_inc(g_p, 1)
            for c in range(KC):
                m = mm(ps[0:NSEG, 2, 0:D], xg(c), wig[:, c, 2 * D:3 * D], start=(c == 0), stop=(c == KC - 1))
            m.then_inc(g_p, 1)
            pe.wait_ge(g_v, 2)
            for h in range(HG):
                r, c = HDG * (h % 2), h // 2
                m = mm(ps[0:NSEG, 3 + h % 2, c * NSEG:(c + 1) * NSEG], qkt[r:r + HDG, c, 0:NSEG],
                       qkt[r:r + HDG, 2 + c, 0:NSEG])
            m.then_inc(g_p, 1)
            pe.wait_ge(g_a, 2)
            for h in range(HG):
                m = pe.transpose(ps[0:NSEG, 5, h * NSEG:(h + 1) * NSEG], ssub[0:NSEG, h, :],
                                 ident[0:NSEG, 0:NSEG])
            m.then_inc(g_p, 1)
            pe.wait_ge(g_v, 4)
            for h in range(HG):
                m = mm(ps[0:NSEG, 6, h * HDG:(h + 1) * HDG], pt[0:NSEG, h, 0:NSEG],
                       osb[0:NSEG, h * HDG:(h + 1) * HDG])
            m.then_inc(g_p, 1)
            pe.wait_ge(g_v, 5)
            for c in range(KC):
                m = pe.transpose(ps[:, 7, c * NSEG:(c + 1) * NSEG], red[0][0:NSEG, c * P:(c + 1) * P],
                                 ident[0:NSEG, 0:NSEG])
            m.then_inc(g_p, 1)
            pe.wait_ge(g_v, 6)
            for c in range(KC):
                mm(ps[0:NSEG, 0, 0:D], ot[:, c * NSEG:(c + 1) * NSEG], wog[:, c, :], start=(c == 0), stop=False)
                mm(ps[0:NSEG, 0, 0:D], bvb[:, c, :], wol[:, c, :], start=False, stop=False)
                m = mm(ps[0:NSEG, 0, 0:D], bvb[:, KC + c, :], wog[:, c, :], start=False, stop=(c == KC - 1))
            m.then_inc(g_p, 1)

        def pe_attend(pe, s, i, j, route):
            pe.wait_ge(a_xn, i + 1)
            for c in range(KC):
                m = pe.transpose(ps[:, T2, c * P:(c + 1) * P], xn2[:, c * P:(c + 1) * P], ident[:])
            m.then_inc(a_xt, 1)
            pe.wait_ge(a_xts, i + 1)
            for q in range(4):
                for c in range(KC):
                    m = mm(ps[:, QK, q * P:(q + 1) * P], wil[:, c, q * P:(q + 1) * P],
                           xn2t[:, c * P:(c + 1) * P], start=(c == 0), stop=(c == KC - 1))
            m.then_inc(a_qk, 1)
            if route is not None:
                pe_route_t(pe, s, route, 1 - j)
            for c in range(KC):
                m = mm(ps[:, VO, 0:D], xn2t[:, c * P:(c + 1) * P], wil[:, c, 2 * D:3 * D],
                       start=(c == 0), stop=(c == KC - 1))
            m.then_inc(a_v, 1)
            if route is not None:
                pe_route_lg(pe, s, route, 1 - j)
            pe.wait_ge(a_qks, i + 1)
            for c in range(2):
                for g in range(2):
                    for r in range(4):
                        a, b = HDL * r, SEG * g
                        m = mm(ps[b:b + SEG, r, c * SEG:(c + 1) * SEG], qkt[a:a + HDL, c, b:b + SEG],
                               qkt[a:a + HDL, 2 + c, b:b + SEG])
            m.then_inc(a_s, 1)
            if route is not None:
                pe_route_rk(pe, s, route, 1 - j)
            pe.wait_ge(a_pr, i + 1)
            for h in range(HL):
                m = pe.transpose(ps[:, h % 4, P + (h // 4) * P:2 * P + (h // 4) * P], prob[:, h, :], ident[:])
            m.then_inc(a_pt, 1)
            pe.wait_ge(a_pts, i + 1)
            pe.wait_ge(a_vs, i + 1)
            if route is not None:
                pe.wait_ge(s.slots, route + 1)
            for h in range(HL):
                m = mm(ps[:, OL, h * (HDL + 1):(h + 1) * (HDL + 1)], pt[:, h, :], vau[:, h, :])
            m.then_inc(a_o, 1)
            pe.wait_ge(a_os, i + 1)
            for c in range(KC):
                m = pe.transpose(ps[:, c, 384:512], osb[:, c * P:(c + 1) * P], ident[:])
            m.then_inc(a_ot, 1)
            pe.wait_ge(a_ots, i + 1)
            for c in range(KC):
                mm(ps[:, VO, D:2 * D], ot[:, c * P:(c + 1) * P], wol[:, c, :], start=(c == 0), stop=False)
            pe.wait_ge(a_sel, i + 1)
            mm(ps[:, VO, D:2 * D], selt[:], glob[:], start=False, stop=True).then_inc(a_out, 1)

        def pe_pass_b(pe, s):
            pe_attend(pe, s, 0, 0, None)
            pe_attend(pe, s, 1, 1, 0)
            with pe.Fori(1, NT // 2) as pair:
                pe_attend(pe, s, pair * 2, 0, pair * 2 - 1)
                pe_attend(pe, s, pair * 2 + 1, 1, pair * 2)
            pe_route_t(pe, s, NT - 1, 1)
            pe_route_lg(pe, s, NT - 1, 1)
            pe_route_rk(pe, s, NT - 1, 1)

        def act_route_xt(act, s, i, j):
            act.wait_ge(s.xt, i + 1)
            positive(act, s.store[j], 16 * (i // 2) if isinstance(i, int) else i * 8 - 8 * j)
            act.copy(xnt[:, j, :], ps[:, T2, D:2 * D]).then_inc(s.xts, 1)

        def act_route_ex(act, s, i):
            act.wait_ge(s.lg, i + 1)
            positive(act, s.sel, i)
            act.activation(ex[:], ps[:, OL, 288:288 + E], ACT.Exp, scale=-1.0).then_inc(s.ex, 1)

        def act_route(act, s):
            def body(i, j):
                act_route_xt(act, s, i, j)
                act_route_ex(act, s, i)
            by_pairs(act, NT, body)

        def act_experts(act, s):
            def xt_copy(n, j):
                act.wait_ge(s.tx, n + 1)
                positive(act, s.gu, n - 1)
                act.copy(xbt[:, j, :], ps[:, TX + j, 0:D]).then_inc(s.xt, 1)

            def step(n, j, m=None):
                if m is None or n < NB:
                    act.wait_ge(s.gu, n + 1)
                    positive(act, s.h, n - 1)
                    act.activation(sg[:, j, :], ps[:, GU + j, 0:I], ACT.Silu).then_inc(s.sg, 1)
                if m is None or n >= 1:
                    act.wait_ge(s.ht, n)
                    positive(act, s.d, n - 2)
                    act.copy(hbt[:, 1 - j, :], ps[:, HT + 1 - j, 0:P]).then_inc(s.hts, 1)
                if m is None or n + 2 < NB:
                    xt_copy(n + 2, j)

            xt_copy(0, 0)
            xt_copy(1, 1)
            step(0, 0, m=0)
            step(1, 1, m=0)
            step(2, 0, m=0)
            step(3, 1, m=0)
            with act.Fori(2, NB // 2 - 1) as pair:
                step(pair * 2, 0)
                step(pair * 2 + 1, 1)
            for n in range(NB - 2, NB + 1):
                step(n, n % 2, m=0)

        def act_combine(act, s):
            def body(i, j):
                act.wait_ge(s.gu, i + 1)
                positive(act, s.h, i - 1)
                act.activation(ssg[:, j, :], ps[:, j, 0:SI], ACT.Silu).then_inc(s.sg, 1)
            by_pairs(act, NT, body)

        def act_global(act):
            act.wait_ge(g_p, 2)
            act.copy(osb[0:NSEG, :], ps[0:NSEG, 2, 0:D]).then_inc(g_a, 1)
            act.wait_ge(g_v, 3)
            act.activation(ssub[0:NSEG, 0:HG, :], ssub[0:NSEG, HG:2 * HG, :], ACT.Exp,
                           scale=float(HDG) ** -0.5).then_inc(g_a, 1)

        def act_attend(act, s, i, j, route):
            act.wait_ge(a_xt, i + 1)
            positive(act, a_v, i)
            act.copy(xn2t, ps[:, T2, 0:D]).then_inc(a_xts, 1)
            if route is not None:
                act_route_xt(act, s, route, 1 - j)
            act.wait_ge(a_v, i + 1)
            positive(act, a_o, i)
            act.copy(vau[:, :, 0:HDL], ps[:, VO, 0:D].rearrange("p (h d) -> p h d", h=HL)).then_inc(a_vs, 1)
            if route is not None:
                act_route_ex(act, s, route)
            positive(act, a_out, i)
            act.copy(selt[:].rearrange("s (g t) -> s g t", g=2),
                     ident[0:NSEG, bass.ds(i * 2, 2)].unsqueeze(2).to_broadcast([NSEG, 2, SEG])
                     ).then_inc(a_sel, 1)
            act.wait_ge(a_sub, i + 1)
            positive(act, a_pt, i)
            for g in range(2):
                a = act.activation(prob[g * SEG:(g + 1) * SEG, :, g * SEG:(g + 1) * SEG],
                                   ssub[g * SEG:(g + 1) * SEG, :, :], ACT.Exp, scale=float(HDL) ** -0.5)
            a.then_inc(a_pr, 1)
            act.wait_ge(a_pt, i + 1)
            positive(act, a_o, i)
            act.copy(pt.rearrange("p (c r) q -> p r c q", c=2),
                     ps[:, 0:4, P:3 * P].rearrange("p r (c q) -> p r c q", c=2)).then_inc(a_pts, 1)
            act.wait_ge(a_ot, i + 1)
            act.copy(ot.rearrange("p (c q) -> p c q", c=KC), ps[:, 0:2, 384:512]).then_inc(a_ots, 1)

        def act_pass_b(act, s):
            act_attend(act, s, 0, 0, None)
            act_attend(act, s, 1, 1, 0)
            with act.Fori(1, NT // 2) as pair:
                act_attend(act, s, pair * 2, 0, pair * 2 - 1)
                act_attend(act, s, pair * 2 + 1, 1, pair * 2)
            act_route_xt(act, s, NT - 1, 1)
            act_route_ex(act, s, NT - 1)

        def inverse_root(st, var, y, a, b):
            v = nc.vector
            st.then(v.tensor_scalar(a, var, EPS, None, ALU.add))
            st.then(v.tensor_scalar(b.bitcast(I32), a.bitcast(I32), 1, None, ALU.arith_shift_right))
            st.then(v.tensor_scalar(y.bitcast(I32), b.bitcast(I32), -1.0, float(MAGIC), ALU.mult, ALU.add))
            for _ in range(3):
                st.then(v.tensor_tensor(b, y, y, ALU.mult))
                st.then(v.tensor_tensor(b, b, a, ALU.mult))
                st.then(v.tensor_scalar(b, b, -0.5, 1.5, ALU.mult, ALU.add))
                st.then(v.tensor_tensor(y, y, b, ALU.mult))

        def tile_stats(v, st, i):
            st.then_alone(v.bn_stats(stats[:], xres[:, bass.ds(i, 1), :].rearrange("p a d -> p (a d)")), vpassed)
            st.then(v.bn_aggr(mv1[:], stats[:]))

        def xtile(i):
            return xres[:, bass.ds(i, 1), :].rearrange("p a d -> p (a d)")

        def mean_of(i):
            return mv[:, bass.ds(i, 1), 0:1].rearrange("p a b -> p (a b)")

        def v_route_norm(v, st, s, i, j, mean, inv):
            positive(v, s.scat[j], 16 * TOPK * (i // 2) if isinstance(i, int) else i * (8 * TOPK) - 8 * TOPK * j)
            v.tensor_scalar(rows[:, j, 0:D], xtile(i), mean, inv,
                            ALU.subtract, ALU.mult).then_inc(s.xn, 1)

        def v_route_pick(v, st, s, i):
            v.wait_ge(s.ex, i + 1)
            st.then(v.tensor_scalar(ex[:], ex[:], 1.0, None, ALU.add))
            st.then(v.reciprocal(sc[:], ex[:]))
            st.then(v.tensor_tensor(sfc[:], sc[:], gbias[:], ALU.add))
            st.then_alone(v.tensor_reduce(g8[:, 0, :], sfc[:].rearrange("p (g e) -> p g e", g=NG), X_AXIS, ALU.max), vpassed)
            st.then_alone(v.max(out=g8[:, 1, :], in_=g8[:, 0, :]), vpassed)
            st.then(v.max_index(out=gi8[:], in_max=g8[:, 1, :], in_values=g8[:, 0, :]))
            st.then(v.tensor_tensor(og[:], gi8[:, 0:TOPG].unsqueeze(2).to_broadcast([P, TOPG, NG]),
                                    iota_e[:, 0:NG].unsqueeze(1).to_broadcast([P, TOPG, NG]), ALU.is_equal))
            st.then(v.tensor_reduce(g8[:, 2, :], og[:].rearrange("p k g -> p g k"), X_AXIS, ALU.add))
            st.then_alone(v.tensor_tensor(msk[:, 0, :].rearrange("p (g e) -> p g e", g=NG),
                                          sfc[:].rearrange("p (g e) -> p g e", g=NG),
                                          g8[:, 2, :].unsqueeze(2).to_broadcast([P, NG, GS]), ALU.mult), vpassed)
            st.then_alone(v.max(out=t8[:], in_=msk[:, 0, :]), vpassed)
            st.then(v.max_index(out=ti8[:], in_max=t8[:], in_values=msk[:, 0, :]))
            st.then(v.tensor_tensor(oh[:], ti8[:, 0:TOPK].unsqueeze(2).to_broadcast([P, TOPK, E]),
                                    iota_e[:].unsqueeze(1).to_broadcast([P, TOPK, E]), ALU.is_equal))
            v.tensor_reduce(sel[:], oh[:].rearrange("p k e -> p e k"), X_AXIS, ALU.add).then_inc(s.sel, 1)

        def v_route_slots(v, st, s, i, j):
            v.wait_ge(s.sel, i + 1)
            st.did(v.tensor_tensor(cw[:], sc[:], sel[:], ALU.mult))
            st.then(v.tensor_tensor_scan(msk[:, 1, :], ones[:, 0:E], sel[:], 0.0, ALU.mult, ALU.add))
            st.did(v.tensor_scalar(rows[:, j, COL_DEST:ROW], msk[:, 1, :], tok6[:, bass.ds(i, 1)], None, ALU.add))
            st.then(v.tensor_reduce(csum[:, 0:1], cw[:], X_AXIS, ALU.add))
            st.then(v.tensor_scalar(csum[:, 1:2], csum[:, 0:1], 1e-20, None, ALU.add))
            st.then(v.reciprocal(csum[:, 2:3], csum[:, 1:2]))
            st.did(v.tensor_scalar(rows[:, j, COL_W:COL_W + E], cw[:], csum[:, 2:3], SCALE * HALF,
                                   ALU.mult, ALU.mult))
            v.wait_ge(s.rk, i + 1)
            st.then(v.tensor_tensor(slot[:], ps[:, OL, 320:320 + E], base[:], ALU.add))
            st.did(v.tensor_tensor(base[:], ps[:, OL, 352:352 + E], base[:], ALU.add))
            st.then(v.tensor_tensor(ohs[:], oh[:], slot[:].unsqueeze(1).to_broadcast([P, TOPK, E]), ALU.mult))
            with nc.allow_low_precision(reason="one whole number and zeros"):
                v.tensor_reduce(idx[:, j, 0:TOPK], ohs[:], X_AXIS, ALU.add).then_inc(s.slots, 1)

        def v_loop(v, st, body, first=None, per=None):
            start = st.base + st.n
            st.rebase(start)
            body(0, 0)
            one = st.n
            body(1, 1)
            assert st.n == 2 * one, (st.n, one)
            with v.Fori(1, NT // 2) as pair:
                st.rebase(pair * (2 * one) + start)
                body(pair * 2, 0)
                body(pair * 2 + 1, 1)
            st.rebase(start + NT * one)

        def v_route(v, st, s):
            st.then(v.tensor_copy(base[:], iota_cap[:]))

            def body(i, j):
                v_route_norm(v, st, s, i, j, mean_of(i), rstd[:, bass.ds(i, 1)])
                v_route_pick(v, st, s, i)
                v_route_slots(v, st, s, i, j)
            v_loop(v, st, body)

        def v_table(v, st, r, s):
            v.wait_ge(r.slots, NT)
            v.tensor_copy(ptab[:], base[0:1, :]).then_inc(s.ptab, 1)
            cnt, nb, cum = tbl[:, 0, :], tbl[:, 1, :], tbl[:, 2, :]
            st.then(v.tensor_tensor(cnt, base[:], iota_cap[:], ALU.subtract))
            st.then(v.tensor_tensor(cmp_[:], cnt.unsqueeze(2).to_broadcast([P, E, E]),
                                    iota_thr[:].unsqueeze(1).to_broadcast([P, E, E]), ALU.is_gt))
            st.then(v.tensor_reduce(nb, cmp_[:], X_AXIS, ALU.add))
            st.then(v.tensor_tensor_scan(cum, ones[:, 0:E], nb, 0.0, ALU.mult, ALU.add))
            for h in range(2):
                ge, start = tbl[:, 3, :], tbl[:, 4, :]
                ecol, scol, fcol = (tcol[:, 3 * h + k:3 * h + k + 1] for k in range(3))
                st.then(v.tensor_scalar(ge, cum, iota_blk[:, h:h + 1], None, ALU.is_le))
                st.did(v.tensor_reduce(ecol, ge, X_AXIS, ALU.add))
                st.then(v.tensor_tensor(start, ge, cum, ALU.mult))
                st.then(v.tensor_reduce(scol, start, X_AXIS, ALU.max))
                st.then(v.tensor_tensor(fcol, iota_blk[:, h:h + 1], scol, ALU.subtract))
                st.then(v.tensor_scalar(fcol, fcol, float(P), None, ALU.mult))
                st.then(v.tensor_scalar(tcol[:, 6 + h:7 + h], ecol, float(CAP), None, ALU.mult))
                st.then(v.tensor_tensor(fcol, fcol, tcol[:, 6 + h:7 + h], ALU.add))
                st.then(v.tensor_scalar(fcol, fcol, float(DUMMY), None, ALU.min))
                st.then(v.tensor_scalar(ecol, ecol, float(E - 1), None, ALU.min))
                st.did(v.tensor_scalar(diag[:, h, :], ident[:], ecol, None, ALU.mult))
                st.then(v.tensor_scalar(diag[:, 2 + h, :], ident[:], fcol, None, ALU.mult))
            v.sem_inc(s.cnt, 1)
            v.wait_ge(s.bc, 1)
            st.did(v.tensor_copy(etab[:], ps[:, 0, 0:2 * P]))
            st.then(v.tensor_copy(itab[:], ps[0:1, 0, :]))
            v.sem_inc(s.tab, 1)

        def v_experts(v, st, s):
            start = st.base + st.n
            st.rebase(start)

            def pick(n, q):
                v.wait_ge(s.ld[q], 16 * (n // 4 + 1) if isinstance(n, int) else n * 4 + (16 - 4 * q))
                positive(v, s.pick, n * 2)
                positive(v, s.h, n - 3)
                for k, (col, out_) in enumerate(((COL_W, wcol), (COL_DEST, dcol))):
                    v.scalar_tensor_tensor(
                        out=picked[:, k, :], in0=iota_e[:], scalar=etab[:, bass.ds(n, 1)],
                        in1=blk[:, q, col:col + E], op0=ALU.is_equal, op1=ALU.mult,
                        accum_out=out_[:, q:q + 1]).then_inc(s.pick, 1)

            def step(n, q, m=None):
                j = q % 2
                if m is None or n < NB:
                    v.wait_ge(s.sg, n + 1)
                    positive(v, s.ht, n - 1)
                    v.wait_ge(s.pick, n * 2 + 2)
                    v.scalar_tensor_tensor(out=hb[:, j, :], in0=ps[:, GU + j, I:2 * I],
                                           scalar=wcol[:, q:q + 1], in1=sg[:, j, :],
                                           op0=ALU.mult, op1=ALU.mult).then_inc(s.h, 1)
                if m is None or n >= 2:
                    k = (q + 2) % 4
                    positive(v, s.scat[k],
                             16 * ((n - 2) // 4) if isinstance(n, int) else n * 4 - (8 + 4 * k))
                    st.did(v.tensor_copy(didx[:, k:k + 1], dcol[:, k:k + 1]))
                    v.wait_ge(s.d, n - 1)
                    v.tensor_copy(yb[:, k, :], ps[:, DN + j, 0:D]).then_inc(s.y, 1)
                    st.sync()
                if m is None or n + 2 < NB:
                    pick(n + 2, (q + 2) % 4)

            pick(0, 0)
            pick(1, 1)
            for n in range(4):
                step(n, n % 4, m=0)
            one = 1
            with v.Fori(1, NB // 4 - 1) as g:
                for q in range(4):
                    st.rebase(g * (4 * one) + (start + q - 2))
                    step(g * 4 + q, q)
            st.rebase(start + NB - 4 - 2)
            for n in range(NB - 4, NB + 2):
                step(n, n % 4, m=0)

        def v_combine(v, st, s, last):
            def hidden(i, j):
                v.wait_ge(s.sg, i + 1)
                positive(v, s.d, i - 1)
                v.tensor_tensor(hsh[:, j, :], ssg[:, j, :], ps[:, j, SI:2 * SI], ALU.mult).then_inc(s.h, 1)

            def stats_of(i):
                v.wait_ge(s.sum, i + 1)
                v.sem_inc(vpassed, 1)
                st.did(v.bn_stats(stats[:], xtile(i)))

            def finish_stats(i):
                st.then(v.bn_aggr(mv1[:], stats[:]))
                st.did(v.tensor_copy(mv[:, bass.ds(i, 1), :].rearrange("p a d -> p (a d)"), mv1[:]))

            def final(i, j):
                v.wait_ge(s.part, i + 1)
                v.wait_ge(s.d, i + 1)
                v.scalar_tensor_tensor(out=xtile(i), in0=ps[:, 2 + j, 0:D], scalar=HALF, in1=xtile(i),
                                       op0=ALU.mult, op1=ALU.add).then_inc(s.sum, 1)

            def body(i, j, m=None):
                if m is None or i + 1 < NT:
                    hidden(i + 1, 1 - j)
                stats_now = not last and (m is None or i >= 2)
                if stats_now:
                    stats_of(i - 2)
                v.wait_ge(s.ans[j], 16 * (i // 2 + 1) if isinstance(i, int) else i * 8 + (16 - 8 * j))
                positive(v, s.part, i - 1)
                v.tensor_reduce(red[j], ans[:, j, :].rearrange("p (k d) -> p d k", k=TOPK),
                                X_AXIS, ALU.add).then_inc(s.red, 1)
                if stats_now:
                    st.sync()
                    v.sem_inc(vpassed, 1)
                    finish_stats(i - 2)
                if m is None or i >= 1:
                    final(i - 1, 1 - j)

            hidden(0, 0)
            body(0, 0, m=0)
            body(1, 1, m=0)
            start = st.base + st.n
            n0 = st.n
            body(2, 0, m=0)
            one = st.n - n0
            body(3, 1, m=0)
            with v.Fori(2, NT // 2 - 1) as pair:
                st.rebase(pair * (2 * one) + (start - 2 * one))
                body(pair * 2, 0)
                body(pair * 2 + 1, 1)
            st.rebase(start + (NT - 4) * one)
            body(NT - 2, 0, m=0)
            body(NT - 1, 1, m=0)
            final(NT - 1, 1)
            if not last:
                for i in range(NT - 2, NT):
                    stats_of(i)
                    st.sync()
                    v.sem_inc(vpassed, 1)
                    finish_stats(i)

        def v_means(v, st):
            st.sync()
            inverse_root(st, mv[:, :, 1], rstd[:], newt[:, 0, :], newt[:, 1, :])

            def body(i, j):
                positive(v, m_mm, i - 1)
                v.tensor_scalar(rows[:, j, 0:D], xtile(i), mean_of(i), rstd[:, bass.ds(i, 1)],
                                ALU.subtract, ALU.mult).then_inc(m_xn, 1)
            v_loop(v, st, body)

        def v_global(v, st):
            v.wait_ge(m_mm, NT)
            for k, b in enumerate((bil, big)):
                for c in range(KC):
                    st.did(v.tensor_copy(bvb[:, k * KC + c, :],
                                         b[:, 2 * KC + c:2 * KC + c + 1].to_broadcast([P, NSEG])))
            st.then(v.tensor_copy(xn2t[:, 0:KC * NSEG], ps[:, 0, 0:KC * NSEG]))
            v.sem_inc(g_v, 1)
            v.wait_ge(g_p, 2)
            v.tensor_tensor(qkt[:, :, 0:NSEG], ps[:, 1, 0:4 * NSEG].rearrange("p (m t) -> p m t", m=4),
                            big[:, 0:4].unsqueeze(2).to_broadcast([P, 4, NSEG]), ALU.add).then_inc(g_v, 1)
            v.wait_ge(g_p, 3)
            sview = ps[0:NSEG, 3:5, 0:2 * NSEG].rearrange("p r (c k) -> p r c k", c=2)
            mview = smax[0:NSEG, 0:HG].rearrange("p (c r) -> p r c", c=2)
            st.then(v.tensor_reduce(mview, sview, X_AXIS, ALU.max))
            v.tensor_tensor(ssub[0:NSEG, HG:2 * HG, :].rearrange("p (c r) k -> p r c k", c=2), sview,
                            mview.unsqueeze(3).to_broadcast([NSEG, 2, 2, NSEG]), ALU.subtract).then_inc(g_v, 1)
            v.wait_ge(g_a, 2)
            st.then(v.tensor_reduce(smax[0:NSEG, 0:HG], ssub[0:NSEG, 0:HG, :], X_AXIS, ALU.add))
            st.then(v.reciprocal(rden[0:NSEG, 0:HG], smax[0:NSEG, 0:HG]))
            v.wait_ge(g_p, 4)
            v.tensor_copy(pt[0:NSEG, 0:HG, 0:NSEG],
                          ps[0:NSEG, 5, 0:HG * NSEG].rearrange("p (h q) -> p h q", h=HG)).then_inc(g_v, 1)
            v.wait_ge(g_p, 5)
            v.tensor_tensor(red[0][0:NSEG, :].rearrange("p (h d) -> p h d", h=HG),
                            ps[0:NSEG, 6, 0:D].rearrange("p (h d) -> p h d", h=HG),
                            rden[0:NSEG, 0:HG].unsqueeze(2).to_broadcast([NSEG, HG, HDG]),
                            ALU.mult).then_inc(g_v, 1)
            v.wait_ge(g_p, 6)
            v.tensor_copy(ot[:, 0:KC * NSEG], ps[:, 7, 0:KC * NSEG]).then_inc(g_v, 1)
            v.wait_ge(g_p, 7)
            st.then(v.tensor_tensor(glob[:], ps[0:NSEG, 0, 0:D], bout[0:NSEG, 0, :], ALU.add))
            v.tensor_tensor(glob[:], glob[:], bout[0:NSEG, 1, :], ALU.add).then_inc(g_v, 1)

        def v_attend(v, st, s, i, j, route):
            positive(v, a_xt, i)
            v.tensor_scalar(xn2, xtile(i), mean_of(i), rstd[:, bass.ds(i, 1)],
                            ALU.subtract, ALU.mult).then_inc(a_xn, 1)
            if route is not None:
                v.wait_ge(a_x2, route + 1)
                v.sem_inc(vpassed, 1)
                tile_stats(v, st, route)
                inverse_root(st, mv1[:, 1:2], rstd1[:], newt[:, 0, 0:1], newt[:, 1, 0:1])
                v_route_norm(v, st, s, route, 1 - j, mv1[:, 0:1], rstd1[:])
            v.wait_ge(a_qk, i + 1)
            v.tensor_tensor(qkt, ps[:, QK, :].rearrange("p (m t) -> p m t", m=4),
                            bil[:, 0:4].unsqueeze(2).to_broadcast([P, 4, P]), ALU.add).then_inc(a_qks, 1)
            if route is not None:
                v_route_pick(v, st, s, route)
            v.wait_ge(a_s, i + 1)
            sview = ps[:, 0:4, 0:2 * SEG].rearrange("p r (c k) -> p r c k", c=2)
            mview = smax[:].rearrange("p (c r) -> p r c", c=2)
            st.then(v.tensor_reduce(mview, sview, X_AXIS, ALU.max))
            v.tensor_tensor(ssub.rearrange("p (c r) k -> p r c k", c=2), sview,
                            mview.unsqueeze(3).to_broadcast([P, 4, 2, SEG]), ALU.subtract).then_inc(a_sub, 1)
            if route is not None:
                v_route_slots(v, st, s, route, 1 - j)
            v.wait_ge(a_o, i + 1)
            oview = ps[:, OL, 0:HL * (HDL + 1)].rearrange("p (h d) -> p h d", h=HL)
            st.then(v.reciprocal(rden[:].unsqueeze(2), oview[:, :, HDL:HDL + 1]))
            v.tensor_tensor(osb.rearrange("p (h d) -> p h d", h=HL), oview[:, :, 0:HDL],
                            rden[:].unsqueeze(2).to_broadcast([P, HL, HDL]), ALU.mult).then_inc(a_os, 1)
            v.wait_ge(a_out, i + 1)
            v.tensor_tensor(xtile(i), ps[:, VO, D:2 * D], xtile(i), ALU.add).then_inc(a_x2, 1)

        def v_pass_b(v, st, s):
            st.then(v.tensor_copy(base[:], iota_cap[:]))
            v_attend(v, st, s, 0, 0, None)
            start = st.base + st.n
            st.rebase(start)
            v_attend(v, st, s, 1, 1, 0)
            one = st.n
            with v.Fori(1, NT // 2) as pair:
                st.rebase(pair * (2 * one) + (start - one))
                v_attend(v, st, s, pair * 2, 0, pair * 2 - 1)
                v_attend(v, st, s, pair * 2 + 1, 1, pair * 2)
            st.rebase(start + (NT - 1) * one)
            i, j = NT - 1, 1
            v.wait_ge(a_x2, NT)
            tile_stats(v, st, i)
            inverse_root(st, mv1[:, 1:2], rstd1[:], newt[:, 0, 0:1], newt[:, 1, 0:1])
            v_route_norm(v, st, s, i, j, mv1[:, 0:1], rstd1[:])
            v_route_pick(v, st, s, i)
            v_route_slots(v, st, s, i, j)

        def v_first(v, st):
            for h in range(2):
                v.wait_ge(ld_x[h], 16)
                for i in range(h * NT // 2, (h + 1) * NT // 2):
                    tile_stats(v, st, i)
                    st.then(v.tensor_copy(mv[:, i, :], mv1[:]))
            v.wait_ge(consts, N_CONST)
            v.wait_ge(ld_small, N_SMALL)
            inverse_root(st, mv[:, :, 1], rstd[:], newt[:, 0, :], newt[:, 1, :])

        out_tiles = out.rearrange("b (n p) d -> p (b n) d", p=P)

        @block.sync
        def _(sp):
            load_inputs(sp)
            sp_route(sp, R[0])
            pad_experts(sp, X[0], 0)
            sp_experts(sp, R[0], X[0])
            sp_combine(sp, X[0], C[0], R[0], False)
            sp_route(sp, R[1])
            pad_experts(sp, X[1], 0)
            sp_experts(sp, R[1], X[1])
            sp_combine(sp, X[1], C[1], R[1], True)

        @block.gpsimd
        def _(pool):
            make_consts(pool)
            pool_route(pool, R[0])
            pool_experts(pool, X[0])
            pool_combine(pool, C[0])
            pool_route(pool, R[1])
            pool_experts(pool, X[1])
            pool_combine(pool, C[1])

        @block.tensor
        def _(pe):
            pe.wait_ge(consts, N_CONST)
            pe.wait_ge(ld_small, N_SMALL)
            pe_route(pe, R[0])
            pe_table(pe, X[0])
            pe_experts_run(pe, X[0])
            pe_combine(pe, C[0])
            pe_means(pe)
            pe_global(pe)
            pe.wait_ge(g_v, 7)
            pe_pass_b(pe, R[1])
            pe_table(pe, X[1])
            pe_experts_run(pe, X[1])
            pe_combine(pe, C[1])

        @block.scalar
        def _(act):
            act.wait_ge(consts, N_CONST)
            act_route(act, R[0])
            pad_experts(act, X[0], 1)
            act_experts(act, X[0])
            act_combine(act, C[0])
            act_global(act)
            act.wait_ge(g_v, 7)
            act_pass_b(act, R[1])
            pad_experts(act, X[1], 1)
            act_experts(act, X[1])
            act_combine(act, C[1])
            for k in range(4):
                n = NT // 4
                act.wait_ge(C[1].sum, (k + 1) * n)
                act.dma_start(out_tiles[:, k * n:(k + 1) * n, :],
                              xres[:, k * n:(k + 1) * n, :]).then_inc(C[1].out, 16)
            act.wait_ge(C[1].out, 64)

        @block.vector
        def _(v):
            st = Steps(v, vstep)
            v_first(v, st)
            v_route(v, st, R[0])
            v_table(v, st, R[0], X[0])
            v_experts(v, st, X[0])
            v_combine(v, st, C[0], False)
            v_means(v, st)
            v_global(v, st)
            v_pass_b(v, st, R[1])
            v_table(v, st, R[1], X[1])
            v_experts(v, st, X[1])
            v_combine(v, st, C[1], True)


def kernel(L0_attn_x, L0_attn_w_in_local, L0_attn_b_in_local, L0_attn_w_out_local, L0_attn_b_out_local,
           L0_attn_w_in_global, L0_attn_b_in_global, L0_attn_w_out_global, L0_attn_b_out_global,
           L0_ffn_gate_weight, L0_ffn_e_score_correction_bias, L0_ffn_experts_gate_up, L0_ffn_experts_down,
           L0_ffn_shared_gate_w, L0_ffn_shared_up_w, L0_ffn_shared_down_w):
    from concourse import bacc
    from concourse.bass_utils import run_bass_kernel_spmd

    c = np.ascontiguousarray
    arrays = {
        "in_x": c(L0_attn_x),
        "in_gate": c(np.asarray(L0_ffn_gate_weight).T),
        "in_gate_bias": c(L0_ffn_e_score_correction_bias),
        "in_gate_up": c(np.asarray(L0_ffn_experts_gate_up).transpose(2, 0, 1)).reshape(KC, P, E * 2 * I),
        "in_down": c(np.asarray(L0_ffn_experts_down).transpose(2, 0, 1)).reshape(I, E * D),
        "in_shared_gate": c(np.asarray(L0_ffn_shared_gate_w).T),
        "in_shared_up": c(np.asarray(L0_ffn_shared_up_w).T),
        "in_shared_down": c(np.asarray(L0_ffn_shared_down_w).T),
        "in_wi_local": c(np.asarray(L0_attn_w_in_local).T),
        "in_bi_local": c(L0_attn_b_in_local),
        "in_wo_local": c(np.asarray(L0_attn_w_out_local).T),
        "in_bo_local": c(L0_attn_b_out_local),
        "in_wi_global": c(np.asarray(L0_attn_w_in_global).T),
        "in_bi_global": c(L0_attn_b_in_global),
        "in_wo_global": c(np.asarray(L0_attn_w_out_global).T),
        "in_bo_global": c(L0_attn_b_out_global),
    }
    nc = bacc.Bacc("TRN2", target_bir_lowering=False, num_devices=1)
    args = [nc.dram_tensor(n, a.shape, F32, kind="ExternalInput").ap() for n, a in arrays.items()]
    args.append(nc.dram_tensor("out", L0_attn_x.shape, F32, kind="ExternalOutput").ap())
    build(nc, *args)
    r = run_bass_kernel_spmd(nc, [arrays], core_ids=[0])
    return r.results[0]["out"]
```

```python
from contextlib import ExitStack

import numpy as np

import concourse.bass as bass
from concourse import mybir

F32 = mybir.dt.float32
I32 = mybir.dt.int32
U32 = mybir.dt.uint32
ALU = mybir.AluOpType
ACT = mybir.ActivationFunctionType
X_AXIS = mybir.AxisListType.X

P = 128
D = 256
KC = D // P
T = 4096
NT = T // P
E = 32
I = 128
SI = 256
TOPK = 6
NG = 8
GS = E // NG
TOPG = 4
SCALE = 2.5
HALF = 0.5
SEG = 64
NSEG = T // SEG
HL, HDL = 8, 32
HG, HDG = 4, 64
EPS = 1e-5

ROW = D + 2 * E
COL_W, COL_DEST = D, D + E
CAP = T + P
DUMMY = E * CAP
NOWHERE = 2 * T * TOPK
NB = 224
MAGIC = 0x5F3759DF


def positive(eng, sem, value):
    if isinstance(value, int) and value <= 0:
        return
    eng.wait_ge(sem, value)


def by_pairs(eng, n, body):
    body(0, 0)
    body(1, 1)
    with eng.Fori(1, n // 2) as pair:
        body(pair * 2, 0)
        body(pair * 2 + 1, 1)


def visits(i, r, n, per):
    return per * (i // n) if isinstance(i, int) else i * (per // n) - (per // n) * r


def exists(i):
    return not isinstance(i, int) or 0 <= i < NT


def pair_exists(p):
    return not isinstance(p, int) or 0 <= p < NT // 2


def pairs_by_two(eng, body, last):
    body(0, 0)
    body(1, 1)
    with eng.Fori(1, NT // 4 - 1) as g:
        body(g * 2, 0)
        body(g * 2 + 1, 1)
    for p in range(NT // 2 - 2, last):
        body(p, p % 2)


class Steps:

    def __init__(self, eng, sem):
        self.eng, self.sem, self.base, self.n = eng, sem, 0, 0

    def rebase(self, base):
        self.base, self.n = base, 0

    def did(self, ins):
        ins.then_inc(self.sem, 1)
        self.n += 1

    def sync(self):
        self.eng.wait_ge(self.sem, self.base + self.n)

    def then(self, ins):
        self.did(ins)
        self.sync()

    def then_alone(self, ins, passed):
        self.then(ins)
        self.eng.sem_inc(passed, 1)


def build(nc, x_in, gate_t, gate_bias, wgu_in, wdn_in, wsg_in, wsu_in, wsd_in,
          wi_l, bi_l, wo_l, bo_l, wi_g, bi_g, wo_g, bo_g, out):
    ctx = ExitStack()
    with ctx:
        def sb(name, shape, dt=F32):
            return ctx.enter_context(nc.sbuf_tensor(name, shape, dt))

        def sem(name):
            return ctx.enter_context(nc.semaphore(name))

        rows_dram = nc.dram_tensor("dispatch_rows", [DUMMY + P, ROW], F32).ap()
        answers_dram = nc.dram_tensor("answers", [T * TOPK, D], F32).ap()
        xnt_dram = nc.dram_tensor("normed_transposed", [NT, P, D], F32).ap()

        wgu = sb("wgu", [P, KC, E * 2 * I])
        wdn = sb("wdn", [P, E * D])
        wsgu = sb("wsgu", [P, KC, 2 * SI])
        wsd = sb("wsd", [P, SI // P, D])
        wgate = sb("wgate", [P, KC, E])
        wil = sb("wil", [P, KC, 3 * D])
        wol = sb("wol", [P, KC, D])
        wig = sb("wig", [P, KC, 3 * D])
        wog = sb("wog", [P, KC, D])
        bil = sb("bil", [P, 3 * KC])
        big = sb("big", [P, 3 * KC])
        bout = sb("bout", [P, 2, D])
        gbias = sb("gbias", [P, E])
        ident = sb("ident", [P, P])
        ones = sb("ones", [P, P])
        before = sb("before", [P, P])
        seg_mean = sb("seg_mean", [P, 2])
        iota_e = sb("iota_e", [P, E])
        iota_cap = sb("iota_cap", [P, E])
        iota_thr = sb("iota_thr", [P, E])
        iota_blk = sb("iota_blk", [P, 2])
        tok6 = sb("tok6", [P, NT])
        magic = sb("magic", [P, 1])
        padt = sb("padt", [P, ROW])

        xres = sb("xres", [P, NT, D])
        mv = sb("mv", [P, NT, 2])
        rstd = sb("rstd", [P, NT])
        newt = sb("newt", [P, 3, NT])
        stats = sb("stats", [P, 6])
        mv1 = sb("mv1", [P, 2])
        mv2 = sb("mv2", [P, 2, 2])
        stats2 = sb("stats2", [P, 2, 6])
        rstd2 = sb("rstd2", [P, 2])

        xnt = sb("xnt", [P, 2, D])
        ex = sb("ex", [P, 2, E])
        sc = sb("sc", [P, 2, E])
        sfc = sb("sfc", [P, 2, E])
        gmax = sb("gmax", [P, 2, NG])
        gtop = sb("gtop", [P, 2, 8])
        gi8 = sb("gi8", [P, 2, 8], U32)
        og = sb("og", [P, 2, TOPG, NG])
        gkeep = sb("gkeep", [P, 2, NG])
        t8 = sb("t8", [P, 2, 8])
        ti8 = sb("ti8", [P, 2, 8], U32)
        oh = sb("oh", [P, 2, TOPK, E])
        ohs = sb("ohs", [P, 2, TOPK, E])
        msk = sb("msk", [P, 2, E])
        nth = sb("nth", [P, 2, E])
        sel = sb("sel", [P, 2, E])
        cw = sb("cw", [P, 2, E])
        csum = sb("csum", [P, 3, 2])
        slot = sb("slot", [P, 2, E])
        base = sb("base", [P, E])
        idx = sb("idx", [P, 4, 8], I32)

        tbl = sb("tbl", [P, 6, E])
        tcol = sb("tcol", [P, 12])
        etab = sb("etab", [P, 2 * P])
        itab = sb("itab", [1, 4 * P], I32)
        ptab = sb("ptab", [1, E], I32)

        blk = sb("blk", [P, 4, ROW])
        rows = blk
        xbt = sb("xbt", [P, 2, D])
        sg = sb("sg", [P, 2, I])
        hb = sb("hb", [P, 2, I])
        hbt = sb("hbt", [P, 2, I])
        yb = sb("yb", [P, 4, D])
        picked = sb("picked", [P, 2, E])
        wcol = sb("wcol", [P, 4])
        dcol = sb("dcol", [P, 4])
        didx = sb("didx", [P, 4], I32)

        ans = sb("ans", [P, 2, TOPK * D])
        red = [sb("red", [P, D])[:], hb[:].rearrange("p j i -> p (j i)")]
        xn = yb
        xs = yb
        ssg = sb("ssg", [P, 2, SI])
        hsh = sb("hsh", [P, 2, SI])
        diag = ssg[:].rearrange("p j (a b) -> p (j a) b", a=2)

        flat = ans[:].rearrange("p j n -> p (j n)")
        cmp_ = flat[:, 0:E * E].rearrange("p (e j) -> p e j", e=E)
        at = [0]

        def share(*shape):
            n = int(np.prod(shape))
            v = flat[:, at[0]:at[0] + n]
            at[0] += n
            if len(shape) == 2:
                v = v.rearrange("p (a b) -> p a b", a=shape[0])
            return v

        xn2 = share(D)
        xn2t = share(D)
        qkt = share(4, P)
        ssub = share(HL, SEG)
        pt = share(HL, P)
        osb = share(D)
        ot = share(D)
        vau = sb("vau", [P, HL, HDL + 1])
        smax = sb("smax", [P, HL])
        prob = sb("prob", [P, HL, P])
        rden = sb("rden", [P, HL])
        selt = sb("selt", [NSEG, P])
        glob = sb("glob", [NSEG, D])
        bvb = sb("bvb", [P, 2 * KC, NSEG])

        ps = ctx.enter_context(nc.psum_tensor("ps", [P, 8, 512], F32))

        ld_x = [sem("ld_x0"), sem("ld_x1")]
        ld_small = sem("ld_small")
        ld_exp = sem("ld_exp")
        consts = sem("consts")
        vstep = sem("vector_step")
        vpassed = sem("vector_passed")
        pstep = sem("pool_step")

        block = ctx.enter_context(nc.Block())

        class RouteSems:
            def __init__(self, n):
                s = lambda name: sem(f"{name}_{n}")
                self.xn = s("rt_xn")
                self.xt = s("rt_xt")
                self.xts = s("rt_xts")
                self.store = [s("rt_store0"), s("rt_store1")]
                self.lg = s("rt_lg")
                self.ex = s("rt_ex")
                self.sel = s("rt_sel")
                self.rk = s("rt_rk")
                self.rkr = s("rt_rkr")
                self.rx = s("rt_rx")
                self.slots = s("rt_slots")
                self.take = s("rt_take")
                self.scat = [s(f"rt_scat{q}") for q in range(4)]

        class ExpertSems:
            def __init__(self, n):
                self.n = n
                s = lambda name: sem(f"{name}_{n}")
                self.cnt = s("tb_diag")
                self.bc = s("tb_bc")
                self.tab = s("tb_tab")
                self.ptab = s("tb_ptab")
                self.pad = [s("tb_pad_sp"), s("tb_pad_act")]
                self.ld = [s(f"ex_ld{q}") for q in range(4)]
                self.tx = s("ex_tx")
                self.xt = s("ex_xt")
                self.pick = s("ex_pick")
                self.gu = s("ex_gu")
                self.sg = s("ex_sg")
                self.h = s("ex_h")
                self.ht = s("ex_ht")
                self.hts = s("ex_hts")
                self.d = s("ex_d")
                self.y = s("ex_y")
                self.take = s("ex_take")
                self.scat = [s(f"ex_scat{q}") for q in range(4)]

        class CombineSems:
            def __init__(self, n):
                s = lambda name: sem(f"{name}_{n}")
                self.ans = [s("cb_ans0"), s("cb_ans1")]
                self.xs = [s(f"cb_xs{q}") for q in range(4)]
                self.gu = s("cb_gu")
                self.sg = s("cb_sg")
                self.h = s("cb_h")
                self.d = s("cb_d")
                self.red = s("cb_red")
                self.part = s("cb_part")
                self.sum = s("cb_sum")
                self.out = s("cb_out")

        R = [RouteSems(n) for n in range(2)]
        X = [ExpertSems(n) for n in range(2)]
        C = [CombineSems(n) for n in range(2)]
        m_xn = sem("mean_xn")
        m_mm = sem("mean_mm")
        g_v = sem("glob_vector")
        g_p = sem("glob_tensor")
        g_a = sem("glob_scalar")
        a_xn = sem("at_xn")
        a_xt = sem("at_xt")
        a_xts = sem("at_xts")
        a_qk = sem("at_qk")
        a_qks = sem("at_qks")
        a_v = sem("at_v")
        a_vs = sem("at_vs")
        a_s = sem("at_s")
        a_sub = sem("at_sub")
        a_pr = sem("at_prob")
        a_pt = sem("at_pt")
        a_pts = sem("at_pts")
        a_o = sem("at_o")
        a_os = sem("at_os")
        a_ot = sem("at_ot")
        a_ots = sem("at_ots")
        a_sel = sem("at_sel")
        a_out = sem("at_out")
        a_x2 = sem("at_x2")

        N_SMALL = 16 * 14

        def load_inputs(sp):
            x_tiles = x_in.rearrange("b (n p) d -> p (b n) d", p=P)
            sp.dma_start(wgate[:], gate_t.rearrange("(c p) e -> p c e", p=P)).then_inc(ld_small, 16)
            for h in range(2):
                half = NT // 2
                sp.dma_start(xres[:, h * half:(h + 1) * half, :],
                             x_tiles[:, h * half:(h + 1) * half, :]).then_inc(ld_x[h], 16)
            sp.dma_start(gbias[:], gate_bias.rearrange("(a e) -> a e", a=1).to_broadcast([P, E])
                         ).then_inc(ld_small, 16)
            sp.dma_start(wsgu[:, :, 0:SI], wsg_in.rearrange("(c p) s -> p c s", p=P)).then_inc(ld_small, 16)
            sp.dma_start(wsgu[:, :, SI:2 * SI], wsu_in.rearrange("(c p) s -> p c s", p=P)).then_inc(ld_small, 16)
            sp.dma_start(wsd[:], wsd_in.rearrange("(c p) d -> p c d", p=P)).then_inc(ld_small, 16)
            for dst, src in ((wil, wi_l), (wol, wo_l), (wig, wi_g), (wog, wo_g)):
                sp.dma_start(dst[:], src.rearrange("(c p) d -> p c d", p=P)).then_inc(ld_small, 16)
            with nc.allow_non_contiguous_dma(reason="biases to partitions, once"):
                sp.dma_start(bil[:], bi_l.rearrange("(c p) -> p c", p=P)).then_inc(ld_small, 16)
                sp.dma_start(big[:], bi_g.rearrange("(c p) -> p c", p=P)).then_inc(ld_small, 16)
            for k, b in enumerate((bo_l, bo_g)):
                sp.dma_start(bout[:, k, :], b.rearrange("(a d) -> a d", a=1).to_broadcast([P, D])
                             ).then_inc(ld_small, 16)
            sp.dma_start(wdn[:], wdn_in).then_inc(ld_exp, 16)
            sp.wait_ge(consts, N_CONST)
            sp.dma_start(rows_dram[DUMMY:DUMMY + P, :], padt[:]).then_inc(ld_small, 16)
            sp.dma_start(wgu[:, 0, :], wgu_in[0]).then_inc(ld_exp, 16)
            sp.dma_start(wgu[:, 1, :], wgu_in[1]).then_inc(ld_exp, 16)

        def sp_route(sp, s):
            def body(i, j):
                sp.wait_ge(s.xts, i + 1)
                sp.dma_start(xnt_dram[bass.ds(i, 1)].rearrange("a p d -> (a p) d"),
                             xnt[:, j, :]).then_inc(s.store[j], 16)
            by_pairs(sp, NT, body)

        def pad_experts(eng, s, half):
            eng.wait_ge(s.ptab, 1)
            with eng.Fori(0, E // 2) as k:
                first = eng.value_load(ptab[0:1, bass.ds(k * 2 + half, 1)], min_val=0, max_val=DUMMY - P)
                eng.dma_start(rows_dram[bass.ds(first, P), :], padt[:]).then_inc(s.pad[half], 16)

        def sp_experts(sp, r, s):
            sp.wait_ge(s.tab, 1)
            for q in range(4):
                sp.wait_ge(r.scat[q], 16 * TOPK * (NT // 4))
            for j in range(2):
                sp.wait_ge(s.pad[j], 16 * (E // 2))
            sp.wait_ge(ld_small, N_SMALL)

            def body(g, peeled):
                for q in range(4):
                    n = g * 4 + q
                    first = sp.value_load(itab[0:1, bass.ds(n + 2 * P, 1)], min_val=0, max_val=DUMMY)
                    if not peeled:
                        sp.wait_ge(s.tx, n - 3)
                        sp.wait_ge(s.pick, n * 2 - 6)
                    sp.dma_start(blk[:, q, :], rows_dram[bass.ds(first, P), :]).then_inc(s.ld[q], 16)
            body(0, True)
            with sp.Fori(1, NB // 4) as g:
                body(g, False)

        def sp_combine(sp, x, s, r, last):
            for q in range(4):
                sp.wait_ge(x.scat[q], 16 * (NB // 4))
            for j in range(2):
                sp.wait_ge(r.store[j], 16 * (NT // 2))
            ans_v = answers_dram.rearrange("(n p k) d -> n p (k d)", p=P, k=TOPK)

            def load_tokens(i, q):
                sp.dma_start(xs[:, q, :], xnt_dram[bass.ds(i, 1)].rearrange("a p d -> (a p) d")
                             ).then_inc(s.xs[q], 16)

            def load_answers(i, j):
                positive(sp, s.red, i - 1)
                sp.dma_start(ans[:, j, :], ans_v[bass.ds(i, 1)].rearrange("a p d -> (a p) d")
                             ).then_inc(s.ans[j], 16)

            for q in range(4):
                load_tokens(q, q)
            for q in range(2):
                load_answers(q, q % 2)
            with sp.Fori(0, NT // 4 - 1) as g:
                for q in range(4):
                    i = g * 4 + (q + 4)
                    sp.wait_ge(s.gu, i - 3)
                    load_tokens(i, q)
                    load_answers(i - 2, q % 2)
            for q in range(2, 4):
                load_answers(NT - 4 + q, q % 2)

        def make_consts(pool):
            st = Steps(pool, pstep)
            st.did(pool.memset(ones[:], 1.0))
            st.did(pool.memset(padt[:, 0:COL_DEST], 0.0))
            st.did(pool.memset(padt[:, COL_DEST:ROW], float(NOWHERE)))
            st.did(pool.memset(prob[:], 0.0))
            st.did(pool.memset(vau[:, :, HDL:HDL + 1], 1.0))
            st.did(pool.memset(seg_mean[:], 1.0 / SEG))
            st.sync()
            pool.affine_select(out=ident[:], in_=ones[:], compare_op=ALU.is_equal, fill=0.0, base=0,
                               pattern=[[-1, P]], channel_multiplier=1).then_inc(consts, 1)
            pool.affine_select(out=before[:], in_=ones[:], compare_op=ALU.is_gt, fill=0.0, base=0,
                               pattern=[[1, P]], channel_multiplier=-1).then_inc(consts, 1)
            st.then(pool.affine_select(out=seg_mean[:, 0:1], in_=seg_mean[:, 0:1], compare_op=ALU.is_gt,
                                       fill=0.0, base=SEG, pattern=[[0, 1]], channel_multiplier=-1))
            pool.affine_select(out=seg_mean[:, 1:2], in_=seg_mean[:, 1:2], compare_op=ALU.is_ge,
                               fill=0.0, base=-SEG, pattern=[[0, 1]], channel_multiplier=1).then_inc(consts, 1)

            def iota(dst, pattern, first, mul):
                pool.iota(dst, pattern=pattern, base=first, channel_multiplier=mul,
                          allow_small_or_imprecise_dtypes=True).then_inc(consts, 1)
            iota(iota_e[:], [[1, E]], 0, 0)
            iota(iota_cap[:], [[CAP, E]], 0, 0)
            iota(iota_thr[:], [[P, E]], 0, 0)
            iota(iota_blk[:], [[P, 2]], 0, 1)
            iota(tok6[:], [[TOPK * P, NT]], -1, TOPK)
            iota(magic[:], [[0, 1]], MAGIC, 0)

        N_CONST = 9

        def pool_route(pool, s):
            def body(g, q0):
                p = g * 2 + q0 // 2
                pool.wait_ge(s.slots, p + 1)
                pool.wait_ge(s.rx, p + 1)
                pool.sem_inc(s.take, 1)
                for q in (q0, q0 + 1):
                    for k in range(TOPK):
                        pool.indirect_dma_start(
                            out=rows_dram, out_offset=bass.IndirectOffsetOnAxis(ap=idx[:, q, k:k + 1], axis=0),
                            in_=rows[:, q, :], in_offset=None).then_inc(s.scat[q], 16)
            with pool.Fori(0, NT // 4) as g:
                body(g, 0)
                body(g, 2)

        def pool_experts(pool, s):
            with pool.Fori(0, NB // 4) as g:
                for q in range(4):
                    pool.wait_ge(s.y, g * 4 + (q + 1))
                    pool.sem_inc(s.take, 1)
                    pool.indirect_dma_start(
                        out=answers_dram, out_offset=bass.IndirectOffsetOnAxis(ap=didx[:, q:q + 1], axis=0),
                        in_=yb[:, q, :], in_offset=None, bounds_check=T * TOPK - 1,
                        oob_is_err=False).then_inc(s.scat[q], 16)

        def pool_combine(pool, s):
            def body(i, j):
                pool.wait_ge(s.red, i + 1)
                pool.tensor_tensor(xtile(i), xtile(i), red[j], ALU.add).then_inc(s.part, 1)
            by_pairs(pool, NT, body)

        QK, T2, VO, RT = 4, 5, 6, 7
        LG0, RK0 = 2 * P, 2 * P + 2 * E

        def mm(out_, lhs, rhs, start=True, stop=True):
            return nc.tensor.matmul(out_, lhs, rhs, start=start, stop=stop)

        def pe_route_t(pe, s, i, q):
            pe.wait_ge(s.xn, i + 1)
            positive(pe, s.xts, i)
            for c in range(KC):
                m = pe.transpose(ps[:, RT, c * P:(c + 1) * P], xn[:, q, c * P:(c + 1) * P], ident[:])
            m.then_inc(s.xt, 1)

        def pe_route_lg(pe, s, i, q):
            pe.wait_ge(s.xts, i + 1)
            j = q % 2
            for c in range(KC):
                m = mm(ps[:, RT, LG0 + j * E:LG0 + (j + 1) * E], xnt[:, j, c * P:(c + 1) * P], wgate[:, c, :],
                       start=(c == 0), stop=(c == KC - 1))
            if j == 1:
                m.then_inc(s.lg, 1)

        def pe_route_rk(pe, s, p, bank):
            pe.wait_ge(s.sel, p + 1)
            rk = lambda k: ps[:, bank, RK0 + k * E:RK0 + (k + 1) * E]
            mm(rk(0), before[:], sel[:, 0, :])
            mm(rk(1), before[:], sel[:, 1, :], stop=False)
            mm(rk(1), ones[:], sel[:, 0, :], start=False)
            mm(rk(2), ones[:], sel[:, 0, :], stop=False)
            mm(rk(2), ones[:], sel[:, 1, :], start=False).then_inc(s.rk, 1)

        def pe_route(pe, s):
            def transposed(p, k):
                if pair_exists(p):
                    for t in range(2):
                        if t == 0:
                            positive(pe, s.ex, p)
                        pe_route_t(pe, s, p * 2 + t, 2 * k + t)
                        pe_route_lg(pe, s, p * 2 + t, 2 * k + t)

            def body(p, k):
                transposed(p + 1, 1 - k)
                positive(pe, s.rkr, p)
                pe_route_rk(pe, s, p, VO)
            transposed(0, 0)
            pairs_by_two(pe, body, NT // 2)

        def pe_table(pe, s):
            pe.wait_ge(s.cnt, 1)
            for k in range(4):
                m = mm(ps[:, 0, k * P:(k + 1) * P], ones[:], diag[:, k, :])
            m.then_inc(s.bc, 1)

        TX, GU, HT, DN = 0, 2, 4, 6

        def pe_experts(pe, s):
            now = [pe.alloc_register(f"expert_now{j}_{s.n}") for j in range(2)]
            old = [pe.alloc_register(f"expert_old{j}_{s.n}") for j in range(2)]
            pe.wait_ge(s.tab, 1)
            pe.wait_ge(ld_exp, 48)
            pe.reg_load(now[0], itab[0:1, 0:1])
            pe.reg_mov(now[1], 0)
            pe.reg_mov(old[0], 0)
            pe.reg_mov(old[1], 0)

            def tx(n, q):
                pe.wait_ge(s.ld[q], 16 * (n // 4 + 1) if isinstance(n, int) else n * 4 + (16 - 4 * q))
                for c in range(KC):
                    m = pe.transpose(ps[:, TX + q % 2, c * P:(c + 1) * P], blk[:, q, c * P:(c + 1) * P], ident[:])
                m.then_inc(s.tx, 1)

            def step(n, q, first=False, m=None):
                j = q % 2
                if m is None or n < NB:
                    e = pe.snap(now[j], min_val=0, max_val=E - 1)
                    pe.wait_ge(s.xt, n + 1)
                    for c in range(KC):
                        g = mm(ps[:, GU + j, 0:2 * I], xbt[:, j, c * P:(c + 1) * P],
                               wgu[:, c, bass.ds(e * (2 * I), 2 * I)], start=(c == 0), stop=(c == KC - 1))
                    g.then_inc(s.gu, 1)
                if m is None or n + 1 < NB:
                    pe.reg_mov(old[1 - j], now[1 - j])
                    pe.reg_load(now[1 - j], itab[0:1, bass.ds(n + 1, 1)])
                elif n + 1 == NB:
                    pe.reg_mov(old[1 - j], now[1 - j])
                if m is None or n >= 2:
                    e2 = pe.snap(old[j], min_val=0, max_val=E - 1)
                    if m is not None and n >= NB:
                        e2 = pe.snap(old[j] if n == NB else old[j], min_val=0, max_val=E - 1)
                    pe.wait_ge(s.hts, n - 1)
                    positive(pe, s.y, n - 3)
                    mm(ps[:, DN + j, 0:D], hbt[:, j, :], wdn[:, bass.ds(e2 * D, D)]).then_inc(s.d, 1)
                if m is None or 1 <= n < NB + 1:
                    pe.wait_ge(s.h, n)
                    pe.transpose(ps[:, HT + 1 - j, 0:P], hb[:, 1 - j, :], ident[:]).then_inc(s.ht, 1)
                if m is None or n + 2 < NB:
                    tx(n + 2, (q + 2) % 4)

            tx(0, 0)
            tx(1, 1)
            return step

        def pe_experts_run(pe, s):
            step = pe_experts(pe, s)
            for n in range(4):
                step(n, n % 4, m=0)
            with pe.Fori(1, NB // 4 - 1) as g:
                for q in range(4):
                    step(g * 4 + q, q)
            for n in range(NB - 4, NB + 2):
                step(n, n % 4, m=0)

        def pe_combine(pe, s):
            def gate_up(i, q):
                pe.wait_ge(s.xs[q], 16 * (i // 4 + 1) if isinstance(i, int) else i * 4 + (16 - 4 * q))
                for k in range(4):
                    for c in range(KC):
                        m = mm(ps[:, q % 2, k * P:(k + 1) * P], wsgu[:, c, k * P:(k + 1) * P],
                               xs[:, q, c * P:(c + 1) * P], start=(c == 0), stop=(c == KC - 1))
                m.then_inc(s.gu, 1)

            def down(i, j):
                pe.wait_ge(s.h, i + 1)
                positive(pe, s.sum, i - 1)
                for c in range(SI // P):
                    m = mm(ps[:, 2 + j, 0:D], hsh[:, j, c * P:(c + 1) * P], wsd[:, c, :],
                           start=(c == 0), stop=(c == SI // P - 1))
                m.then_inc(s.d, 1)

            gate_up(0, 0)
            for i in range(3):
                gate_up(i + 1, i + 1)
                down(i, i % 2)
            with pe.Fori(1, NT // 4) as g:
                for q in range(4):
                    gate_up(g * 4 + q, q)
                    down(g * 4 + (q - 1), (q + 1) % 2)
            down(NT - 1, 1)

        def pe_means(pe):
            def body(i, j):
                pe.wait_ge(m_xn, i + 1)
                for c in range(KC):
                    m = mm(ps[:, 0, bass.ds(c * NSEG + 2 * i, 2)], rows[:, j, c * P:(c + 1) * P], seg_mean[:])
                m.then_inc(m_mm, 1)
            by_pairs(pe, NT, body)

        def pe_global(pe):
            pe.wait_ge(g_v, 1)
            xg = lambda c: xn2t[:, c * NSEG:(c + 1) * NSEG]
            for m_ in range(4):
                for c in range(KC):
                    m = mm(ps[:, 1, m_ * NSEG:(m_ + 1) * NSEG], wig[:, c, m_ * P:(m_ + 1) * P], xg(c),
                           start=(c == 0), stop=(c == KC - 1))
            m.then_inc(g_p, 1)
            for c in range(KC):
                m = mm(ps[0:NSEG, 2, 0:D], xg(c), wig[:, c, 2 * D:3 * D], start=(c == 0), stop=(c == KC - 1))
            m.then_inc(g_p, 1)
            pe.wait_ge(g_v, 2)
            for h in range(HG):
                r, c = HDG * (h % 2), h // 2
                m = mm(ps[0:NSEG, 3 + h % 2, c * NSEG:(c + 1) * NSEG], qkt[r:r + HDG, c, 0:NSEG],
                       qkt[r:r + HDG, 2 + c, 0:NSEG])
            m.then_inc(g_p, 1)
            pe.wait_ge(g_a, 2)
            for h in range(HG):
                m = pe.transpose(ps[0:NSEG, 5, h * NSEG:(h + 1) * NSEG], ssub[0:NSEG, h, :],
                                 ident[0:NSEG, 0:NSEG])
            m.then_inc(g_p, 1)
            pe.wait_ge(g_v, 4)
            for h in range(HG):
                m = mm(ps[0:NSEG, 6, h * HDG:(h + 1) * HDG], pt[0:NSEG, h, 0:NSEG],
                       osb[0:NSEG, h * HDG:(h + 1) * HDG])
            m.then_inc(g_p, 1)
            pe.wait_ge(g_v, 5)
            for c in range(KC):
                m = pe.transpose(ps[:, 7, c * NSEG:(c + 1) * NSEG], red[0][0:NSEG, c * P:(c + 1) * P],
                                 ident[0:NSEG, 0:NSEG])
            m.then_inc(g_p, 1)
            pe.wait_ge(g_v, 6)
            for c in range(KC):
                mm(ps[0:NSEG, 0, 0:D], ot[:, c * NSEG:(c + 1) * NSEG], wog[:, c, :], start=(c == 0), stop=False)
                mm(ps[0:NSEG, 0, 0:D], bvb[:, c, :], wol[:, c, :], start=False, stop=False)
                m = mm(ps[0:NSEG, 0, 0:D], bvb[:, KC + c, :], wog[:, c, :], start=False, stop=(c == KC - 1))
            m.then_inc(g_p, 1)

        def pe_qk(pe, i):
            pe.wait_ge(a_xts, i + 1)
            positive(pe, a_ots, i - 1)
            for q in range(4):
                for c in range(KC):
                    m = mm(ps[:, QK, q * P:(q + 1) * P], wil[:, c, q * P:(q + 1) * P],
                           xn2t[:, c * P:(c + 1) * P], start=(c == 0), stop=(c == KC - 1))
            m.then_inc(a_qk, 1)

        def pe_v(pe, i):
            positive(pe, a_x2, i - 1)
            for c in range(KC):
                m = mm(ps[:, VO, 0:D], xn2t[:, c * P:(c + 1) * P], wil[:, c, 2 * D:3 * D],
                       start=(c == 0), stop=(c == KC - 1))
            m.then_inc(a_v, 1)

        def pe_t2(pe, i):
            pe.wait_ge(a_xn, i + 1)
            positive(pe, a_xts, i)
            for c in range(KC):
                m = pe.transpose(ps[:, T2, c * P:(c + 1) * P], xn2[:, c * P:(c + 1) * P], ident[:])
            m.then_inc(a_xt, 1)

        def pe_out(pe, i):
            pe.wait_ge(a_ots, i + 1)
            pe.wait_ge(a_vs, i + 1)
            for c in range(KC):
                mm(ps[:, VO, D:2 * D], ot[:, c * P:(c + 1) * P], wol[:, c, :], start=(c == 0), stop=False)
            pe.wait_ge(a_sel, i + 1)
            mm(ps[:, VO, D:2 * D], selt[:], glob[:], start=False, stop=True).then_inc(a_out, 1)

        def pe_attend(pe, i, between):
            def turn(place):
                if place in between:
                    between[place]()
            pe.wait_ge(a_qks, i + 1)
            positive(pe, a_pts, i)
            for c in range(2):
                for g in range(2):
                    for r in range(4):
                        a, b = HDL * r, SEG * g
                        m = mm(ps[b:b + SEG, r, c * SEG:(c + 1) * SEG], qkt[a:a + HDL, c, b:b + SEG],
                               qkt[a:a + HDL, 2 + c, b:b + SEG])
            m.then_inc(a_s, 1)
            if exists(i - 1):
                pe_out(pe, i - 1)
            turn("after out")
            if exists(i + 1):
                pe_qk(pe, i + 1)
            pe.wait_ge(a_pr, i + 1)
            for h in range(HL):
                m = pe.transpose(ps[:, h % 4, P + (h // 4) * P:2 * P + (h // 4) * P], prob[:, h, :], ident[:])
            m.then_inc(a_pt, 1)
            if exists(i + 2):
                pe_t2(pe, i + 2)
            turn("before mix")
            pe.wait_ge(a_pts, i + 1)
            pe.wait_ge(a_vs, i + 1)
            if exists(i + 1):
                pe.wait_ge(a_qks, i + 2)
            for h in range(HL):
                m = mm(ps[:, QK, h * (HDL + 1):(h + 1) * (HDL + 1)], pt[:, h, :], vau[:, h, :])
            m.then_inc(a_o, 1)
            turn("after mix")
            if exists(i + 1):
                pe_v(pe, i + 1)
            turn("before heads")
            pe.wait_ge(a_os, i + 1)
            for c in range(KC):
                m = pe.transpose(ps[:, QK, c * P:(c + 1) * P], osb[:, c * P:(c + 1) * P], ident[:])
            m.then_inc(a_ot, 1)
            turn("last")

        def pe_pass_b(pe, s):
            def body(p, k):
                odd = {}
                if pair_exists(p - 2):
                    odd["after out"] = lambda: pe_route_rk(pe, s, p - 2, RT)
                if pair_exists(p - 1):
                    def first():
                        if pair_exists(p - 2):
                            pe.wait_ge(s.rkr, p - 1)
                        pe_route_t(pe, s, p * 2 - 2, 2 * (1 - k))
                    odd["before mix"] = first
                    odd["after mix"] = lambda: pe_route_lg(pe, s, p * 2 - 2, 2 * (1 - k))
                    odd["before heads"] = lambda: pe_route_t(pe, s, p * 2 - 1, 2 * (1 - k) + 1)
                    odd["last"] = lambda: pe_route_lg(pe, s, p * 2 - 1, 2 * (1 - k) + 1)
                if pair_exists(p):
                    pe_attend(pe, p * 2, {})
                    pe_attend(pe, p * 2 + 1, odd)
                else:
                    if p == NT // 2:
                        pe_out(pe, NT - 1)
                    for place in ("after out", "before mix", "after mix", "before heads", "last"):
                        if place in odd:
                            odd[place]()

            pe_t2(pe, 0)
            pe_qk(pe, 0)
            pe_v(pe, 0)
            pe_t2(pe, 1)
            pairs_by_two(pe, body, NT // 2 + 2)

        def act_route_xt(act, s, i, q):
            j = q % 2
            act.wait_ge(s.xt, i + 1)
            positive(act, s.store[j], visits(i, j, 2, 16))
            act.copy(xnt[:, j, :], ps[:, RT, 0:D]).then_inc(s.xts, 1)

        def act_route_ex(act, s, p):
            act.wait_ge(s.lg, p + 1)
            positive(act, s.sel, p)
            act.activation(ex[:], ps[:, RT, LG0:LG0 + 2 * E].rearrange("p (t e) -> p t e", t=2),
                           ACT.Exp, scale=-1.0).then_inc(s.ex, 1)

        def act_route_rows(act, s, p, k):
            for q in (2 * k, 2 * k + 1):
                positive(act, s.scat[q], visits(p, k, 2, 16 * TOPK))
            act.wait_ge(s.xn, p * 2 + 2)
            act.copy(rows[:, 2 * k:2 * k + 2, 0:D], xn[:, 2 * k:2 * k + 2, :]).then_inc(s.rx, 1)

        def act_route(act, s):
            def transposed(p, k):
                if pair_exists(p):
                    for t in range(2):
                        act_route_xt(act, s, p * 2 + t, 2 * k + t)
                    act_route_ex(act, s, p)

            def body(p, k):
                transposed(p + 1, 1 - k)
                act_route_rows(act, s, p, k)
            transposed(0, 0)
            pairs_by_two(act, body, NT // 2)

        def act_experts(act, s):
            def xt_copy(n, j):
                act.wait_ge(s.tx, n + 1)
                positive(act, s.gu, n - 1)
                act.copy(xbt[:, j, :], ps[:, TX + j, 0:D]).then_inc(s.xt, 1)

            def step(n, j, m=None):
                if m is None or n < NB:
                    act.wait_ge(s.gu, n + 1)
                    positive(act, s.h, n - 1)
                    act.activation(sg[:, j, :], ps[:, GU + j, 0:I], ACT.Silu).then_inc(s.sg, 1)
                if m is None or n >= 1:
                    act.wait_ge(s.ht, n)
                    positive(act, s.d, n - 2)
                    act.copy(hbt[:, 1 - j, :], ps[:, HT + 1 - j, 0:P]).then_inc(s.hts, 1)
                if m is None or n + 2 < NB:
                    xt_copy(n + 2, j)

            xt_copy(0, 0)
            xt_copy(1, 1)
            step(0, 0, m=0)
            step(1, 1, m=0)
            step(2, 0, m=0)
            step(3, 1, m=0)
            with act.Fori(2, NB // 2 - 1) as pair:
                step(pair * 2, 0)
                step(pair * 2 + 1, 1)
            for n in range(NB - 2, NB + 1):
                step(n, n % 2, m=0)

        def act_combine(act, s):
            def body(i, j):
                act.wait_ge(s.gu, i + 1)
                positive(act, s.h, i - 1)
                act.activation(ssg[:, j, :], ps[:, j, 0:SI], ACT.Silu).then_inc(s.sg, 1)
            by_pairs(act, NT, body)

        def act_global(act):
            act.wait_ge(g_p, 2)
            act.copy(osb[0:NSEG, :], ps[0:NSEG, 2, 0:D]).then_inc(g_a, 1)
            act.wait_ge(g_v, 3)
            act.activation(ssub[0:NSEG, 0:HG, :], ssub[0:NSEG, HG:2 * HG, :], ACT.Exp,
                           scale=float(HDG) ** -0.5).then_inc(g_a, 1)

        def act_v(act, i):
            act.wait_ge(a_v, i + 1)
            positive(act, a_o, i)
            act.copy(vau[:, :, 0:HDL], ps[:, VO, 0:D].rearrange("p (h d) -> p h d", h=HL)).then_inc(a_vs, 1)

        def act_xt(act, i):
            act.wait_ge(a_xt, i + 1)
            positive(act, a_v, i)
            act.copy(xn2t, ps[:, T2, 0:D]).then_inc(a_xts, 1)

        def act_attend(act, i, between):
            def turn(place):
                if place in between:
                    between[place]()
            act.wait_ge(a_sub, i + 1)
            positive(act, a_pt, i)
            for g in range(2):
                a = act.activation(prob[g * SEG:(g + 1) * SEG, :, g * SEG:(g + 1) * SEG],
                                   ssub[g * SEG:(g + 1) * SEG, :, :], ACT.Exp, scale=float(HDL) ** -0.5)
            a.then_inc(a_pr, 1)
            turn("after exp")
            act.wait_ge(a_pt, i + 1)
            positive(act, a_o, i)
            act.copy(pt.rearrange("p (c r) q -> p r c q", c=2),
                     ps[:, 0:4, P:3 * P].rearrange("p r (c q) -> p r c q", c=2)).then_inc(a_pts, 1)
            turn("before v")
            if exists(i + 1):
                act_v(act, i + 1)
            if exists(i + 2):
                act_xt(act, i + 2)
            turn("before heads")
            act.wait_ge(a_ot, i + 1)
            positive(act, a_out, i)
            act.copy(ot, ps[:, QK, 0:D]).then_inc(a_ots, 1)
            act.copy(selt[:].rearrange("s (g t) -> s g t", g=2),
                     ident[0:NSEG, bass.ds(i * 2, 2)].unsqueeze(2).to_broadcast([NSEG, 2, SEG])
                     ).then_inc(a_sel, 1)
            turn("last")

        def act_pass_b(act, s):
            def body(p, k):
                odd = {}
                if pair_exists(p - 2):
                    odd["after exp"] = lambda: act_route_rows(act, s, p - 2, k)
                if pair_exists(p - 1):
                    odd["before v"] = lambda: act_route_xt(act, s, p * 2 - 2, 2 * (1 - k))
                    odd["before heads"] = lambda: act_route_xt(act, s, p * 2 - 1, 2 * (1 - k) + 1)
                    odd["last"] = lambda: act_route_ex(act, s, p - 1)
                if pair_exists(p):
                    act_attend(act, p * 2, {})
                    act_attend(act, p * 2 + 1, odd)
                else:
                    for place in ("after exp", "before v", "before heads", "last"):
                        if place in odd:
                            odd[place]()

            act_xt(act, 0)
            act_v(act, 0)
            act_xt(act, 1)
            pairs_by_two(act, body, NT // 2 + 2)

        def inverse_root(st, var, y, a, b):
            v = nc.vector
            st.then(v.tensor_scalar(a, var, EPS, None, ALU.add))
            st.then(v.tensor_scalar(b.bitcast(I32), a.bitcast(I32), 1, None, ALU.arith_shift_right))
            st.then(v.tensor_scalar(y.bitcast(I32), b.bitcast(I32), -1.0, float(MAGIC), ALU.mult, ALU.add))
            for _ in range(3):
                st.then(v.tensor_tensor(b, y, y, ALU.mult))
                st.then(v.scalar_tensor_tensor(out=b, in0=b, scalar=-0.5, in1=a, op0=ALU.mult, op1=ALU.mult))
                st.then(v.scalar_tensor_tensor(out=y, in0=b, scalar=1.5, in1=y, op0=ALU.add, op1=ALU.mult))

        def tile_stats(v, st, i):
            st.then_alone(v.bn_stats(stats[:], xres[:, bass.ds(i, 1), :].rearrange("p a d -> p (a d)")), vpassed)
            st.then(v.bn_aggr(mv1[:], stats[:]))

        def xtile(i):
            return xres[:, bass.ds(i, 1), :].rearrange("p a d -> p (a d)")

        def mean_of(i):
            return mv[:, bass.ds(i, 1), 0:1].rearrange("p a b -> p (a b)")

        def v_route_norm(v, s, p, q, mean, inv):
            i = p * 2 + q % 2
            positive(v, s.xt, p * 2 - 2)
            positive(v, s.rx, p - 1)
            v.tensor_scalar(xn[:, q, :], xtile(i), mean, inv, ALU.subtract, ALU.mult).then_inc(s.xn, 1)

        def v_route_pick(v, st, s, p):
            def both(f):
                st.sync()
                v.sem_inc(vpassed, 1)
                for t in range(2):
                    st.did(f(t))
            v.wait_ge(s.ex, p + 1)
            st.then(v.tensor_scalar(ex[:], ex[:], 1.0, None, ALU.add))
            st.then(v.reciprocal(sc[:], ex[:]))
            st.then(v.tensor_tensor(sfc[:], sc[:], gbias[:].unsqueeze(1).to_broadcast([P, 2, E]), ALU.add))
            st.did(v.tensor_reduce(gmax[:], sfc[:].rearrange("p t (g e) -> p t g e", g=NG), X_AXIS, ALU.max))
            both(lambda t: v.max(out=gtop[:, t, :], in_=gmax[:, t, :]))
            both(lambda t: v.max_index(out=gi8[:, t, :], in_max=gtop[:, t, :], in_values=gmax[:, t, :]))
            st.sync()
            st.then(v.tensor_tensor(
                og[:], gi8[:, :, 0:TOPG].unsqueeze(3).to_broadcast([P, 2, TOPG, NG]),
                iota_e[:, 0:NG].unsqueeze(1).unsqueeze(1).to_broadcast([P, 2, TOPG, NG]), ALU.is_equal))
            st.then(v.tensor_reduce(gkeep[:], og[:].rearrange("p t k g -> p t g k"), X_AXIS, ALU.add))
            st.did(v.tensor_tensor(msk[:].rearrange("p t (g e) -> p t g e", g=NG),
                                   sfc[:].rearrange("p t (g e) -> p t g e", g=NG),
                                   gkeep[:].unsqueeze(3).to_broadcast([P, 2, NG, GS]), ALU.mult))
            both(lambda t: v.max(out=t8[:, t, :], in_=msk[:, t, :]))
            both(lambda t: v.max_index(out=ti8[:, t, :], in_max=t8[:, t, :], in_values=msk[:, t, :]))
            st.sync()
            st.then(v.tensor_tensor(
                oh[:], ti8[:, :, 0:TOPK].unsqueeze(3).to_broadcast([P, 2, TOPK, E]),
                iota_e[:].unsqueeze(1).unsqueeze(1).to_broadcast([P, 2, TOPK, E]), ALU.is_equal))
            v.tensor_reduce(sel[:], oh[:].rearrange("p t k e -> p t e k"), X_AXIS, ALU.add).then_inc(s.sel, 1)

        def v_route_ranks(v, st, s, p, bank):
            v.wait_ge(s.rk, p + 1)
            st.then(v.tensor_tensor(slot[:], ps[:, bank, RK0:RK0 + 2 * E].rearrange("p (t e) -> p t e", t=2),
                                    base[:].unsqueeze(1).to_broadcast([P, 2, E]), ALU.add))
            v.tensor_tensor(base[:], ps[:, bank, RK0 + 2 * E:RK0 + 3 * E], base[:], ALU.add).then_inc(s.rkr, 1)

        def v_route_weights(v, st, s, p, k):
            two = slice(2 * k, 2 * k + 2)
            v.wait_ge(s.sel, p + 1)
            st.did(v.tensor_tensor(cw[:], sc[:], sel[:], ALU.mult))
            for t in range(2):
                st.did(v.tensor_tensor_scan(nth[:, t, :], ones[:, 0:E], sel[:, t, :], 0.0, ALU.mult, ALU.add))
            st.sync()
            for q in (2 * k, 2 * k + 1):
                positive(v, s.scat[q], visits(p, k, 2, 16 * TOPK))
            st.did(v.tensor_reduce(csum[:, 0, :], cw[:], X_AXIS, ALU.add))
            for t in range(2):
                st.did(v.tensor_scalar(rows[:, 2 * k + t, COL_DEST:ROW], nth[:, t, :],
                                       tok6[:, bass.ds(p * 2 + t, 1)], None, ALU.add))
            st.sync()
            st.then(v.tensor_scalar(csum[:, 1, :], csum[:, 0, :], 1e-20, None, ALU.add))
            st.then(v.reciprocal(csum[:, 2, :], csum[:, 1, :]))
            st.did(v.scalar_tensor_tensor(out=rows[:, two, COL_W:COL_W + E], in0=cw[:], scalar=SCALE * HALF,
                                          in1=csum[:, 2, :].unsqueeze(2).to_broadcast([P, 2, E]),
                                          op0=ALU.mult, op1=ALU.mult))

        def v_route_slots(v, st, s, p, k):
            v.wait_ge(s.rkr, p + 1)
            st.then(v.tensor_tensor(ohs[:], oh[:], slot[:].unsqueeze(2).to_broadcast([P, 2, TOPK, E]), ALU.mult))
            with nc.allow_low_precision(reason="one whole number and zeros"):
                v.tensor_reduce(idx[:, 2 * k:2 * k + 2, 0:TOPK], ohs[:], X_AXIS, ALU.add).then_inc(s.slots, 1)

        def v_pairs(v, st, body, last, steps):
            body(0, 0)
            body(1, 1)
            start = st.base + st.n
            with v.Fori(1, NT // 4 - 1) as g:
                st.rebase(g * (2 * steps) + (start - 2 * steps))
                for k in range(2):
                    body(g * 2 + k, k)
                    assert st.n == (k + 1) * steps, (st.n, steps)
            st.rebase(start + (NT // 2 - 4) * steps)
            for p in range(NT // 2 - 2, last):
                body(p, p % 2)

        def v_loop(v, st, body, first=None, per=None):
            start = st.base + st.n
            st.rebase(start)
            body(0, 0)
            one = st.n
            body(1, 1)
            assert st.n == 2 * one, (st.n, one)
            with v.Fori(1, NT // 2) as pair:
                st.rebase(pair * (2 * one) + start)
                body(pair * 2, 0)
                body(pair * 2 + 1, 1)
            st.rebase(start + NT * one)

        ROUTE_STEPS = 27

        def v_route(v, st, s):
            st.then(v.tensor_copy(base[:], iota_cap[:]))

            def norm(p, k):
                if pair_exists(p):
                    for t in range(2):
                        i = p * 2 + t
                        v_route_norm(v, s, p, 2 * k + t, mean_of(i), rstd[:, bass.ds(i, 1)])

            def body(p, k):
                norm(p + 1, 1 - k)
                v_route_pick(v, st, s, p)
                v_route_weights(v, st, s, p, k)
                v_route_ranks(v, st, s, p, VO)
                v_route_slots(v, st, s, p, k)
            norm(0, 0)
            v_pairs(v, st, body, NT // 2, ROUTE_STEPS)

        def v_table(v, st, r, s):
            v.wait_ge(r.slots, NT // 2)
            v.tensor_copy(ptab[:], base[0:1, :]).then_inc(s.ptab, 1)
            cnt, nb, cum = tbl[:, 0, :], tbl[:, 1, :], tbl[:, 2, :]
            st.then(v.tensor_tensor(cnt, base[:], iota_cap[:], ALU.subtract))
            st.then(v.tensor_tensor(cmp_[:], cnt.unsqueeze(2).to_broadcast([P, E, E]),
                                    iota_thr[:].unsqueeze(1).to_broadcast([P, E, E]), ALU.is_gt))
            st.then(v.tensor_reduce(nb, cmp_[:], X_AXIS, ALU.add))
            st.then(v.tensor_tensor_scan(cum, ones[:, 0:E], nb, 0.0, ALU.mult, ALU.add))
            for h in range(2):
                ge, start = tbl[:, 3, :], tbl[:, 4, :]
                ecol, scol, fcol = (tcol[:, 3 * h + k:3 * h + k + 1] for k in range(3))
                st.then(v.tensor_scalar(ge, cum, iota_blk[:, h:h + 1], None, ALU.is_le))
                st.did(v.tensor_reduce(ecol, ge, X_AXIS, ALU.add))
                st.then(v.tensor_tensor(start, ge, cum, ALU.mult))
                st.then(v.tensor_reduce(scol, start, X_AXIS, ALU.max))
                st.then(v.tensor_tensor(fcol, iota_blk[:, h:h + 1], scol, ALU.subtract))
                st.then(v.tensor_scalar(fcol, fcol, float(P), None, ALU.mult))
                st.then(v.tensor_scalar(tcol[:, 6 + h:7 + h], ecol, float(CAP), None, ALU.mult))
                st.then(v.tensor_tensor(fcol, fcol, tcol[:, 6 + h:7 + h], ALU.add))
                st.then(v.tensor_scalar(fcol, fcol, float(DUMMY), None, ALU.min))
                st.then(v.tensor_scalar(ecol, ecol, float(E - 1), None, ALU.min))
                st.did(v.tensor_scalar(diag[:, h, :], ident[:], ecol, None, ALU.mult))
                st.then(v.tensor_scalar(diag[:, 2 + h, :], ident[:], fcol, None, ALU.mult))
            v.sem_inc(s.cnt, 1)
            v.wait_ge(s.bc, 1)
            st.did(v.tensor_copy(etab[:], ps[:, 0, 0:2 * P]))
            st.then(v.tensor_copy(itab[:], ps[0:1, 0, :]))
            v.sem_inc(s.tab, 1)

        def v_experts(v, st, s):
            start = st.base + st.n
            st.rebase(start)

            def pick(n, q):
                v.wait_ge(s.ld[q], 16 * (n // 4 + 1) if isinstance(n, int) else n * 4 + (16 - 4 * q))
                positive(v, s.pick, n * 2)
                positive(v, s.h, n - 3)
                for k, (col, out_) in enumerate(((COL_W, wcol), (COL_DEST, dcol))):
                    v.scalar_tensor_tensor(
                        out=picked[:, k, :], in0=iota_e[:], scalar=etab[:, bass.ds(n, 1)],
                        in1=blk[:, q, col:col + E], op0=ALU.is_equal, op1=ALU.mult,
                        accum_out=out_[:, q:q + 1]).then_inc(s.pick, 1)

            def step(n, q, m=None):
                j = q % 2
                if m is None or n < NB:
                    v.wait_ge(s.sg, n + 1)
                    positive(v, s.ht, n - 1)
                    v.wait_ge(s.pick, n * 2 + 2)
                    v.scalar_tensor_tensor(out=hb[:, j, :], in0=ps[:, GU + j, I:2 * I],
                                           scalar=wcol[:, q:q + 1], in1=sg[:, j, :],
                                           op0=ALU.mult, op1=ALU.mult).then_inc(s.h, 1)
                if m is None or n >= 2:
                    k = (q + 2) % 4
                    positive(v, s.scat[k],
                             16 * ((n - 2) // 4) if isinstance(n, int) else n * 4 - (8 + 4 * k))
                    st.did(v.tensor_copy(didx[:, k:k + 1], dcol[:, k:k + 1]))
                    v.wait_ge(s.d, n - 1)
                    v.tensor_copy(yb[:, k, :], ps[:, DN + j, 0:D]).then_inc(s.y, 1)
                    st.sync()
                if m is None or n + 2 < NB:
                    pick(n + 2, (q + 2) % 4)

            pick(0, 0)
            pick(1, 1)
            for n in range(4):
                step(n, n % 4, m=0)
            one = 1
            with v.Fori(1, NB // 4 - 1) as g:
                for q in range(4):
                    st.rebase(g * (4 * one) + (start + q - 2))
                    step(g * 4 + q, q)
            st.rebase(start + NB - 4 - 2)
            for n in range(NB - 4, NB + 2):
                step(n, n % 4, m=0)

        def v_combine(v, st, s, last):
            def hidden(i, j):
                v.wait_ge(s.sg, i + 1)
                positive(v, s.d, i - 1)
                v.tensor_tensor(hsh[:, j, :], ssg[:, j, :], ps[:, j, SI:2 * SI], ALU.mult).then_inc(s.h, 1)

            def stats_of(i):
                v.wait_ge(s.sum, i + 1)
                v.sem_inc(vpassed, 1)
                st.did(v.bn_stats(stats[:], xtile(i)))

            def finish_stats(i):
                st.then(v.bn_aggr(mv1[:], stats[:]))
                st.did(v.tensor_copy(mv[:, bass.ds(i, 1), :].rearrange("p a d -> p (a d)"), mv1[:]))

            def final(i, j):
                v.wait_ge(s.part, i + 1)
                v.wait_ge(s.d, i + 1)
                v.scalar_tensor_tensor(out=xtile(i), in0=ps[:, 2 + j, 0:D], scalar=HALF, in1=xtile(i),
                                       op0=ALU.mult, op1=ALU.add).then_inc(s.sum, 1)

            def body(i, j, m=None):
                if m is None or i + 1 < NT:
                    hidden(i + 1, 1 - j)
                stats_now = not last and (m is None or i >= 2)
                if stats_now:
                    stats_of(i - 2)
                v.wait_ge(s.ans[j], 16 * (i // 2 + 1) if isinstance(i, int) else i * 8 + (16 - 8 * j))
                positive(v, s.part, i - 1)
                v.tensor_reduce(red[j], ans[:, j, :].rearrange("p (k d) -> p d k", k=TOPK),
                                X_AXIS, ALU.add).then_inc(s.red, 1)
                if stats_now:
                    st.sync()
                    v.sem_inc(vpassed, 1)
                    finish_stats(i - 2)
                if m is None or i >= 1:
                    final(i - 1, 1 - j)

            hidden(0, 0)
            body(0, 0, m=0)
            body(1, 1, m=0)
            start = st.base + st.n
            n0 = st.n
            body(2, 0, m=0)
            one = st.n - n0
            body(3, 1, m=0)
            with v.Fori(2, NT // 2 - 1) as pair:
                st.rebase(pair * (2 * one) + (start - 2 * one))
                body(pair * 2, 0)
                body(pair * 2 + 1, 1)
            st.rebase(start + (NT - 4) * one)
            body(NT - 2, 0, m=0)
            body(NT - 1, 1, m=0)
            final(NT - 1, 1)
            if not last:
                for i in range(NT - 2, NT):
                    stats_of(i)
                    st.sync()
                    v.sem_inc(vpassed, 1)
                    finish_stats(i)

        def v_means(v, st):
            st.sync()
            inverse_root(st, mv[:, :, 1], rstd[:], newt[:, 0, :], newt[:, 1, :])

            def body(i, j):
                positive(v, m_mm, i - 1)
                v.tensor_scalar(rows[:, j, 0:D], xtile(i), mean_of(i), rstd[:, bass.ds(i, 1)],
                                ALU.subtract, ALU.mult).then_inc(m_xn, 1)
            v_loop(v, st, body)

        def v_global(v, st):
            v.wait_ge(m_mm, NT)
            for k, b in enumerate((bil, big)):
                for c in range(KC):
                    st.did(v.tensor_copy(bvb[:, k * KC + c, :],
                                         b[:, 2 * KC + c:2 * KC + c + 1].to_broadcast([P, NSEG])))
            st.then(v.tensor_copy(xn2t[:, 0:KC * NSEG], ps[:, 0, 0:KC * NSEG]))
            v.sem_inc(g_v, 1)
            v.wait_ge(g_p, 2)
            v.tensor_tensor(qkt[:, :, 0:NSEG], ps[:, 1, 0:4 * NSEG].rearrange("p (m t) -> p m t", m=4),
                            big[:, 0:4].unsqueeze(2).to_broadcast([P, 4, NSEG]), ALU.add).then_inc(g_v, 1)
            v.wait_ge(g_p, 3)
            sview = ps[0:NSEG, 3:5, 0:2 * NSEG].rearrange("p r (c k) -> p r c k", c=2)
            mview = smax[0:NSEG, 0:HG].rearrange("p (c r) -> p r c", c=2)
            st.then(v.tensor_reduce(mview, sview, X_AXIS, ALU.max))
            v.tensor_tensor(ssub[0:NSEG, HG:2 * HG, :].rearrange("p (c r) k -> p r c k", c=2), sview,
                            mview.unsqueeze(3).to_broadcast([NSEG, 2, 2, NSEG]), ALU.subtract).then_inc(g_v, 1)
            v.wait_ge(g_a, 2)
            st.then(v.tensor_reduce(smax[0:NSEG, 0:HG], ssub[0:NSEG, 0:HG, :], X_AXIS, ALU.add))
            st.then(v.reciprocal(rden[0:NSEG, 0:HG], smax[0:NSEG, 0:HG]))
            v.wait_ge(g_p, 4)
            v.tensor_copy(pt[0:NSEG, 0:HG, 0:NSEG],
                          ps[0:NSEG, 5, 0:HG * NSEG].rearrange("p (h q) -> p h q", h=HG)).then_inc(g_v, 1)
            v.wait_ge(g_p, 5)
            v.tensor_tensor(red[0][0:NSEG, :].rearrange("p (h d) -> p h d", h=HG),
                            ps[0:NSEG, 6, 0:D].rearrange("p (h d) -> p h d", h=HG),
                            rden[0:NSEG, 0:HG].unsqueeze(2).to_broadcast([NSEG, HG, HDG]),
                            ALU.mult).then_inc(g_v, 1)
            v.wait_ge(g_p, 6)
            v.tensor_copy(ot[:, 0:KC * NSEG], ps[:, 7, 0:KC * NSEG]).then_inc(g_v, 1)
            v.wait_ge(g_p, 7)
            st.then(v.tensor_tensor(glob[:], ps[0:NSEG, 0, 0:D], bout[0:NSEG, 0, :], ALU.add))
            v.tensor_tensor(glob[:], glob[:], bout[0:NSEG, 1, :], ALU.add).then_inc(g_v, 1)

        def v_xn2(v, i):
            positive(v, a_xt, i)
            v.tensor_scalar(xn2, xtile(i), mean_of(i), rstd[:, bass.ds(i, 1)],
                            ALU.subtract, ALU.mult).then_inc(a_xn, 1)

        def v_qk(v, i):
            v.wait_ge(a_qk, i + 1)
            positive(v, a_s, i)
            v.tensor_tensor(qkt, ps[:, QK, :].rearrange("p (m t) -> p m t", m=4),
                            bil[:, 0:4].unsqueeze(2).to_broadcast([P, 4, P]), ALU.add).then_inc(a_qks, 1)

        def v_out(v, i):
            v.wait_ge(a_out, i + 1)
            v.tensor_tensor(xtile(i), ps[:, VO, D:2 * D], xtile(i), ALU.add).then_inc(a_x2, 1)

        def v_attend(v, st, i, between):
            def turn(place):
                if place in between:
                    between[place]()
            v.wait_ge(a_s, i + 1)
            sview = ps[:, 0:4, 0:2 * SEG].rearrange("p r (c k) -> p r c k", c=2)
            mview = smax[:].rearrange("p (c r) -> p r c", c=2)
            st.then(v.tensor_reduce(mview, sview, X_AXIS, ALU.max))
            positive(v, a_pr, i)
            v.tensor_tensor(ssub.rearrange("p (c r) k -> p r c k", c=2), sview,
                            mview.unsqueeze(3).to_broadcast([P, 4, 2, SEG]), ALU.subtract).then_inc(a_sub, 1)
            if exists(i - 1):
                v_out(v, i - 1)
            turn("after out")
            if exists(i + 1):
                v_qk(v, i + 1)
            turn("before mix")
            v.wait_ge(a_o, i + 1)
            positive(v, a_ot, i)
            oview = ps[:, QK, 0:HL * (HDL + 1)].rearrange("p (h d) -> p h d", h=HL)
            st.then(v.reciprocal(rden[:].unsqueeze(2), oview[:, :, HDL:HDL + 1]))
            v.tensor_tensor(osb.rearrange("p (h d) -> p h d", h=HL), oview[:, :, 0:HDL],
                            rden[:].unsqueeze(2).to_broadcast([P, HL, HDL]), ALU.mult).then_inc(a_os, 1)
            if exists(i + 3):
                v_xn2(v, i + 3)
            turn("last")

        def v_pass_b(v, st, s):
            def norm(p, k):
                v.wait_ge(a_x2, p * 2 + 2)
                v.sem_inc(vpassed, 1)
                for t in range(2):
                    st.did(v.bn_stats(stats2[:, t, :], xtile(p * 2 + t)))
                st.sync()
                v.sem_inc(vpassed, 1)
                for t in range(2):
                    st.did(v.bn_aggr(mv2[:, t, :], stats2[:, t, :]))
                st.sync()
                inverse_root(st, mv2[:, :, 1], rstd2[:], newt[:, 0, 0:2], newt[:, 1, 0:2])
                for t in range(2):
                    v_route_norm(v, s, p, 2 * k + t, mv2[:, t, 0:1], rstd2[:, t:t + 1])

            def body(p, k):
                even, odd = {}, {}
                if pair_exists(p - 1):
                    even["before mix"] = lambda: norm(p - 1, 1 - k)
                if pair_exists(p - 2):
                    even["last"] = lambda: v_route_pick(v, st, s, p - 2)
                    odd["after out"] = lambda: v_route_ranks(v, st, s, p - 2, RT)

                    def finish():
                        v_route_weights(v, st, s, p - 2, k)
                        v_route_slots(v, st, s, p - 2, k)
                    odd["before mix"] = finish
                if pair_exists(p):
                    v_attend(v, st, p * 2, even)
                    v_attend(v, st, p * 2 + 1, odd)
                else:
                    if p == NT // 2:
                        v_out(v, NT - 1)
                    for turns, place in ((even, "before mix"), (even, "last"), (odd, "after out"),
                                         (odd, "before mix")):
                        if place in turns:
                            turns[place]()

            st.then(v.tensor_copy(base[:], iota_cap[:]))
            v_xn2(v, 0)
            v_qk(v, 0)
            v_xn2(v, 1)
            v_xn2(v, 2)
            v_pairs(v, st, body, NT // 2 + 2, ROUTE_STEPS + 20)

        def v_first(v, st):
            for h in range(2):
                v.wait_ge(ld_x[h], 16)
                for i in range(h * NT // 2, (h + 1) * NT // 2):
                    tile_stats(v, st, i)
                    st.then(v.tensor_copy(mv[:, i, :], mv1[:]))
            v.wait_ge(consts, N_CONST)
            v.wait_ge(ld_small, N_SMALL)
            inverse_root(st, mv[:, :, 1], rstd[:], newt[:, 0, :], newt[:, 1, :])

        out_tiles = out.rearrange("b (n p) d -> p (b n) d", p=P)

        @block.sync
        def _(sp):
            load_inputs(sp)
            sp_route(sp, R[0])
            pad_experts(sp, X[0], 0)
            sp_experts(sp, R[0], X[0])
            sp_combine(sp, X[0], C[0], R[0], False)
            sp_route(sp, R[1])
            pad_experts(sp, X[1], 0)
            sp_experts(sp, R[1], X[1])
            sp_combine(sp, X[1], C[1], R[1], True)

        @block.gpsimd
        def _(pool):
            make_consts(pool)
            pool_route(pool, R[0])
            pool_experts(pool, X[0])
            pool_combine(pool, C[0])
            pool_route(pool, R[1])
            pool_experts(pool, X[1])
            pool_combine(pool, C[1])

        @block.tensor
        def _(pe):
            pe.wait_ge(consts, N_CONST)
            pe.wait_ge(ld_small, N_SMALL)
            pe_route(pe, R[0])
            pe_table(pe, X[0])
            pe_experts_run(pe, X[0])
            pe_combine(pe, C[0])
            pe_means(pe)
            pe_global(pe)
            pe.wait_ge(g_v, 7)
            pe_pass_b(pe, R[1])
            pe_table(pe, X[1])
            pe_experts_run(pe, X[1])
            pe_combine(pe, C[1])

        @block.scalar
        def _(act):
            act.wait_ge(consts, N_CONST)
            act_route(act, R[0])
            pad_experts(act, X[0], 1)
            act_experts(act, X[0])
            act_combine(act, C[0])
            act_global(act)
            act.wait_ge(g_v, 7)
            act_pass_b(act, R[1])
            pad_experts(act, X[1], 1)
            act_experts(act, X[1])
            act_combine(act, C[1])
            for k in range(4):
                n = NT // 4
                act.wait_ge(C[1].sum, (k + 1) * n)
                act.dma_start(out_tiles[:, k * n:(k + 1) * n, :],
                              xres[:, k * n:(k + 1) * n, :]).then_inc(C[1].out, 16)
            act.wait_ge(C[1].out, 64)

        @block.vector
        def _(v):
            st = Steps(v, vstep)
            v_first(v, st)
            v_route(v, st, R[0])
            v_table(v, st, R[0], X[0])
            v_experts(v, st, X[0])
            v_combine(v, st, C[0], False)
            v_means(v, st)
            v_global(v, st)
            v_pass_b(v, st, R[1])
            v_table(v, st, R[1], X[1])
            v_experts(v, st, X[1])
            v_combine(v, st, C[1], True)


def kernel(L0_attn_x, L0_attn_w_in_local, L0_attn_b_in_local, L0_attn_w_out_local, L0_attn_b_out_local,
           L0_attn_w_in_global, L0_attn_b_in_global, L0_attn_w_out_global, L0_attn_b_out_global,
           L0_ffn_gate_weight, L0_ffn_e_score_correction_bias, L0_ffn_experts_gate_up, L0_ffn_experts_down,
           L0_ffn_shared_gate_w, L0_ffn_shared_up_w, L0_ffn_shared_down_w):
    from concourse import bacc
    from concourse.bass_utils import run_bass_kernel_spmd

    c = np.ascontiguousarray
    arrays = {
        "in_x": c(L0_attn_x),
        "in_gate": c(np.asarray(L0_ffn_gate_weight).T),
        "in_gate_bias": c(L0_ffn_e_score_correction_bias),
        "in_gate_up": c(np.asarray(L0_ffn_experts_gate_up).transpose(2, 0, 1)).reshape(KC, P, E * 2 * I),
        "in_down": c(np.asarray(L0_ffn_experts_down).transpose(2, 0, 1)).reshape(I, E * D),
        "in_shared_gate": c(np.asarray(L0_ffn_shared_gate_w).T),
        "in_shared_up": c(np.asarray(L0_ffn_shared_up_w).T),
        "in_shared_down": c(np.asarray(L0_ffn_shared_down_w).T),
        "in_wi_local": c(np.asarray(L0_attn_w_in_local).T),
        "in_bi_local": c(L0_attn_b_in_local),
        "in_wo_local": c(np.asarray(L0_attn_w_out_local).T),
        "in_bo_local": c(L0_attn_b_out_local),
        "in_wi_global": c(np.asarray(L0_attn_w_in_global).T),
        "in_bi_global": c(L0_attn_b_in_global),
        "in_wo_global": c(np.asarray(L0_attn_w_out_global).T),
        "in_bo_global": c(L0_attn_b_out_global),
    }
    nc = bacc.Bacc("TRN2", target_bir_lowering=False, num_devices=1)
    args = [nc.dram_tensor(n, a.shape, F32, kind="ExternalInput").ap() for n, a in arrays.items()]
    args.append(nc.dram_tensor("out", L0_attn_x.shape, F32, kind="ExternalOutput").ap())
    build(nc, *args)
    r = run_bass_kernel_spmd(nc, [arrays], core_ids=[0])
    return r.results[0]["out"]
```

```python
from contextlib import ExitStack

import numpy as np

import concourse.bass as bass
from concourse import mybir

F32 = mybir.dt.float32
I32 = mybir.dt.int32
U32 = mybir.dt.uint32
ALU = mybir.AluOpType
ACT = mybir.ActivationFunctionType
X_AXIS = mybir.AxisListType.X

P = 128
D = 256
KC = D // P
T = 4096
NT = T // P
E = 32
I = 128
SI = 256
TOPK = 6
NG = 8
GS = E // NG
TOPG = 4
SCALE = 2.5
HALF = 0.5
SEG = 64
NSEG = T // SEG
HL, HDL = 8, 32
HG, HDG = 4, 64
EPS = 1e-5

ROW = D + 2 * E
COL_W, COL_DEST = D, D + E
CAP = P + T
NOWHERE = 2 * T * TOPK
NB = 224
MAGIC = 0x5F3759DF


def positive(eng, sem, value):
    if isinstance(value, int) and value <= 0:
        return
    eng.wait_ge(sem, value)


def by_pairs(eng, n, body):
    body(0, 0)
    body(1, 1)
    with eng.Fori(1, n // 2) as pair:
        body(pair * 2, 0)
        body(pair * 2 + 1, 1)


def visits(i, r, n, per):
    return per * (i // n) if isinstance(i, int) else i * (per // n) - (per // n) * r


def exists(i):
    return not isinstance(i, int) or 0 <= i < NT


def pair_exists(p):
    return not isinstance(p, int) or 0 <= p < NT // 2


def pairs_by_two(eng, body, last):
    body(0, 0)
    body(1, 1)
    with eng.Fori(1, NT // 4 - 1) as g:
        body(g * 2, 0)
        body(g * 2 + 1, 1)
    for p in range(NT // 2 - 2, last):
        body(p, p % 2)


class Steps:

    def __init__(self, eng, sem):
        self.eng, self.sem, self.base, self.n = eng, sem, 0, 0

    def rebase(self, base):
        self.base, self.n = base, 0

    def did(self, ins):
        ins.then_inc(self.sem, 1)
        self.n += 1

    def sync(self):
        self.eng.wait_ge(self.sem, self.base + self.n)

    def then(self, ins):
        self.did(ins)
        self.sync()


def build(nc, x_in, gate_t, gate_bias, wgu_in, wdn_in, wsg_in, wsu_in, wsd_in,
          wi_l, bi_l, wo_l, bo_l, wi_g, bi_g, wo_g, bo_g, out):
    ctx = ExitStack()
    with ctx:
        def sb(name, shape, dt=F32):
            return ctx.enter_context(nc.sbuf_tensor(name, shape, dt))

        def sem(name):
            return ctx.enter_context(nc.semaphore(name))

        rows_dram = nc.dram_tensor("dispatch_rows", [E * CAP, ROW], F32).ap()
        answers_dram = nc.dram_tensor("answers", [T * TOPK, D], F32).ap()
        xnt_dram = nc.dram_tensor("normed_transposed", [NT, P, D], F32).ap()

        wgu = sb("wgu", [P, KC, E * 2 * I])
        wdn = sb("wdn", [P, E * D])
        wsgu = sb("wsgu", [P, KC, 2 * SI])
        wsd = sb("wsd", [P, SI // P, D])
        wgate = sb("wgate", [P, KC, E])
        wil = sb("wil", [P, KC, 3 * D])
        wol = sb("wol", [P, KC, D])
        wig = sb("wig", [P, KC, 3 * D])
        wog = sb("wog", [P, KC, D])
        bil = sb("bil", [P, 3 * KC])
        big = sb("big", [P, 3 * KC])
        bout = sb("bout", [P, 2, D])
        gbias = sb("gbias", [P, E])
        ident = sb("ident", [P, P])
        ones = sb("ones", [P, P])
        before = sb("before", [P, P])
        seg_mean = sb("seg_mean", [P, 4, 8])
        iota_e = sb("iota_e", [P, E])
        iota_cap = sb("iota_cap", [P, E])
        iota_thr = sb("iota_thr", [P, E])
        iota_blk = sb("iota_blk", [P, 2])
        tok6 = sb("tok6", [P, NT])
        magic = sb("magic", [P, 1])
        padt = sb("padt", [P, ROW])

        xres = sb("xres", [P, NT, D])
        mv = sb("mv", [P, NT, 2])
        rstd = sb("rstd", [P, NT])
        newt = sb("newt", [P, 3, NT])
        stats = sb("stats", [P, 6])
        mv4 = sb("mv4", [P, 4, 2])
        stats4 = sb("stats4", [P, 4, 6])
        rstd4 = sb("rstd4", [P, 4])

        xnt = sb("xnt", [P, 2, D])
        ex = sb("ex", [P, 2, E])
        sc = sb("sc", [P, 2, E])
        sfc = sb("sfc", [P, 2, E])
        gmax = sb("gmax", [P, 2, NG])
        gtop = sb("gtop", [P, 2, 8])
        gi8 = sb("gi8", [P, 2, 8], U32)
        og = sb("og", [P, 2, TOPG, NG])
        gkeep = sb("gkeep", [P, 2, NG])
        t8 = sb("t8", [P, 2, 8])
        ti8 = sb("ti8", [P, 2, 8], U32)
        oh = sb("oh", [P, 2, TOPK, E])
        ohs = sb("ohs", [P, 2, TOPK, E])
        msk = sb("msk", [P, 2, E])
        nth = sb("nth", [P, 2, E])
        sel = sb("sel", [P, 3, E])
        cw = sb("cw", [P, 2, E])
        csum = sb("csum", [P, 3, 2])
        slot = sb("slot", [P, 2, E])
        base = sb("base", [P, E])
        idx = sb("idx", [P, 4, 8], I32)

        tbl = sb("tbl", [P, 6, E])
        tcol = sb("tcol", [P, 12])
        etab = sb("etab", [P, 2 * P])
        itab = sb("itab", [1, 4 * P], I32)

        blk = sb("blk", [P, 4, ROW])
        rows = blk
        xbt = sb("xbt", [P, 2, D])
        sg = sb("sg", [P, 2, I])
        hb = sb("hb", [P, 2, I])
        hbt = sb("hbt", [P, 2, I])
        yb = sb("yb", [P, 4, D])
        picked = sb("picked", [P, 2, E])
        wcol = sb("wcol", [P, 4])
        dcol = sb("dcol", [P, 4])
        didx = sb("didx", [P, 4], I32)

        ans = sb("ans", [P, 2, TOPK * D])
        PARTS = ((0, 4), (4, TOPK))
        red = sb("red", [P, D])
        two_sums = [yb[:, 2 * j:2 * j + 2, :] for j in range(2)]
        third_sum = [red[:], sg[:].rearrange("p j i -> p (j i)")]
        xn = yb
        xs = blk
        ssg = sb("ssg", [P, 2, SI])
        hsh = sb("hsh", [P, 2, SI])
        diag = ssg[:].rearrange("p j (a b) -> p (j a) b", a=2)

        flat = ans[:].rearrange("p j n -> p (j n)")
        cmp_ = flat[:, 0:E * E].rearrange("p (e j) -> p e j", e=E)
        diag_twice = flat[:, E * E:E * E + 2 * P].rearrange("p (h b) -> p h b", h=2)
        skip = flat[:, E * E + 2 * P:E * E + 4 * P]
        at = [0]

        def share(*shape):
            n = int(np.prod(shape))
            v = flat[:, at[0]:at[0] + n]
            at[0] += n
            if len(shape) == 2:
                v = v.rearrange("p (a b) -> p a b", a=shape[0])
            return v

        xn2 = share(D)
        xn2t = share(D)
        qkt = share(4, P)
        ssub = share(HL, SEG)
        pt = share(HL, P)
        osb = share(D)
        ot = share(D)
        means = flat[:, TOPK * D * 2 - 2 * 4 * D:]
        vv = sb("vv", [P, 2, D])
        smax = sb("smax", [P, HL])
        nmax = sb("nmax", [P, HL])
        psum_ = sb("psum_", [P, HL])
        prob = sb("prob", [P, HL, P])
        rden = sb("rden", [P, HL])
        selt = sb("selt", [NSEG, P])
        glob = sb("glob", [NSEG, D])
        bvb = hsh[:].rearrange("p j s -> p (j s)")[:, 0:2 * KC * NSEG].rearrange("p (k s) -> p k s", k=2 * KC)

        ps = ctx.enter_context(nc.psum_tensor("ps", [P, 8, 512], F32))

        ld_x = [sem(f"ld_x{k}") for k in range(3)]
        ld_gate = sem("ld_gate")
        ld_small = sem("ld_small")
        ld_exp = sem("ld_exp")
        padded = sem("padded")
        consts = sem("consts")
        vstep = sem("vector_step")
        vpassed = sem("vector_passed")
        ppassed = sem("pool_passed")
        pstep = sem("pool_step")

        block = ctx.enter_context(nc.Block())

        class RouteSems:
            def __init__(self, n):
                s = lambda name: sem(f"{name}_{n}")
                self.xn = s("rt_xn")
                self.xt = s("rt_xt")
                self.xts = s("rt_xts")
                self.store = [s("rt_store0"), s("rt_store1")]
                self.lg = s("rt_lg")
                self.ex = s("rt_ex")
                self.sel = s("rt_sel")
                self.rk = s("rt_rk")
                self.rkr = s("rt_rkr")
                self.rx = s("rt_rx")
                self.slots = s("rt_slots")
                self.take = s("rt_take")
                self.scat = [s(f"rt_scat{q}") for q in range(4)]

        class ExpertSems:
            def __init__(self, n):
                self.n = n
                s = lambda name: sem(f"{name}_{n}")
                self.cnt = s("tb_diag")
                self.bc = s("tb_bc")
                self.tab = s("tb_tab")
                self.ld = [s(f"ex_ld{q}") for q in range(4)]
                self.tx = s("ex_tx")
                self.xt = s("ex_xt")
                self.pick = s("ex_pick")
                self.gu = s("ex_gu")
                self.sg = s("ex_sg")
                self.h = s("ex_h")
                self.ht = s("ex_ht")
                self.hts = s("ex_hts")
                self.d = s("ex_d")
                self.y = s("ex_y")
                self.take = s("ex_take")
                self.scat = [s(f"ex_scat{q}") for q in range(4)]

        class CombineSems:
            def __init__(self, n):
                s = lambda name: sem(f"{name}_{n}")
                self.ans = [[s(f"cb_ans{part}_{j}") for j in range(2)] for part in range(2)]
                self.xs = [s(f"cb_xs{q}") for q in range(4)]
                self.gu = s("cb_gu")
                self.sg = s("cb_sg")
                self.h = s("cb_h")
                self.d = s("cb_d")
                self.red = s("cb_red")
                self.part = s("cb_part")
                self.sum = s("cb_sum")
                self.out = s("cb_out")

        R = [RouteSems(n) for n in range(2)]
        X = [ExpertSems(n) for n in range(2)]
        C = [CombineSems(n) for n in range(2)]
        m_xn = sem("mean_xn")
        m_mm = sem("mean_mm")
        m_passed = sem("mean_passed")
        m_sb = sem("mean_sb")
        m_t = sem("mean_t")
        g_v = sem("glob_vector")
        g_p = sem("glob_tensor")
        g_a = sem("glob_scalar")
        a_xn = sem("at_xn")
        a_xt = sem("at_xt")
        a_xts = sem("at_xts")
        a_qk = sem("at_qk")
        a_qks = sem("at_qks")
        a_v = sem("at_v")
        a_vs = sem("at_vs")
        a_s = sem("at_s")
        a_max = sem("at_max")
        a_ex = sem("at_ex")
        a_pr = sem("at_prob")
        a_pt = sem("at_pt")
        a_pts = sem("at_pts")
        a_o = sem("at_o")
        a_ots = sem("at_ots")
        a_sel = sem("at_sel")
        a_out = sem("at_out")
        a_x2 = sem("at_x2")

        N_SMALL = 16 * 11
        X_PIECES = (0, 4, 8, NT)

        def load_inputs(sp):
            x_tiles = x_in.rearrange("b (n p) d -> p (b n) d", p=P)
            for k in range(3):
                sp.dma_start(xres[:, X_PIECES[k]:X_PIECES[k + 1], :],
                             x_tiles[:, X_PIECES[k]:X_PIECES[k + 1], :]).then_inc(ld_x[k], 16)
                if k == 0:
                    sp.dma_start(wgate[:], gate_t.rearrange("(c p) e -> p c e", p=P)).then_inc(ld_gate, 16)
                    sp.dma_start(gbias[:], gate_bias.rearrange("(a e) -> a e", a=1).to_broadcast([P, E])
                                 ).then_inc(ld_gate, 16)

        def load_dense(sp):
            sp.dma_start(wsgu[:, :, 0:SI], wsg_in.rearrange("(c p) s -> p c s", p=P)).then_inc(ld_small, 16)
            sp.dma_start(wsgu[:, :, SI:2 * SI], wsu_in.rearrange("(c p) s -> p c s", p=P)).then_inc(ld_small, 16)
            sp.dma_start(wsd[:], wsd_in.rearrange("(c p) d -> p c d", p=P)).then_inc(ld_small, 16)
            for dst, src in ((wil, wi_l), (wol, wo_l), (wig, wi_g), (wog, wo_g)):
                sp.dma_start(dst[:], src.rearrange("(c p) d -> p c d", p=P)).then_inc(ld_small, 16)
            with nc.allow_non_contiguous_dma(reason="biases to partitions, once"):
                sp.dma_start(bil[:], bi_l.rearrange("(c p) -> p c", p=P)).then_inc(ld_small, 16)
                sp.dma_start(big[:], bi_g.rearrange("(c p) -> p c", p=P)).then_inc(ld_small, 16)
            for k, b in enumerate((bo_l, bo_g)):
                sp.dma_start(bout[:, k, :], b.rearrange("(a d) -> a d", a=1).to_broadcast([P, D])
                             ).then_inc(ld_small, 16)

        def load_experts(sp, p):
            assert E == NT
            if isinstance(p, int):
                sp.wait_ge(consts, N_CONST)
            for k in range(2):
                sp.dma_start(rows_dram[bass.ds(p * (2 * CAP) + k * CAP, P), :], padt[:]).then_inc(padded, 16)
            sp.dma_start(wdn[:, bass.ds(p * (2 * D), 2 * D)], wdn_in[:, bass.ds(p * (2 * D), 2 * D)]
                         ).then_inc(ld_exp, 16)
            for c in range(KC):
                part = bass.ds(p * (4 * I), 4 * I)
                sp.dma_start(wgu[:, c, part], wgu_in[c][:, part]).then_inc(ld_exp, 16)

        def sp_route(sp, s, more=None):
            def store(i, j):
                sp.wait_ge(s.xts, i + 1)
                sp.dma_start(xnt_dram[bass.ds(i, 1)].rearrange("a p d -> (a p) d"),
                             xnt[:, j, :]).then_inc(s.store[j], 16)

            def pair(p):
                for j in range(2):
                    store(p * 2 + j, j)
                if more:
                    more(p)
            pair(0)
            with sp.Fori(1, NT // 2) as p:
                pair(p)

        def sp_experts(sp, r, s):
            sp.wait_ge(s.tab, 1)
            for q in range(4):
                sp.wait_ge(r.scat[q], 16 * TOPK * (NT // 4))
            sp.wait_ge(padded, 16 * E)
            sp.wait_ge(ld_small, N_SMALL)

            def body(g, peeled):
                for q in range(4):
                    n = g * 4 + q
                    first = sp.value_load(itab[0:1, bass.ds(n + 2 * P, 1)], min_val=0, max_val=E * CAP - P)
                    if not peeled:
                        sp.wait_ge(s.tx, n - 3)
                        sp.wait_ge(s.pick, n * 2 - 6)
                    sp.dma_start(blk[:, q, :], rows_dram[bass.ds(first, P), :]).then_inc(s.ld[q], 16)
            body(0, True)
            with sp.Fori(1, NB // 4) as g:
                body(g, False)

        def sp_combine(sp, x, s, r, last):
            for j in range(2):
                sp.wait_ge(r.store[j], 16 * (NT // 2))
            ans_v = answers_dram.rearrange("(n p k) d -> n p (k d)", p=P, k=TOPK)

            def load_tokens(i, q):
                sp.dma_start(xs[:, q, 0:D], xnt_dram[bass.ds(i, 1)].rearrange("a p d -> (a p) d")
                             ).then_inc(s.xs[q], 16)

            def load_answers(i, j):
                for k, (a, b) in enumerate(PARTS):
                    positive(sp, s.red, i * 2 - 3 + k)
                    part = slice(a * D, b * D)
                    sp.dma_start(ans[:, j, part], ans_v[bass.ds(i, 1)][:, :, part].rearrange("a p d -> (a p) d")
                                 ).then_inc(s.ans[k][j], 16)

            sp.wait_ge(x.tx, NB)
            sp.wait_ge(x.pick, 2 * NB)
            for q in range(4):
                load_tokens(q, q)
            for q in range(4):
                sp.wait_ge(x.scat[q], 16 * (NB // 4))
            for q in range(2):
                load_answers(q, q % 2)
            with sp.Fori(0, NT // 4 - 1) as g:
                for q in range(4):
                    i = g * 4 + (q + 4)
                    sp.wait_ge(s.gu, i - 3)
                    load_tokens(i, q)
                    load_answers(i - 2, q % 2)
            for q in range(2, 4):
                load_answers(NT - 4 + q, q % 2)

        def make_consts(pool):
            st = Steps(pool, pstep)
            st.did(pool.memset(ones[:], 1.0))
            st.did(pool.memset(sel[:, 2, :], 0.0))
            st.did(pool.memset(padt[:, 0:COL_DEST], 0.0))
            st.did(pool.memset(padt[:, COL_DEST:ROW], float(NOWHERE)))
            st.did(pool.memset(prob[:], 0.0))
            st.did(pool.memset(seg_mean[:], 0.0))
            st.sync()
            pool.affine_select(out=ident[:], in_=ones[:], compare_op=ALU.is_equal, fill=0.0, base=0,
                               pattern=[[-1, P]], channel_multiplier=1).then_inc(consts, 1)
            pool.affine_select(out=before[:], in_=ones[:], compare_op=ALU.is_gt, fill=0.0, base=0,
                               pattern=[[1, P]], channel_multiplier=-1).then_inc(consts, 1)
            for q in range(4):
                for g in range(2):
                    st.then(pool.memset(seg_mean[g * SEG:(g + 1) * SEG, q, 2 * q + g:2 * q + g + 1], 1.0 / SEG))
            pool.sem_inc(consts, 1)

            def iota(dst, pattern, first, mul):
                pool.iota(dst, pattern=pattern, base=first, channel_multiplier=mul,
                          allow_small_or_imprecise_dtypes=True).then_inc(consts, 1)
            iota(iota_e[:], [[1, E]], 0, 0)
            iota(iota_cap[:], [[CAP, E]], P, 0)
            iota(iota_thr[:], [[P, E]], 0, 0)
            iota(iota_blk[:], [[P, 2]], 0, 1)
            iota(tok6[:], [[TOPK * P, NT]], -1, TOPK)
            iota(magic[:], [[0, 1]], MAGIC, 0)

        N_CONST = 9

        def pool_route(pool, s):
            def body(g, q0):
                p = g * 2 + q0 // 2
                pool.wait_ge(s.slots, p + 1)
                pool.wait_ge(s.rx, p + 1)
                pool.sem_inc(s.take, 1)
                for q in (q0, q0 + 1):
                    for k in range(TOPK):
                        pool.indirect_dma_start(
                            out=rows_dram, out_offset=bass.IndirectOffsetOnAxis(ap=idx[:, q, k:k + 1], axis=0),
                            in_=rows[:, q, :], in_offset=None).then_inc(s.scat[q], 16)
            with pool.Fori(0, NT // 4) as g:
                body(g, 0)
                body(g, 2)

        def pool_experts(pool, s):
            with pool.Fori(0, NB // 4) as g:
                for q in range(4):
                    pool.wait_ge(s.y, g * 4 + (q + 1))
                    pool.sem_inc(s.take, 1)
                    pool.indirect_dma_start(
                        out=answers_dram, out_offset=bass.IndirectOffsetOnAxis(ap=didx[:, q:q + 1], axis=0),
                        in_=yb[:, q, :], in_offset=None, bounds_check=T * TOPK - 1,
                        oob_is_err=False).then_inc(s.scat[q], 16)

        def pool_combine(pool, s):
            def body(i, j):
                for k, sums in enumerate((two_sums[j][:, 0, :], two_sums[j][:, 1, :], third_sum[j])):
                    pool.wait_ge(s.red, i * 2 + (1 if k < 2 else 2))
                    if k:
                        pool.wait_ge(s.part, i * 3 + k)
                    pool.sem_inc(ppassed, 1)
                    pool.tensor_tensor(xtile(i), xtile(i), sums, ALU.add).then_inc(s.part, 1)
            by_pairs(pool, NT, body)

        QK, HD, VO, RT = 4, 5, 6, 7
        T2, OUT = 0, HD
        RK_ATTEND = 1
        AFTER_S = P
        LG0, RK0 = 2 * P, 2 * P + 2 * E

        def mm(out_, lhs, rhs, start=True, stop=True):
            return nc.tensor.matmul(out_, lhs, rhs, start=start, stop=stop)

        def pe_route_t(pe, s, i, q):
            pe.wait_ge(s.xn, i + 1)
            positive(pe, s.xts, i)
            for c in range(KC):
                m = pe.transpose(ps[:, RT, c * P:(c + 1) * P], xn[:, q, c * P:(c + 1) * P], ident[:])
            m.then_inc(s.xt, 1)

        def pe_route_lg(pe, s, i, q):
            pe.wait_ge(s.xts, i + 1)
            j = q % 2
            for c in range(KC):
                m = mm(ps[:, RT, LG0 + j * E:LG0 + (j + 1) * E], xnt[:, j, c * P:(c + 1) * P], wgate[:, c, :],
                       start=(c == 0), stop=(c == KC - 1))
            if j == 1:
                m.then_inc(s.lg, 1)

        def pe_route_rk(pe, s, p, bank):
            pe.wait_ge(s.sel, p + 1)
            rk = lambda k, n: ps[:, bank, RK0 + k * E:RK0 + (k + n) * E]
            mm(rk(0, 3), before[:], sel[:], stop=False)
            mm(rk(1, 2), ones[:], sel[:, 0:1, :].to_broadcast([P, 2, E]), start=False, stop=False)
            mm(rk(2, 1), ones[:], sel[:, 1, :], start=False).then_inc(s.rk, 1)

        def pe_route(pe, s):
            def transposed(p, k):
                if pair_exists(p):
                    for t in range(2):
                        if t == 0:
                            positive(pe, s.ex, p)
                        pe_route_t(pe, s, p * 2 + t, 2 * k + t)
                        pe_route_lg(pe, s, p * 2 + t, 2 * k + t)

            def body(p, k):
                transposed(p + 1, 1 - k)
                positive(pe, s.rkr, p)
                pe_route_rk(pe, s, p, VO)
            transposed(0, 0)
            pairs_by_two(pe, body, NT // 2)

        def pe_table(pe, s):
            pe.wait_ge(s.cnt, 1)
            for k in range(4):
                m = mm(ps[:, 0, k * P:(k + 1) * P], ones[:], diag[:, k, :])
            for h in range(2):
                m = mm(ps[:, 1, h * P:(h + 1) * P], ones[:], diag_twice[:, h, :])
            m.then_inc(s.bc, 1)

        TX, GU, HT, DN = 0, 2, 4, 6

        def pe_experts(pe, s):
            now = [pe.alloc_register(f"expert_now{j}_{s.n}") for j in range(2)]
            old = [pe.alloc_register(f"expert_old{j}_{s.n}") for j in range(2)]
            pe.wait_ge(s.tab, 1)
            pe.wait_ge(ld_exp, 16 * 3 * (NT // 2))
            pe.reg_load(now[0], itab[0:1, 0:1])
            pe.reg_mov(now[1], 0)
            pe.reg_mov(old[0], 0)
            pe.reg_mov(old[1], 0)

            def tx(n, q):
                pe.wait_ge(s.ld[q], 16 * (n // 4 + 1) if isinstance(n, int) else n * 4 + (16 - 4 * q))
                for c in range(KC):
                    m = pe.transpose(ps[:, TX + q % 2, c * P:(c + 1) * P], blk[:, q, c * P:(c + 1) * P], ident[:])
                m.then_inc(s.tx, 1)

            def step(n, q, m=None):
                j = q % 2
                if m is None or n < NB:
                    e = pe.snap(now[j], min_val=0, max_val=E - 1)
                    pe.wait_ge(s.xt, n + 1)
                    for c in range(KC):
                        g = mm(ps[:, GU + j, 0:2 * I], xbt[:, j, c * P:(c + 1) * P],
                               wgu[:, c, bass.ds(e * (2 * I), 2 * I)], start=(c == 0), stop=(c == KC - 1))
                    g.then_inc(s.gu, 1)
                if m is None or n + 1 < NB:
                    pe.reg_mov(old[1 - j], now[1 - j])
                    pe.reg_load(now[1 - j], itab[0:1, bass.ds(n + 1, 1)])
                elif n + 1 == NB:
                    pe.reg_mov(old[1 - j], now[1 - j])
                if m is None or n >= 2:
                    e2 = pe.snap(old[j], min_val=0, max_val=E - 1)
                    pe.wait_ge(s.hts, n - 1)
                    positive(pe, s.y, n - 3)
                    mm(ps[:, DN + j, 0:D], hbt[:, j, :], wdn[:, bass.ds(e2 * D, D)]).then_inc(s.d, 1)
                if m is None or 1 <= n < NB + 1:
                    pe.wait_ge(s.h, n)
                    pe.transpose(ps[:, HT + 1 - j, 0:P], hb[:, 1 - j, :], ident[:]).then_inc(s.ht, 1)
                if m is None or n + 2 < NB:
                    tx(n + 2, (q + 2) % 4)

            tx(0, 0)
            tx(1, 1)
            return step

        def pe_experts_run(pe, s):
            step = pe_experts(pe, s)
            for n in range(4):
                step(n, n % 4, m=0)
            with pe.Fori(1, NB // 4 - 1) as g:
                for q in range(4):
                    step(g * 4 + q, q)
            for n in range(NB - 4, NB + 2):
                step(n, n % 4, m=0)

        def pe_combine(pe, s):
            def gate_up(i, q):
                pe.wait_ge(s.xs[q], 16 * (i // 4 + 1) if isinstance(i, int) else i * 4 + (16 - 4 * q))
                for k in range(4):
                    for c in range(KC):
                        m = mm(ps[:, q % 2, k * P:(k + 1) * P], wsgu[:, c, k * P:(k + 1) * P],
                               xs[:, q, c * P:(c + 1) * P], start=(c == 0), stop=(c == KC - 1))
                m.then_inc(s.gu, 1)

            def down(i, q):
                j = q % 2
                pe.wait_ge(s.h, i + 1)
                positive(pe, s.sum, i - 3)
                for c in range(SI // P):
                    m = mm(ps[:, 2 + q, 0:D], hsh[:, j, c * P:(c + 1) * P], wsd[:, c, :],
                           start=(c == 0), stop=(c == SI // P - 1))
                m.then_inc(s.d, 1)

            gate_up(0, 0)
            for i in range(3):
                gate_up(i + 1, i + 1)
                down(i, i)
            with pe.Fori(1, NT // 4) as g:
                for q in range(4):
                    gate_up(g * 4 + q, q)
                    down(g * 4 + (q - 1), (q + 3) % 4)
            down(NT - 1, 3)

        def pe_means(pe):
            out_ = ps[:].rearrange("p b n -> p (b n)")
            with pe.Fori(0, NT // 4) as g:
                for q in range(4):
                    pe.wait_ge(m_xn, g * 4 + (q + 1))
                    pe.sem_inc(m_passed, 1)
                    mm(out_[0:8, bass.ds(g * D, D)], seg_mean[:, q, :], rows[:, q, 0:D],
                       start=(q == 0), stop=(q == 3)).then_inc(m_mm, 1)
            pe.wait_ge(m_sb, 2)
            for c in range(KC):
                for g in range(NT // 4):
                    m = pe.transpose(ps[:, 4, c * NSEG + 8 * g:c * NSEG + 8 * (g + 1)],
                                     means[0:8, g * D + c * P:g * D + (c + 1) * P], ident[0:8, 0:8])
            m.then_inc(m_t, 1)

        def pe_global(pe):
            pe.wait_ge(g_v, 1)
            xg = lambda c: xn2t[:, c * NSEG:(c + 1) * NSEG]
            for m_ in range(4):
                for c in range(KC):
                    m = mm(ps[:, 1, m_ * NSEG:(m_ + 1) * NSEG], wig[:, c, m_ * P:(m_ + 1) * P], xg(c),
                           start=(c == 0), stop=(c == KC - 1))
            m.then_inc(g_p, 1)
            for c in range(KC):
                m = mm(ps[0:NSEG, 2, 0:D], xg(c), wig[:, c, 2 * D:3 * D], start=(c == 0), stop=(c == KC - 1))
            m.then_inc(g_p, 1)
            pe.wait_ge(g_v, 2)
            for h in range(HG):
                r, c = HDG * (h % 2), h // 2
                m = mm(ps[0:NSEG, 3 + h % 2, c * NSEG:(c + 1) * NSEG], qkt[r:r + HDG, c, 0:NSEG],
                       qkt[r:r + HDG, 2 + c, 0:NSEG])
            m.then_inc(g_p, 1)
            pe.wait_ge(g_a, 2)
            for h in range(HG):
                m = pe.transpose(ps[0:NSEG, 5, h * NSEG:(h + 1) * NSEG], ssub[0:NSEG, h, :],
                                 ident[0:NSEG, 0:NSEG])
            m.then_inc(g_p, 1)
            pe.wait_ge(g_v, 4)
            for h in range(HG):
                m = mm(ps[0:NSEG, 6, h * HDG:(h + 1) * HDG], pt[0:NSEG, h, 0:NSEG],
                       osb[0:NSEG, h * HDG:(h + 1) * HDG])
            m.then_inc(g_p, 1)
            pe.wait_ge(g_v, 5)
            for c in range(KC):
                m = pe.transpose(ps[:, 7, c * NSEG:(c + 1) * NSEG], red[0:NSEG, c * P:(c + 1) * P],
                                 ident[0:NSEG, 0:NSEG])
            m.then_inc(g_p, 1)
            pe.wait_ge(g_v, 6)
            for c in range(KC):
                mm(ps[0:NSEG, 0, 0:D], ot[:, c * NSEG:(c + 1) * NSEG], wog[:, c, :], start=(c == 0), stop=False)
                mm(ps[0:NSEG, 0, 0:D], bvb[:, c, :], wol[:, c, :], start=False, stop=False)
                m = mm(ps[0:NSEG, 0, 0:D], bvb[:, KC + c, :], wog[:, c, :], start=False, stop=(c == KC - 1))
            m.then_inc(g_p, 1)

        def pe_qk(pe, i):
            pe.wait_ge(a_xts, i + 1)
            positive(pe, a_pts, i - 1)
            for q in range(4):
                for c in range(KC):
                    m = mm(ps[:, QK, q * P:(q + 1) * P], wil[:, c, q * P:(q + 1) * P],
                           xn2t[:, c * P:(c + 1) * P], start=(c == 0), stop=(c == KC - 1))
            m.then_inc(a_qk, 1)

        def pe_v(pe, i):
            positive(pe, a_vs, i)
            for c in range(KC):
                m = mm(ps[:, VO, 0:D], xn2t[:, c * P:(c + 1) * P], wil[:, c, 2 * D:3 * D],
                       start=(c == 0), stop=(c == KC - 1))
            m.then_inc(a_v, 1)

        def pe_t2(pe, i):
            pe.wait_ge(a_xn, i + 1)
            positive(pe, a_ex, i - 1)
            positive(pe, a_xts, i)
            for c in range(KC):
                m = pe.transpose(ps[:, T2, AFTER_S + c * P:AFTER_S + (c + 1) * P],
                                 xn2[:, c * P:(c + 1) * P], ident[:])
            m.then_inc(a_xt, 1)

        def pe_out(pe, i):
            pe.wait_ge(a_ots, i + 1)
            for c in range(KC):
                mm(ps[:, OUT, D:2 * D], ot[:, c * P:(c + 1) * P], wol[:, c, :],
                   start=(c == 0), stop=False)
            pe.wait_ge(a_sel, i + 1)
            mm(ps[:, OUT, D:2 * D], selt[:], glob[:], start=False, stop=True).then_inc(a_out, 1)

        def pe_mix(pe, i, j):
            pe.wait_ge(a_pts, i + 1)
            pe.wait_ge(a_vs, i + 1)
            for c in range(KC):
                for r in range(4):
                    h = 4 * c + r
                    m = mm(ps[HDL * r:HDL * (r + 1), HD, c * P:(c + 1) * P],
                           vv[:, j, h * HDL:(h + 1) * HDL], pt[:, h, :])
            m.then_inc(a_o, 1)

        def pe_attend(pe, i, j, between):
            def turn(place):
                if place in between:
                    between[place]()
            pe.wait_ge(a_qks, i + 1)
            if exists(i + 1):
                pe.wait_ge(a_xts, i + 2)
            for c in range(2):
                for g in range(2):
                    for r in range(4):
                        a, b = HDL * r, SEG * g
                        m = mm(ps[b:b + SEG, r, c * SEG:(c + 1) * SEG], qkt[a:a + HDL, c, b:b + SEG],
                               qkt[a:a + HDL, 2 + c, b:b + SEG])
            m.then_inc(a_s, 1)
            if exists(i - 1):
                pe_mix(pe, i - 1, 1 - j)
            if exists(i + 1):
                pe_qk(pe, i + 1)
            turn("after qk")
            if exists(i - 1):
                pe_out(pe, i - 1)
            turn("after out")
            if exists(i + 1):
                pe_v(pe, i + 1)
            turn("after v")
            if exists(i + 2):
                pe_t2(pe, i + 2)
            turn("before prob")
            pe.wait_ge(a_pr, i + 1)
            positive(pe, a_x2, i)
            if exists(i + 1):
                pe.wait_ge(a_qks, i + 2)
            for h in range(HL):
                m = pe.transpose(ps[:, QK + h // 4, (h % 4) * P:(h % 4 + 1) * P], prob[:, h, :], ident[:])
            m.then_inc(a_pt, 1)
            turn("last")

        def pe_pass_b(pe, s):
            def body(p, k):
                def first():
                    if pair_exists(p - 2):
                        pe.wait_ge(s.ex, p - 1)
                    pe_route_t(pe, s, p * 2 - 2, 2 * (1 - k))

                def ranks():
                    if pair_exists(p - 2):
                        pe.wait_ge(a_ex, min(p * 2 + 2, NT) if isinstance(p, int) else p * 2 + 2)
                        pe_route_rk(pe, s, p - 2, RK_ATTEND)

                def second():
                    pe_route_lg(pe, s, p * 2 - 2, 2 * (1 - k))
                    pe_route_t(pe, s, p * 2 - 1, 2 * (1 - k) + 1)

                def before_prob():
                    ranks()
                    if pair_exists(p - 1):
                        second()

                odd = {}
                odd["before prob"] = before_prob
                if pair_exists(p - 1):
                    odd["after v"] = first
                    odd["last"] = lambda: pe_route_lg(pe, s, p * 2 - 1, 2 * (1 - k) + 1)
                if pair_exists(p - 3):
                    pe.wait_ge(s.rkr, p - 2)
                if pair_exists(p):
                    pe_attend(pe, p * 2, 0, {})
                    pe_attend(pe, p * 2 + 1, 1, odd)
                else:
                    if p == NT // 2:
                        pe_mix(pe, NT - 1, 1)
                        pe_out(pe, NT - 1)
                    ranks()
                    if pair_exists(p - 1):
                        first()
                        second()
                        odd["last"]()

            pe_t2(pe, 0)
            pe_qk(pe, 0)
            pe_v(pe, 0)
            pe_t2(pe, 1)
            pairs_by_two(pe, body, NT // 2 + 2)

        def act_route_xt(act, s, i, q):
            j = q % 2
            act.wait_ge(s.xt, i + 1)
            positive(act, s.store[j], visits(i, j, 2, 16))
            act.copy(xnt[:, j, :], ps[:, RT, 0:D]).then_inc(s.xts, 1)

        def act_route_ex(act, s, p):
            act.wait_ge(s.lg, p + 1)
            positive(act, s.sel, p)
            act.activation(ex[:], ps[:, RT, LG0:LG0 + 2 * E].rearrange("p (t e) -> p t e", t=2),
                           ACT.Exp, scale=-1.0).then_inc(s.ex, 1)

        def act_route_rows(act, s, p, k):
            for q in (2 * k, 2 * k + 1):
                positive(act, s.scat[q], visits(p, k, 2, 16 * TOPK))
            act.wait_ge(s.xn, p * 2 + 2)
            act.copy(rows[:, 2 * k:2 * k + 2, 0:D], xn[:, 2 * k:2 * k + 2, :]).then_inc(s.rx, 1)

        def act_route(act, s):
            def transposed(p, k):
                if pair_exists(p):
                    for t in range(2):
                        act_route_xt(act, s, p * 2 + t, 2 * k + t)
                    act_route_ex(act, s, p)

            def body(p, k):
                transposed(p + 1, 1 - k)
                act_route_rows(act, s, p, k)
            transposed(0, 0)
            pairs_by_two(act, body, NT // 2)

        def act_experts(act, s):
            def xt_copy(n, j):
                act.wait_ge(s.tx, n + 1)
                positive(act, s.gu, n - 1)
                act.copy(xbt[:, j, :], ps[:, TX + j, 0:D]).then_inc(s.xt, 1)

            def step(n, j, m=None):
                if m is None or n < NB:
                    act.wait_ge(s.gu, n + 1)
                    positive(act, s.h, n - 1)
                    act.activation(sg[:, j, :], ps[:, GU + j, 0:I], ACT.Silu).then_inc(s.sg, 1)
                if m is None or n >= 1:
                    act.wait_ge(s.ht, n)
                    positive(act, s.d, n - 2)
                    act.copy(hbt[:, 1 - j, :], ps[:, HT + 1 - j, 0:P]).then_inc(s.hts, 1)
                if m is None or n + 2 < NB:
                    xt_copy(n + 2, j)

            xt_copy(0, 0)
            xt_copy(1, 1)
            step(0, 0, m=0)
            step(1, 1, m=0)
            step(2, 0, m=0)
            step(3, 1, m=0)
            with act.Fori(2, NB // 2 - 1) as pair:
                step(pair * 2, 0)
                step(pair * 2 + 1, 1)
            for n in range(NB - 2, NB + 1):
                step(n, n % 2, m=0)

        def act_combine(act, s):
            def body(i, j):
                act.wait_ge(s.gu, i + 1)
                positive(act, s.h, i - 1)
                act.activation(ssg[:, j, :], ps[:, j, 0:SI], ACT.Silu).then_inc(s.sg, 1)
            by_pairs(act, NT, body)

        def act_global(act):
            act.wait_ge(m_mm, NT)
            act.copy(means[0:8, 4 * D:8 * D].rearrange("p (b n) -> p b n", b=2), ps[0:8, 2:4, :]).then_inc(m_sb, 1)
            act.wait_ge(g_p, 2)
            act.copy(osb[0:NSEG, :], ps[0:NSEG, 2, 0:D]).then_inc(g_a, 1)
            act.wait_ge(g_v, 3)
            act.activation(ssub[0:NSEG, 0:HG, :], ssub[0:NSEG, HG:2 * HG, :], ACT.Exp,
                           scale=float(HDG) ** -0.5).then_inc(g_a, 1)

        def act_v(act, i, j):
            act.wait_ge(a_v, i + 1)
            positive(act, a_o, i - 1)
            act.copy(vv[:, j, :], ps[:, VO, 0:D]).then_inc(a_vs, 1)

        def act_qk(act, i):
            act.wait_ge(a_qk, i + 1)
            positive(act, a_s, i)
            for m_ in range(2 * KC):
                a = act.activation(qkt[:, m_, :], ps[:, QK, m_ * P:(m_ + 1) * P], ACT.Identity,
                                   bias=bil[:, m_:m_ + 1])
            a.then_inc(a_qks, 1)

        def act_heads(act, i):
            act.wait_ge(a_o, i + 1)
            positive(act, a_out, i)
            act.copy(ot, ps[:, HD, 0:D]).then_inc(a_ots, 1)
            act.copy(selt[:].rearrange("s (g t) -> s g t", g=2),
                     ident[0:NSEG, bass.ds(i * 2, 2)].unsqueeze(2).to_broadcast([NSEG, 2, SEG])
                     ).then_inc(a_sel, 1)

        def act_xt(act, i):
            act.wait_ge(a_xt, i + 1)
            positive(act, a_v, i)
            act.copy(xn2t, ps[:, T2, AFTER_S:AFTER_S + D]).then_inc(a_xts, 1)

        def act_prob(act, i):
            act.wait_ge(a_pt, i + 1)
            positive(act, a_o, i)
            act.copy(pt, ps[:, QK:QK + 2, :].rearrange("p b (h q) -> p (b h) q", h=4)).then_inc(a_pts, 1)

        def act_attend(act, i, j, between):
            def turn(place):
                if place in between:
                    between[place]()
            if exists(i - 1):
                act_prob(act, i - 1)
            turn("first")
            if exists(i - 1):
                act_heads(act, i - 1)
            act.wait_ge(a_max, i + 1)
            for h in range(HL):
                r, c = h % 4, h // 4
                a = act.activation(ssub[:, h, :], ps[:, r, c * SEG:(c + 1) * SEG], ACT.Exp,
                                   bias=nmax[:, h:h + 1], scale=float(HDL) ** -0.5,
                                   accum_out=psum_[:, h:h + 1])
            a.then_inc(a_ex, 1)
            if exists(i + 1):
                act_qk(act, i + 1)
                act_v(act, i + 1, 1 - j)
            turn("after v")
            if exists(i + 2):
                act_xt(act, i + 2)
            turn("last")

        def act_pass_b(act, s):
            def body(p, k):
                even, odd = {}, {}
                if pair_exists(p - 2):
                    even["first"] = lambda: act_route_ex(act, s, p - 2)
                if pair_exists(p - 1):
                    odd["after v"] = lambda: act_route_xt(act, s, p * 2 - 2, 2 * (1 - k))

                def last():
                    if pair_exists(p - 1):
                        act_route_xt(act, s, p * 2 - 1, 2 * (1 - k) + 1)
                    if pair_exists(p - 2):
                        act_route_rows(act, s, p - 2, k)
                odd["last"] = last
                if pair_exists(p):
                    act_attend(act, p * 2, 0, even)
                    act_attend(act, p * 2 + 1, 1, odd)
                else:
                    act_route_ex(act, s, p - 2)
                    if p == NT // 2:
                        act_prob(act, NT - 1)
                        act_heads(act, NT - 1)
                        for t in range(2):
                            act_route_xt(act, s, p * 2 - 2 + t, 2 * (1 - k) + t)
                    act_route_rows(act, s, p - 2, k)

            act_xt(act, 0)
            act_qk(act, 0)
            act_v(act, 0, 0)
            act_xt(act, 1)
            pairs_by_two(act, body, NT // 2 + 2)

        def inverse_root(st, var, y, a, b, steps=3):
            v = nc.vector
            st.then(v.tensor_scalar(a, var, EPS, None, ALU.add))
            st.then(v.tensor_scalar(b.bitcast(I32), a.bitcast(I32), 1, None, ALU.arith_shift_right))
            st.then(v.tensor_scalar(y.bitcast(I32), b.bitcast(I32), -1.0, float(MAGIC), ALU.mult, ALU.add))
            newton(st, y, a, b, steps)

        def newton(st, y, a, b, steps):
            v = nc.vector
            for _ in range(steps):
                st.then(v.tensor_tensor(b, y, y, ALU.mult))
                st.then(v.scalar_tensor_tensor(out=b, in0=b, scalar=-0.5, in1=a, op0=ALU.mult, op1=ALU.mult))
                st.then(v.scalar_tensor_tensor(out=y, in0=b, scalar=1.5, in1=y, op0=ALU.add, op1=ALU.mult))

        def xtile(i):
            return xres[:, bass.ds(i, 1), :].rearrange("p a d -> p (a d)")

        def mean_of(i):
            return mv[:, bass.ds(i, 1), 0:1].rearrange("p a b -> p (a b)")

        def v_statistics(v, st, i, n, steps=3):
            st.sync()
            v.sem_inc(vpassed, 1)
            for t in range(n):
                st.did(v.bn_stats(stats4[:, t, :], xtile(i + t)))
            st.sync()
            v.sem_inc(vpassed, 1)
            for t in range(n):
                st.did(v.bn_aggr(mv4[:, t, :], stats4[:, t, :]))
            st.sync()
            inverse_root(st, mv4[:, 0:n, 1], rstd4[:, 0:n], newt[:, 0, 0:n], newt[:, 1, 0:n],
                         steps)

        def v_norm(v, s, p, k, at):
            positive(v, s.xt, p * 2 - 2)
            positive(v, s.rx, p - 1)
            for t in range(2):
                v.tensor_scalar(xn[:, 2 * k + t, :], xtile(p * 2 + t), mv4[:, at + t, 0:1],
                                rstd4[:, at + t:at + t + 1], ALU.subtract, ALU.mult).then_inc(s.xn, 1)

        def v_route_groups(v, st, s, p):
            def both(f):
                st.sync()
                v.sem_inc(vpassed, 1)
                for t in range(2):
                    st.did(f(t))
            v.wait_ge(s.ex, p + 1)
            st.then(v.tensor_scalar(ex[:], ex[:], 1.0, None, ALU.add))
            st.then(v.reciprocal(sc[:], ex[:]))
            st.then(v.tensor_tensor(sfc[:], sc[:], gbias[:].unsqueeze(1).to_broadcast([P, 2, E]), ALU.add))
            st.did(v.tensor_reduce(gmax[:], sfc[:].rearrange("p t (g e) -> p t g e", g=NG), X_AXIS, ALU.max))
            both(lambda t: v.max(out=gtop[:, t, :], in_=gmax[:, t, :]))
            both(lambda t: v.max_index(out=gi8[:, t, :], in_max=gtop[:, t, :], in_values=gmax[:, t, :]))
            st.sync()
            st.then(v.tensor_tensor(
                og[:], gi8[:, :, 0:TOPG].unsqueeze(3).to_broadcast([P, 2, TOPG, NG]),
                iota_e[:, 0:NG].unsqueeze(1).unsqueeze(1).to_broadcast([P, 2, TOPG, NG]), ALU.is_equal))
            st.then(v.tensor_reduce(gkeep[:], og[:].rearrange("p t k g -> p t g k"), X_AXIS, ALU.add))
            st.did(v.tensor_tensor(msk[:].rearrange("p t (g e) -> p t g e", g=NG),
                                   sfc[:].rearrange("p t (g e) -> p t g e", g=NG),
                                   gkeep[:].unsqueeze(3).to_broadcast([P, 2, NG, GS]), ALU.mult))

        def v_route_six(v, st, s, p):
            def both(f):
                st.sync()
                v.sem_inc(vpassed, 1)
                for t in range(2):
                    st.did(f(t))
            both(lambda t: v.max(out=t8[:, t, :], in_=msk[:, t, :]))
            both(lambda t: v.max_index(out=ti8[:, t, :], in_max=t8[:, t, :], in_values=msk[:, t, :]))
            st.sync()
            st.then(v.tensor_tensor(
                oh[:], ti8[:, :, 0:TOPK].unsqueeze(3).to_broadcast([P, 2, TOPK, E]),
                iota_e[:].unsqueeze(1).unsqueeze(1).to_broadcast([P, 2, TOPK, E]), ALU.is_equal))
            v.tensor_reduce(sel[:, 0:2, :], oh[:].rearrange("p t k e -> p t e k"), X_AXIS, ALU.add).then_inc(s.sel, 1)

        def v_route_ranks(v, st, s, p, bank):
            v.wait_ge(s.rk, p + 1)
            st.then(v.tensor_tensor(slot[:], ps[:, bank, RK0:RK0 + 2 * E].rearrange("p (t e) -> p t e", t=2),
                                    base[:].unsqueeze(1).to_broadcast([P, 2, E]), ALU.add))
            v.tensor_tensor(base[:], ps[:, bank, RK0 + 2 * E:RK0 + 3 * E], base[:], ALU.add).then_inc(s.rkr, 1)

        def v_route_weights(v, st, s, p, k):
            two = slice(2 * k, 2 * k + 2)
            v.wait_ge(s.sel, p + 1)
            st.did(v.tensor_tensor(cw[:], sc[:], sel[:, 0:2, :], ALU.mult))
            for t in range(2):
                st.did(v.tensor_tensor_scan(nth[:, t, :], ones[:, 0:E], sel[:, t, :], 0.0, ALU.mult, ALU.add))
            st.sync()
            for q in (2 * k, 2 * k + 1):
                positive(v, s.scat[q], visits(p, k, 2, 16 * TOPK))
            st.did(v.tensor_reduce(csum[:, 0, :], cw[:], X_AXIS, ALU.add))
            for t in range(2):
                st.did(v.tensor_scalar(rows[:, 2 * k + t, COL_DEST:ROW], nth[:, t, :],
                                       tok6[:, bass.ds(p * 2 + t, 1)], None, ALU.add))
            st.sync()
            st.then(v.tensor_scalar(csum[:, 1, :], csum[:, 0, :], 1e-20, None, ALU.add))
            st.then(v.reciprocal(csum[:, 2, :], csum[:, 1, :]))
            st.did(v.scalar_tensor_tensor(out=rows[:, two, COL_W:COL_W + E], in0=cw[:], scalar=SCALE * HALF,
                                          in1=csum[:, 2, :].unsqueeze(2).to_broadcast([P, 2, E]),
                                          op0=ALU.mult, op1=ALU.mult))

        def v_route_slots(v, st, s, p, k):
            v.wait_ge(s.rkr, p + 1)
            st.then(v.tensor_tensor(ohs[:], oh[:], slot[:].unsqueeze(2).to_broadcast([P, 2, TOPK, E]), ALU.mult))
            with nc.allow_low_precision(reason="one whole number and zeros"):
                v.tensor_reduce(idx[:, 2 * k:2 * k + 2, 0:TOPK], ohs[:], X_AXIS, ALU.add).then_inc(s.slots, 1)

        def v_pairs(v, st, body, last, steps):
            body(0, 0)
            body(1, 1)
            start = st.base + st.n
            with v.Fori(1, NT // 4 - 1) as g:
                st.rebase(g * steps + (start - steps))
                for k in range(2):
                    body(g * 2 + k, k)
                assert st.n == steps, (st.n, steps)
            st.rebase(start + (NT // 4 - 2) * steps)
            for p in range(NT // 2 - 2, last):
                body(p, p % 2)

        ROUTE_STEPS = 27

        def v_route(v, st, s):
            st.then(v.tensor_copy(base[:], iota_cap[:]))

            def statistics(p):
                if pair_exists(p):
                    v_statistics(v, st, p * 2, 4)

            def body(p, k):
                if pair_exists(p + 1):
                    v_norm(v, s, p + 1, 1 - k, 2 - 2 * k)
                v_route_groups(v, st, s, p)
                v_route_six(v, st, s, p)
                v_route_ranks(v, st, s, p, VO)
                v_route_weights(v, st, s, p, k)
                v_route_slots(v, st, s, p, k)
                if isinstance(p, int) and p < 2:
                    v.wait_ge(ld_x[p + 1], 16)
                if k == 0:
                    statistics(p + 2)
            v.wait_ge(ld_x[0], 16)
            statistics(0)
            v_norm(v, s, 0, 0, 0)
            v.wait_ge(ld_gate, 32)
            v_pairs(v, st, body, NT // 2, 2 * ROUTE_STEPS + 20)

        def v_table(v, st, r, s):
            cnt, nb, cum = tbl[:, 0, :], tbl[:, 1, :], tbl[:, 2, :]
            st.then(v.tensor_tensor(cnt, base[:], iota_cap[:], ALU.subtract))
            st.then(v.tensor_tensor(cmp_[:], cnt.unsqueeze(2).to_broadcast([P, E, E]),
                                    iota_thr[:].unsqueeze(1).to_broadcast([P, E, E]), ALU.is_gt))
            st.then(v.tensor_reduce(nb, cmp_[:], X_AXIS, ALU.add))
            st.then(v.tensor_tensor_scan(cum, ones[:, 0:E], nb, 0.0, ALU.mult, ALU.add))
            for h in range(2):
                ge, start = tbl[:, 3, :], tbl[:, 4, :]
                ecol, scol, fcol = (tcol[:, 3 * h + k:3 * h + k + 1] for k in range(3))
                lcol = tcol[:, 8 + h:9 + h]
                st.then(v.tensor_scalar(ge, cum, iota_blk[:, h:h + 1], None, ALU.is_le))
                st.did(v.tensor_reduce(ecol, ge, X_AXIS, ALU.add))
                st.then(v.tensor_tensor(start, ge, cum, ALU.mult))
                st.then(v.tensor_reduce(scol, start, X_AXIS, ALU.max))
                st.then(v.tensor_tensor(fcol, iota_blk[:, h:h + 1], scol, ALU.subtract))
                st.then(v.tensor_scalar(fcol, fcol, float(P), None, ALU.mult))
                st.then(v.tensor_scalar(tcol[:, 6 + h:7 + h], ecol, float(CAP), None, ALU.mult))
                st.then(v.tensor_tensor(fcol, fcol, tcol[:, 6 + h:7 + h], ALU.add))
                st.then(v.scalar_tensor_tensor(out=start, in0=iota_e[:], scalar=ecol, in1=base[:],
                                               op0=ALU.is_equal, op1=ALU.mult, accum_out=lcol))
                st.then(v.tensor_scalar(lcol, lcol, -2.0 * P, None, ALU.add))
                st.did(v.tensor_tensor(tcol[:, 10 + h:11 + h], fcol, lcol, ALU.subtract))
                st.then(v.tensor_tensor(fcol, fcol, lcol, ALU.min))
                st.then(v.tensor_scalar(fcol, fcol, float(P), None, ALU.add))
                st.then(v.tensor_scalar(fcol, fcol, 0.0, None, ALU.max))
                st.then(v.tensor_scalar(ecol, ecol, float(E - 1), None, ALU.min))
                st.did(v.tensor_scalar(diag[:, h, :], ident[:], ecol, None, ALU.mult))
                st.did(v.tensor_scalar(diag[:, 2 + h, :], ident[:], fcol, None, ALU.mult))
                st.then(v.tensor_scalar(diag_twice[:, h, :], ident[:], tcol[:, 10 + h:11 + h], None, ALU.mult))
            v.sem_inc(s.cnt, 1)
            v.wait_ge(s.bc, 1)
            st.did(v.tensor_copy(etab[:], ps[:, 0, 0:2 * P]))
            st.did(v.tensor_scalar(skip, ps[:, 1, 0:2 * P], iota_blk[:, 0:1], float(NOWHERE),
                                   ALU.is_gt, ALU.mult))
            st.then(v.tensor_copy(itab[:], ps[0:1, 0, :]))
            v.sem_inc(s.tab, 1)

        def v_experts(v, st, s):
            start = st.base + st.n
            st.rebase(start)

            def pick(n, q):
                v.wait_ge(s.ld[q], 16 * (n // 4 + 1) if isinstance(n, int) else n * 4 + (16 - 4 * q))
                positive(v, s.pick, n * 2)
                positive(v, s.h, n - 3)
                for k, (col, out_) in enumerate(((COL_W, wcol), (COL_DEST, dcol))):
                    v.scalar_tensor_tensor(
                        out=picked[:, k, :], in0=iota_e[:], scalar=etab[:, bass.ds(n, 1)],
                        in1=blk[:, q, col:col + E], op0=ALU.is_equal, op1=ALU.mult,
                        accum_out=out_[:, q:q + 1]).then_inc(s.pick, 1)

            def step(n, q, m=None):
                j = q % 2
                if m is None or n < NB:
                    v.wait_ge(s.sg, n + 1)
                    positive(v, s.ht, n - 1)
                    v.wait_ge(s.pick, n * 2 + 2)
                    v.scalar_tensor_tensor(out=hb[:, j, :], in0=ps[:, GU + j, I:2 * I],
                                           scalar=wcol[:, q:q + 1], in1=sg[:, j, :],
                                           op0=ALU.mult, op1=ALU.mult).then_inc(s.h, 1)
                if m is None or n >= 2:
                    k = (q + 2) % 4
                    positive(v, s.scat[k],
                             16 * ((n - 2) // 4) if isinstance(n, int) else n * 4 - (8 + 4 * k))
                    st.did(v.tensor_tensor(didx[:, k:k + 1], dcol[:, k:k + 1], skip[:, bass.ds(n - 2, 1)], ALU.add))
                    v.wait_ge(s.d, n - 1)
                    v.tensor_copy(yb[:, k, :], ps[:, DN + j, 0:D]).then_inc(s.y, 1)
                    st.sync()
                if m is None or n + 2 < NB:
                    pick(n + 2, (q + 2) % 4)

            pick(0, 0)
            pick(1, 1)
            for n in range(4):
                step(n, n % 4, m=0)
            one = 1
            with v.Fori(1, NB // 4 - 1) as g:
                for q in range(4):
                    st.rebase(g * (4 * one) + (start + q - 2))
                    step(g * 4 + q, q)
            st.rebase(start + NB - 4 - 2)
            for n in range(NB - 4, NB + 2):
                step(n, n % 4, m=0)

        def v_combine(v, st, s, last):
            def hidden(i, j):
                v.wait_ge(s.sg, i + 1)
                positive(v, s.d, i - 1)
                v.tensor_tensor(hsh[:, j, :], ssg[:, j, :], ps[:, j, SI:2 * SI], ALU.mult).then_inc(s.h, 1)

            def stats_of(i):
                v.wait_ge(s.sum, i + 1)
                st.sync()
                v.sem_inc(vpassed, 1)
                st.did(v.bn_stats(stats[:], xtile(i)))

            def finish_stats(i, q):
                st.did(v.bn_aggr(mv4[:, q, :], stats[:]))
                if q == 3:
                    st.sync()
                    st.did(v.tensor_copy(mv[:, bass.ds(i - 3, 4), :], mv4[:]))

            def final(i, q):
                v.wait_ge(s.part, i * 3 + 3)
                v.wait_ge(s.d, i + 1)
                v.scalar_tensor_tensor(out=xtile(i), in0=ps[:, 2 + q, 0:D], scalar=HALF, in1=xtile(i),
                                       op0=ALU.mult, op1=ALU.add).then_inc(s.sum, 1)

            def body(i, q):
                j = q % 2
                if exists(i + 1):
                    hidden(i + 1, 1 - j)
                stats_now = not last and exists(i - 2)
                if stats_now:
                    stats_of(i - 2)
                v.wait_ge(s.ans[0][j], 16 + visits(i, j, 2, 16))
                positive(v, s.part, i * 3 - 4)
                a = ans[:, j, :].rearrange("p (k d) -> p k d", k=TOPK)
                v.tensor_tensor(two_sums[j], a[:, 0:2, :], a[:, 2:4, :], ALU.add).then_inc(s.red, 1)
                v.wait_ge(s.ans[1][j], 16 + visits(i, j, 2, 16))
                positive(v, s.part, i * 3 - 3)
                v.tensor_tensor(third_sum[j], a[:, 4, :], a[:, 5, :], ALU.add).then_inc(s.red, 1)
                if stats_now:
                    st.sync()
                    v.sem_inc(vpassed, 1)
                    finish_stats(i - 2, (q + 2) % 4)
                if exists(i - 1):
                    final(i - 1, (q + 3) % 4)

            hidden(0, 0)
            for i in range(4):
                body(i, i)
            start = st.base + st.n
            four = 0 if last else 2 * 4 + 1
            with v.Fori(1, NT // 4 - 1) as g:
                st.rebase(g * four + (start - four))
                for q in range(4):
                    body(g * 4 + q, q)
                assert st.n == four
            st.rebase(start + (NT // 4 - 2) * four)
            for q in range(4):
                body(NT - 4 + q, q)
            final(NT - 1, 3)
            if not last:
                for i in range(NT - 2, NT):
                    stats_of(i)
                    st.sync()
                    v.sem_inc(vpassed, 1)
                    finish_stats(i, i % 4)

        def v_means(v, st):
            st.sync()
            inverse_root(st, mv[:, :, 1], rstd[:], newt[:, 0, :], newt[:, 1, :])

            def body(i, q):
                positive(v, m_mm, i - 3)
                v.tensor_scalar(rows[:, q, 0:D], xtile(i), mean_of(i), rstd[:, bass.ds(i, 1)],
                                ALU.subtract, ALU.mult).then_inc(m_xn, 1)
            for q in range(4):
                body(q, q)
            with v.Fori(1, NT // 4) as g:
                for q in range(4):
                    body(g * 4 + q, q)

        def v_global(v, st):
            v.wait_ge(m_mm, NT)
            v.tensor_copy(means[0:8, 0:4 * D].rearrange("p (b n) -> p b n", b=2), ps[0:8, 0:2, :]).then_inc(m_sb, 1)
            for k, b in enumerate((bil, big)):
                for c in range(KC):
                    st.did(v.tensor_copy(bvb[:, k * KC + c, :],
                                         b[:, 2 * KC + c:2 * KC + c + 1].to_broadcast([P, NSEG])))
            v.wait_ge(m_t, 1)
            st.then(v.tensor_copy(xn2t[:, 0:KC * NSEG], ps[:, 4, 0:KC * NSEG]))
            v.sem_inc(g_v, 1)
            v.wait_ge(g_p, 2)
            v.tensor_tensor(qkt[:, :, 0:NSEG], ps[:, 1, 0:4 * NSEG].rearrange("p (m t) -> p m t", m=4),
                            big[:, 0:4].unsqueeze(2).to_broadcast([P, 4, NSEG]), ALU.add).then_inc(g_v, 1)
            v.wait_ge(g_p, 3)
            sview = ps[0:NSEG, 3:5, 0:2 * NSEG].rearrange("p r (c k) -> p r c k", c=2)
            mview = smax[0:NSEG, 0:HG].rearrange("p (c r) -> p r c", c=2)
            st.then(v.tensor_reduce(mview, sview, X_AXIS, ALU.max))
            v.tensor_tensor(ssub[0:NSEG, HG:2 * HG, :].rearrange("p (c r) k -> p r c k", c=2), sview,
                            mview.unsqueeze(3).to_broadcast([NSEG, 2, 2, NSEG]), ALU.subtract).then_inc(g_v, 1)
            v.wait_ge(g_a, 2)
            st.then(v.tensor_reduce(smax[0:NSEG, 0:HG], ssub[0:NSEG, 0:HG, :], X_AXIS, ALU.add))
            st.then(v.reciprocal(rden[0:NSEG, 0:HG], smax[0:NSEG, 0:HG]))
            v.wait_ge(g_p, 4)
            v.tensor_copy(pt[0:NSEG, 0:HG, 0:NSEG],
                          ps[0:NSEG, 5, 0:HG * NSEG].rearrange("p (h q) -> p h q", h=HG)).then_inc(g_v, 1)
            v.wait_ge(g_p, 5)
            v.tensor_tensor(red[0:NSEG, :].rearrange("p (h d) -> p h d", h=HG),
                            ps[0:NSEG, 6, 0:D].rearrange("p (h d) -> p h d", h=HG),
                            rden[0:NSEG, 0:HG].unsqueeze(2).to_broadcast([NSEG, HG, HDG]),
                            ALU.mult).then_inc(g_v, 1)
            v.wait_ge(g_p, 6)
            v.tensor_copy(ot[:, 0:KC * NSEG], ps[:, 7, 0:KC * NSEG]).then_inc(g_v, 1)
            v.wait_ge(g_p, 7)
            st.then(v.tensor_tensor(glob[:], ps[0:NSEG, 0, 0:D], bout[0:NSEG, 0, :], ALU.add))
            v.tensor_tensor(glob[:], glob[:], bout[0:NSEG, 1, :], ALU.add).then_inc(g_v, 1)

        def v_xn2(v, i):
            positive(v, a_xt, i)
            v.tensor_scalar(xn2, xtile(i), mean_of(i), rstd[:, bass.ds(i, 1)],
                            ALU.subtract, ALU.mult).then_inc(a_xn, 1)

        def v_out(v, i):
            v.wait_ge(a_out, i + 1)
            v.tensor_tensor(xtile(i), ps[:, OUT, D:2 * D], xtile(i), ALU.add).then_inc(a_x2, 1)

        def v_attend(v, st, i, between):
            def turn(place):
                if place in between:
                    between[place]()
            v.wait_ge(a_s, i + 1)
            sview = ps[:, 0:4, 0:2 * SEG].rearrange("p r (c k) -> p r c k", c=2)
            mview = smax[:].rearrange("p (c r) -> p r c", c=2)
            st.then(v.tensor_reduce(mview, sview, X_AXIS, ALU.max))
            v.tensor_scalar(nmax[:], smax[:], -float(HDL) ** -0.5, None, ALU.mult).then_inc(a_max, 1)
            turn("after max")
            if exists(i - 1):
                v_out(v, i - 1)
            v.wait_ge(a_ex, i + 1)
            positive(v, a_pt, i)
            st.then(v.reciprocal(rden[:], psum_[:]))
            for g in range(2):
                rows_ = slice(g * SEG, (g + 1) * SEG)
                m = v.tensor_tensor(prob[rows_, :, rows_], ssub[rows_, :, :],
                                    rden[rows_, :].unsqueeze(2).to_broadcast([SEG, HL, SEG]), ALU.mult)
            m.then_inc(a_pr, 1)
            turn("after prob")
            if exists(i + 3):
                v_xn2(v, i + 3)
            turn("last")

        def v_pass_b(v, st, s):
            def body(p, k):
                even, odd = {}, {}

                def statistics():
                    v.wait_ge(a_x2, p * 2)
                    v_statistics(v, st, p * 2 - 2, 2, 1)

                def normed():
                    st.sync()
                    newton(st, rstd4[:, 0:2], newt[:, 0, 0:2], newt[:, 1, 0:2], 2)
                    v_norm(v, s, p - 1, 1 - k, 0)
                if pair_exists(p - 1):
                    even["last"] = statistics
                if pair_exists(p - 2):
                    even["after max"] = lambda: v_route_groups(v, st, s, p - 2)
                    odd["after prob"] = lambda: v_route_ranks(v, st, s, p - 2, RK_ATTEND)

                    def slots():
                        v_route_weights(v, st, s, p - 2, k)
                        v_route_slots(v, st, s, p - 2, k)
                    odd["last"] = slots

                def middle():
                    if pair_exists(p - 1):
                        normed()
                    if pair_exists(p - 2):
                        v_route_six(v, st, s, p - 2)
                odd["after max"] = middle
                if pair_exists(p):
                    v_attend(v, st, p * 2, even)
                    v_attend(v, st, p * 2 + 1, odd)
                else:
                    v_route_groups(v, st, s, p - 2)
                    v_route_six(v, st, s, p - 2)
                    if p == NT // 2:
                        v_out(v, NT - 1)
                        statistics()
                        normed()
                    v_route_ranks(v, st, s, p - 2, RK_ATTEND)
                    v_route_weights(v, st, s, p - 2, k)
                    v_route_slots(v, st, s, p - 2, k)

            st.then(v.tensor_copy(base[:], iota_cap[:]))
            v_xn2(v, 0)
            v_xn2(v, 1)
            v_xn2(v, 2)
            v_pairs(v, st, body, NT // 2 + 2, 2 * (ROUTE_STEPS + 16 + 4))

        out_tiles = out.rearrange("b (n p) d -> p (b n) d", p=P)

        @block.sync
        def _(sp):
            load_inputs(sp)

            def more(p):
                if isinstance(p, int):
                    load_dense(sp)
                load_experts(sp, p)
            sp_route(sp, R[0], more)
            sp_experts(sp, R[0], X[0])
            sp_combine(sp, X[0], C[0], R[0], False)
            sp_route(sp, R[1])
            sp_experts(sp, R[1], X[1])
            sp_combine(sp, X[1], C[1], R[1], True)

        @block.gpsimd
        def _(pool):
            make_consts(pool)
            pool_route(pool, R[0])
            pool_experts(pool, X[0])
            pool_combine(pool, C[0])
            pool_route(pool, R[1])
            pool_experts(pool, X[1])
            pool_combine(pool, C[1])

        @block.tensor
        def _(pe):
            pe.wait_ge(consts, N_CONST)
            pe.wait_ge(ld_gate, 32)
            pe_route(pe, R[0])
            pe.wait_ge(ld_small, N_SMALL)
            pe_table(pe, X[0])
            pe_experts_run(pe, X[0])
            pe_combine(pe, C[0])
            pe_means(pe)
            pe_global(pe)
            pe.wait_ge(g_v, 7)
            pe_pass_b(pe, R[1])
            pe_table(pe, X[1])
            pe_experts_run(pe, X[1])
            pe_combine(pe, C[1])

        @block.scalar
        def _(act):
            act.wait_ge(consts, N_CONST)
            act.activation(sg[:, 0, 0:1], ones[:, 0:1], ACT.Exp)
            act_route(act, R[0])
            act_experts(act, X[0])
            act_combine(act, C[0])
            act.wait_ge(ld_small, N_SMALL)
            act_global(act)
            act.wait_ge(g_v, 7)
            act_pass_b(act, R[1])
            act_experts(act, X[1])
            act_combine(act, C[1])
            for k in range(4):
                n = NT // 4
                act.wait_ge(C[1].sum, (k + 1) * n)
                act.dma_start(out_tiles[:, k * n:(k + 1) * n, :],
                              xres[:, k * n:(k + 1) * n, :]).then_inc(C[1].out, 16)
            act.wait_ge(C[1].out, 64)

        @block.vector
        def _(v):
            st = Steps(v, vstep)
            v.wait_ge(consts, N_CONST)
            v_route(v, st, R[0])
            v_table(v, st, R[0], X[0])
            v_experts(v, st, X[0])
            v_combine(v, st, C[0], False)
            v_means(v, st)
            v.wait_ge(ld_small, N_SMALL)
            v_global(v, st)
            v_pass_b(v, st, R[1])
            v_table(v, st, R[1], X[1])
            v_experts(v, st, X[1])
            v_combine(v, st, C[1], True)


def kernel(L0_attn_x, L0_attn_w_in_local, L0_attn_b_in_local, L0_attn_w_out_local, L0_attn_b_out_local,
           L0_attn_w_in_global, L0_attn_b_in_global, L0_attn_w_out_global, L0_attn_b_out_global,
           L0_ffn_gate_weight, L0_ffn_e_score_correction_bias, L0_ffn_experts_gate_up, L0_ffn_experts_down,
           L0_ffn_shared_gate_w, L0_ffn_shared_up_w, L0_ffn_shared_down_w):
    from concourse import bacc
    from concourse.bass_utils import run_bass_kernel_spmd

    c = np.ascontiguousarray
    arrays = {
        "in_x": c(L0_attn_x),
        "in_gate": c(np.asarray(L0_ffn_gate_weight).T),
        "in_gate_bias": c(L0_ffn_e_score_correction_bias),
        "in_gate_up": c(np.asarray(L0_ffn_experts_gate_up).transpose(2, 0, 1)).reshape(KC, P, E * 2 * I),
        "in_down": c(np.asarray(L0_ffn_experts_down).transpose(2, 0, 1)).reshape(I, E * D),
        "in_shared_gate": c(np.asarray(L0_ffn_shared_gate_w).T),
        "in_shared_up": c(np.asarray(L0_ffn_shared_up_w).T),
        "in_shared_down": c(np.asarray(L0_ffn_shared_down_w).T),
        "in_wi_local": c(np.asarray(L0_attn_w_in_local).T),
        "in_bi_local": c(L0_attn_b_in_local),
        "in_wo_local": c(np.asarray(L0_attn_w_out_local).T),
        "in_bo_local": c(L0_attn_b_out_local),
        "in_wi_global": c(np.asarray(L0_attn_w_in_global).T),
        "in_bi_global": c(L0_attn_b_in_global),
        "in_wo_global": c(np.asarray(L0_attn_w_out_global).T),
        "in_bo_global": c(L0_attn_b_out_global),
    }
    nc = bacc.Bacc("TRN2", target_bir_lowering=False, num_devices=1)
    args = [nc.dram_tensor(n, a.shape, F32, kind="ExternalInput").ap() for n, a in arrays.items()]
    args.append(nc.dram_tensor("out", L0_attn_x.shape, F32, kind="ExternalOutput").ap())
    build(nc, *args)
    r = run_bass_kernel_spmd(nc, [arrays], core_ids=[0])
    return r.results[0]["out"]
```
